# Optimizing a Trainium2 kernel written in Bass

```python
import numpy as np
import jax
import jax.numpy as jnp

def _softmax(x, axis=-1):
    return jax.nn.softmax(x, axis=axis)

def _gelu(x):
    return jax.nn.gelu(x, approximate=True)

def _silu(x):
    return jax.nn.silu(x)

def _sigmoid(x):
    return jax.nn.sigmoid(x)

def _layernorm(x, axis=-1, eps=1e-05):
    m = jnp.mean(x, axis=axis, keepdims=True)
    v = jnp.var(x, axis=axis, keepdims=True)
    return (x - m) / jnp.sqrt(v + eps)

def _scatter_add(tgt, idx, src, axis=0):
    return tgt.at[idx].add(src)

def _segment_sum(src, seg, n):
    return jax.ops.segment_sum(src, seg, n)
kernel_name = 'mk_early_fusion_d1_tok_img768_r4_2d7279'

def setup_inputs(seed: int=0):
    np.random.seed(seed)
    _w = jnp.asarray

    def _rec_inputs():
        import jax
        import jax.numpy as jnp
        _rk = jax.random.key(seed)
        x = -0.00016672 + 0.999947 * jax.random.normal(jax.random.fold_in(_rk, 1), (32, 3, 224, 224), jnp.float32)
        txt = -0.00020034 + 0.55463 * jax.random.normal(jax.random.fold_in(_rk, 2), (32, 77, 192), jnp.float32)
        return (x, txt)
    x, txt = _rec_inputs()

    def _L0_tok_setup():
        import jax, jax.numpy as jnp
        import numpy as np
        PH = PW = 16
        key = jax.random.key(seed)
        k1, k2, k3 = jax.random.split(key, 3)
        B, C, H, W_ = (64, 3, 96, 96)
        embed_dim = 192
        patch_dim = C * PH * PW
        x = jax.random.normal(k1, (B, C, H, W_), dtype=jnp.float32)
        W = jax.random.normal(k2, (embed_dim, patch_dim), dtype=jnp.float32) * 0.02
        b = jax.random.normal(k3, (embed_dim,), dtype=jnp.float32) * 0.02
        return {'x': x, 'W': W, 'b': b}
    _L0_tok_all = _L0_tok_setup()
    _L0_tok_in = {k: v for k, v in _L0_tok_all.items() if k in ('W', 'b')}
    del _L0_tok_all

    def _L0_attn_setup():
        import jax, jax.numpy as jnp
        import numpy as np
        ATTN_DIM = 192
        NEG = -1000000000.0
        key = jax.random.key(seed)
        x = jax.random.normal(key, (4, 1024, ATTN_DIM), dtype=jnp.float32)
        return {'x': x}
    _L0_attn_all = _L0_attn_setup()
    _L0_attn_in = {k: v for k, v in _L0_attn_all.items() if k in ()}
    del _L0_attn_all

    def _L0_ffn_setup():
        import jax, jax.numpy as jnp
        import numpy as np
        ATOM = {'vm': 0, 'im': 1, 'cm': 2, 'sc': 3, 'cc': 4}
        TASK_PAIRS = [('vm', 'sc'), ('vm', 'cc'), ('im', 'sc'), ('im', 'cc'), ('cm', 'sc'), ('cm', 'cc')]
        SRC_IDX = np.array([[ATOM[l], ATOM[r]] for l, r in TASK_PAIRS], dtype=np.int32)
        DST_IDX = np.array([[ATOM[r], ATOM[l]] for l, r in TASK_PAIRS], dtype=np.int32)
        NCLS = 6
        NATOMS = 5

        def _l2norm(x, eps=1e-12):
            return x / jnp.clip(jnp.linalg.norm(x, axis=-1, keepdims=True), eps)
        key = jax.random.key(seed)
        ks = jax.random.split(key, 12)
        B, NPATCH, D, H = (64, 197, 192, 768)
        std = 0.02
        x = jax.random.normal(ks[0], (B, NCLS + NPATCH, D), dtype=jnp.float32)
        fc1_w = jax.random.normal(ks[1], (H, D), dtype=jnp.float32) * std
        fc1_b = jnp.zeros((H,), jnp.float32)
        fc2_w = jax.random.normal(ks[2], (D, H), dtype=jnp.float32) * std
        fc2_b = jnp.zeros((D,), jnp.float32)
        gate_pair = jax.random.normal(ks[3], (NCLS, 2, D), dtype=jnp.float32) * std
        atom_in_w = jax.random.normal(ks[4], (NATOMS, H, D), dtype=jnp.float32) * std
        atom_in_b = jax.random.normal(ks[5], (NATOMS, H), dtype=jnp.float32) * std
        atom_out_w = jax.random.normal(ks[6], (NATOMS, D, H), dtype=jnp.float32) * std
        atom_out_b = jax.random.normal(ks[7], (NATOMS, D), dtype=jnp.float32) * std
        balance_bias = jnp.zeros((NCLS, 2), jnp.float32)
        return {'x': x, 'fc1_w': fc1_w, 'fc1_b': fc1_b, 'fc2_w': fc2_w, 'fc2_b': fc2_b, 'gate_pair': gate_pair, 'atom_in_w': atom_in_w, 'atom_in_b': atom_in_b, 'atom_out_w': atom_out_w, 'atom_out_b': atom_out_b, 'balance_bias': balance_bias}
    _L0_ffn_all = _L0_ffn_setup()
    _L0_ffn_in = {k: v for k, v in _L0_ffn_all.items() if k in ('fc1_w', 'fc1_b', 'fc2_w', 'fc2_b', 'gate_pair', 'atom_in_w', 'atom_in_b', 'atom_out_w', 'atom_out_b', 'balance_bias')}
    del _L0_ffn_all
    return {'x': x, 'txt': txt, 'L0_tok_W': _L0_tok_in['W'], 'L0_tok_b': _L0_tok_in['b'], 'L0_ffn_fc1_w': _L0_ffn_in['fc1_w'], 'L0_ffn_fc1_b': _L0_ffn_in['fc1_b'], 'L0_ffn_fc2_w': _L0_ffn_in['fc2_w'], 'L0_ffn_fc2_b': _L0_ffn_in['fc2_b'], 'L0_ffn_gate_pair': _L0_ffn_in['gate_pair'], 'L0_ffn_atom_in_w': _L0_ffn_in['atom_in_w'], 'L0_ffn_atom_in_b': _L0_ffn_in['atom_in_b'], 'L0_ffn_atom_out_w': _L0_ffn_in['atom_out_w'], 'L0_ffn_atom_out_b': _L0_ffn_in['atom_out_b'], 'L0_ffn_balance_bias': _L0_ffn_in['balance_bias']}

def reference(x, txt, L0_tok_W, L0_tok_b, L0_ffn_fc1_w, L0_ffn_fc1_b, L0_ffn_fc2_w, L0_ffn_fc2_b, L0_ffn_gate_pair, L0_ffn_atom_in_w, L0_ffn_atom_in_b, L0_ffn_atom_out_w, L0_ffn_atom_out_b, L0_ffn_balance_bias):
    import jax
    import jax.numpy as jnp

    def _L0_tok_ref(x, W, b):
        import jax, jax.numpy as jnp
        import numpy as np
        PH = PW = 16
        B, C, H, Wd = x.shape
        Hp, Wp = (H // PH, Wd // PW)
        patches = x.reshape(B, C, Hp, PH, Wp, PW)
        patches = patches.transpose(0, 2, 4, 1, 3, 5).reshape(B, Hp * Wp, C * PH * PW)
        return jnp.einsum('bnp,ep->bne', patches, W) + b

    def _L0_attn_ref(x):
        import jax, jax.numpy as jnp
        import numpy as np
        ATTN_DIM = 192
        NEG = -1000000000.0
        B, S, D = x.shape
        scores = jnp.einsum('bsd,btd->bst', x, x) / jnp.sqrt(jnp.float32(D))
        row = jax.lax.broadcasted_iota(jnp.int32, (S, S), 0)
        col = jax.lax.broadcasted_iota(jnp.int32, (S, S), 1)
        causal = col <= row
        scores = jnp.where(causal[None, :, :], scores, NEG)
        attn = jax.nn.softmax(scores, axis=-1)
        out = jnp.einsum('bst,btd->bsd', attn, x)
        return out

    def _L0_ffn_ref(x, fc1_w, fc1_b, fc2_w, fc2_b, gate_pair, atom_in_w, atom_in_b, atom_out_w, atom_out_b, balance_bias):
        import jax, jax.numpy as jnp
        import numpy as np
        ATOM = {'vm': 0, 'im': 1, 'cm': 2, 'sc': 3, 'cc': 4}
        TASK_PAIRS = [('vm', 'sc'), ('vm', 'cc'), ('im', 'sc'), ('im', 'cc'), ('cm', 'sc'), ('cm', 'cc')]
        SRC_IDX = np.array([[ATOM[l], ATOM[r]] for l, r in TASK_PAIRS], dtype=np.int32)
        DST_IDX = np.array([[ATOM[r], ATOM[l]] for l, r in TASK_PAIRS], dtype=np.int32)
        NCLS = 6
        NATOMS = 5

        def _l2norm(x, eps=1e-12):
            return x / jnp.clip(jnp.linalg.norm(x, axis=-1, keepdims=True), eps)
        src = jnp.asarray(SRC_IDX)
        dst = jnp.asarray(DST_IDX)
        D = x.shape[-1]
        H = atom_in_w.shape[1]
        cls_tokens = x[:, :NCLS]
        patch_tokens = x[:, NCLS:]
        patch_out = jax.nn.gelu(patch_tokens @ fc1_w.T + fc1_b, approximate=False) @ fc2_w.T + fc2_b
        gate_in = _l2norm(cls_tokens.astype(jnp.float32))
        gate_w = _l2norm(gate_pair.astype(jnp.float32))
        gate_logits = jnp.einsum('bnd,nrd->bnr', gate_in, gate_w) + balance_bias[None]
        route_probs = jax.nn.softmax(gate_logits, axis=-1)
        chosen_route = jnp.argmax(route_probs, axis=-1)
        hid_all = jax.nn.gelu(jnp.einsum('bnd,ahd->bnah', cls_tokens, atom_in_w) + atom_in_b[None, None], approximate=False)
        sh_pair = hid_all[:, jnp.arange(NCLS)[:, None], src, :]
        route_out_w = atom_out_w[dst.reshape(-1)].reshape(NCLS, 2, D, H)
        route_candidates = jnp.einsum('bnrh,nrdh->bnrd', sh_pair, route_out_w) + atom_out_b[dst][None]
        chosen_w = jnp.take_along_axis(route_probs, chosen_route[..., None], axis=-1)
        chosen_cand = jnp.take_along_axis(route_candidates, chosen_route[:, :, None, None], axis=2)[:, :, 0]
        cls_out = chosen_cand * chosen_w.astype(chosen_cand.dtype)
        return jnp.concatenate([cls_out, patch_out], axis=1)
    h = _L0_tok_ref(x, L0_tok_W, L0_tok_b)
    h = jnp.concatenate([h, txt], axis=1)
    h = h + _L0_attn_ref(_layernorm(h, axis=-1))
    h = h + _L0_ffn_ref(_layernorm(h, axis=-1), L0_ffn_fc1_w, L0_ffn_fc1_b, L0_ffn_fc2_w, L0_ffn_fc2_b, L0_ffn_gate_pair, L0_ffn_atom_in_w, L0_ffn_atom_in_b, L0_ffn_atom_out_w, L0_ffn_atom_out_b, L0_ffn_balance_bias)
    return h

_drawn_inputs = setup_inputs


def setup_inputs(seed=0):
    import zlib

    import numpy as np

    out = dict(_drawn_inputs(seed))
    spreads = {'L0_ffn_fc1_b': (0.0, 0.405),
     'L0_ffn_fc2_b': (0.0, 0.1),
     'L0_ffn_balance_bias': (0.0, 0.8)}
    factors = {'L0_ffn_gate_pair': 32.124,
     'L0_ffn_atom_in_w': 8.0,
     'L0_ffn_atom_in_b': 8.0,
     'L0_ffn_atom_out_w': 8.0,
     'L0_ffn_atom_out_b': 53.019}
    for name, (base, spread) in spreads.items():
        noise = np.random.default_rng([zlib.crc32(name.encode()), seed]).standard_normal(out[name].shape)
        drawn = base * np.exp(spread * noise) if base else spread * noise
        out[name] = jnp.asarray(drawn.astype(out[name].dtype))
    for name, factor in factors.items():
        out[name] = (out[name] * factor).astype(out[name].dtype)
    return out
```

```python
from contextlib import ExitStack

import concourse.bass as bass
import concourse.mybir as mybir

ALU = mybir.AluOpType
ACT = mybir.ActivationFunctionType
AX = mybir.AxisListType
F32 = mybir.dt.float32
F16 = mybir.dt.float16
U32 = mybir.dt.uint32
ABSMAX = bass.bass_isa.ReduceOp.absmax

NB = 32
D = 192
NI = 196
S = 273
PD = 768
KP = PD // 128
HID = 768
KH = HID // 128
NCLS, NATOM = 6, 5
EPS = 1e-5
MB = NI - 128
MC = S - 256
GC = 7
PC = GC * MC
NC = -(-NB // GC)
PCL = (NB - (NC - 1) * GC) * MC
ONE, HI, HI2, LO2, LO1, VW = 1, 2, 194, 258, 322, 450
FLO2, FLO1, FW = 192, 256, 384
SCALE = D ** -0.5
SHIFT = 15 * 0.6931471805599453 - D ** 0.5
MASKED = -30000.0
TOP = 2.0 ** 14
COLS_A, COLS_B = S, S - 128
PCOL_B, PCOL_C, PCOLS = COLS_A, COLS_A + COLS_B, COLS_A + COLS_B + MC
N_STEP = NB * 2 // 4

PAIRS = [(0, 3), (0, 4), (1, 3), (1, 4), (2, 3), (2, 4)]


def atom_tokens(a):
    return (2 * a, 1, 2, 0) if a < 3 else (a - 3, 2, 3, 1)


def valid(n, last):
    return not isinstance(n, int) or 0 <= n < last


def after(n, least):
    return not isinstance(n, int) or n >= least


def build(nc, x, wtok, btok, txtb, txtc, fc1, b1, fc2, b2, gatew, gateb, ain1, ain2, abin,
          aout, about1, about2, out_ab, out_c, out_cls):
    split_c = nc.dram_tensor("split_c", [NC * PC, VW], F16).ap()
    attn_c = nc.dram_tensor("attn_c", [NC * PC, D], F32).ap()
    ctx = ExitStack()
    with ctx:
        def sb(name, shape, dt, within=ctx):
            return within.enter_context(nc.sbuf_tensor(name, shape, dt))

        def sem(name):
            return ctx.enter_context(nc.semaphore(name))

        bank = [ctx.enter_context(nc.psum_tensor(f"bank{b}", [128, 512], F32)) for b in range(8)]

        h = sb("h", [128, 2 * NB, D], F32)
        hc = sb("hc", [PC, NC, D], F32)
        b2_sb = sb("b2_sb", [128, D], F32)
        ident = sb("ident", [128, 128], F16)
        ident32 = sb("ident32", [128, 128], F32)
        w1hi = sb("w1hi", [128, 2, HID], F16)
        w1lo = sb("w1lo", [128, 2, HID], F16)
        w2hi = sb("w2hi", [128, KH, D], F16)
        w2lo = sb("w2lo", [128, KH, D], F16)
        b1_sb = sb("b1_sb", [128, KH], F32)
        peak = sb("peak", [128, 3], F32)
        peaks = sb("peaks", [128, 4], F32)
        pow2 = sb("pow2", [128, 4], F32)
        up = sb("up", [128, 4], F32)
        down = sb("down", [128, 4], F32)
        shift = sb("shift", [128, 1], F32)
        eps = sb("eps", [128, 8], F32)
        half_neg = sb("half_neg", [128, 8], F32)
        x2 = sb("x2", [128, 2, 4, D], F32)
        v2 = sb("v2", [128, 2, 4, FW], F16)
        xt2 = sb("xt2", [128, 2, 3, 512], F16)
        st2 = sb("st2", [128, 4, 6], F32)
        mv2 = sb("mv2", [128, 4, 2], F32)
        ve2 = sb("ve2", [128, 4], F32)
        rstd2 = sb("rstd2", [128, 4], F32)

        actx = ctx.enter_context(ExitStack())
        x_sb = sb("x_sb", [128, 4, KP, NI], F32, actx)
        wtok_sb = sb("wtok_sb", [128, KP, D], F32, actx)
        hs = sb("hs", [128, 4, 2, D], F32, actx)
        btok_sb = sb("btok_sb", [128, D], F32, actx)
        never = sb("never", [128, 128], F16, actx)
        v = sb("v", [128, 4, 2, VW], F16, actx)
        vcall = sb("vcall", [MC, NB, VW], F16, actx)
        vc = sb("vc", [MC, 2, VW], F16, actx)
        xt = sb("xt", [128, 2, 4, S + 1], F16, actx)
        ct = sb("ct", [128, 4, NC * PC], F16, actx)
        x32 = sb("x32", [128, 2, 2, D], F32, actx)
        p32 = sb("p32", [128, 2, PCOLS], F32, actx)
        phi = sb("phi", [128, 2, PCOLS], F16, actx)
        plo = sb("plo", [128, 2, PCOLS], F16, actx)
        xc32 = sb("xc32", [PC, NC, D], F32, actx)
        vcp = sb("vcp", [PC, NC, VW], F16, actx)
        ac = sb("ac", [MC, 2, D], F32, actx)
        st = sb("st", [128, 2, 6], F32, actx)
        mv = sb("mv", [128, 2, 2], F32, actx)
        ve = sb("ve", [128, 2], F32, actx)
        rstd = sb("rstd", [128, 2], F32, actx)
        stc = sb("stc", [PC, NC, 6], F32, actx)
        mvc = sb("mvc", [PC, NC, 2], F32, actx)
        vec = sb("vec", [PC, NC], F32, actx)
        rstdc = sb("rstdc", [PC, NC], F32, actx)
        rden = sb("rden", [128, 3], F32, actx)
        w1st = sb("w1st", [128, 2, HID], F32, actx)
        w2st = sb("w2st", [128, KH, D], F32, actx)
        actx.close()

        bctx = ctx.enter_context(ExitStack())
        g32 = sb("g32", [128, 3, 512], F32, bctx)
        ghi = sb("ghi", [128, 2, KH, 512], F16, bctx)
        glo = sb("glo", [128, 2, KH, 512], F16, bctx)
        acp = sb("acp", [PC, NC, D], F32, bctx)
        ain1_sb = sb("ain1_sb", [128, NATOM, HID], F32, bctx)
        ain2_sb = sb("ain2_sb", [64, NATOM, HID], F32, bctx)
        aout_sb = sb("aout_sb", [128, NATOM, KH, D], F32, bctx)
        abin_sb = sb("abin_sb", [128, NATOM, KH], F32, bctx)
        about1_sb = sb("about1_sb", [128, NATOM], F32, bctx)
        about2_sb = sb("about2_sb", [64, NATOM], F32, bctx)
        hcls = sb("hcls", [96, 2, D], F32, bctx)
        xcls = sb("xcls", [96, 2, D], F32, bctx)
        gw_sb = sb("gw_sb", [96, 2, 2, D], F32, bctx)
        gb_sb = sb("gb_sb", [96, 2, 2], F32, bctx)
        scr = sb("scr", [96, D], F32, bctx)
        dots = sb("dots", [96, 2, 5], F32, bctx)
        sq = sb("sq", [96, 2, 3], F32, bctx)
        rn = sb("rn", [96, 2, 3], F32, bctx)
        lg = sb("lg", [96, 2, 8], F32, bctx)
        stk = sb("stk", [96, 2, 6], F32, bctx)
        mvk = sb("mvk", [96, 2, 2], F32, bctx)
        xct1 = sb("xct1", [128, NCLS, NB], F32, bctx)
        xct2 = sb("xct2", [64, NCLS, NB], F32, bctx)
        gt = sb("gt", [128, KH, 2, NCLS, NB], F32, bctx)
        cand1 = sb("cand1", [128, 2, NCLS, NB], F32, bctx)
        cand2 = sb("cand2", [64, 2, NCLS, NB], F32, bctx)

        ps_tok = [bank[0], bank[1]]
        ps_t = [bank[b][:, :].bitcast(F16)[:, 0:512].rearrange("p (k n) -> p k n", k=4) for b in (2, 6, 7)]
        ps_s = bank[3]
        ps_o, ps_oc = bank[4], bank[5]
        ps_t2 = [bank[b][:, :].bitcast(F16)[:, 0:768].rearrange("p (a k n) -> p a k n", a=2, k=3) for b in (2, 0)]
        ps_f1 = [bank[1], bank[6], bank[7]]
        ps_f2 = [bank[4], bank[5]]
        ps_ct = bank[3]

        ld_w = sem("ld_w")
        ld_x = [sem(f"ld_x{b}") for b in range(4)]
        ld_txtc = sem("ld_txtc")
        ld_txtb = [sem(f"ld_txtb{b}") for b in range(4)]
        ld_ffn = sem("ld_ffn")
        ld_split = sem("ld_split")
        st_split = sem("st_split")
        st_ac = [sem(f"st_ac{b}") for b in range(2)]
        ld_acp = sem("ld_acp")
        ld_atom = sem("ld_atom")
        ld_hcls = sem("ld_hcls")
        st_out = sem("st_out")
        const_ready = sem("const_ready")
        masks_ready = sem("masks_ready")
        c_stat = sem("c_stat")
        c_mv = sem("c_mv")
        c_ve = sem("c_ve")
        c_rstd = sem("c_rstd")
        c_norm = sem("c_norm")
        c_hi = sem("c_hi")
        c_split = sem("c_split")
        c_turned = sem("c_turned")
        c_kept = sem("c_kept")
        w_peak = sem("w_peak")
        w_peaks = sem("w_peaks")
        w_pow = sem("w_pow")
        w_split = sem("w_split")
        toka_done = sem("toka_done")
        tokb_done = sem("tokb_done")
        ha_ready = sem("ha_ready")
        hb_ready = sem("hb_ready")
        stat_done = sem("stat_done")
        mv_ready = sem("mv_ready")
        ve_ready = sem("ve_ready")
        rstd_ready = sem("rstd_ready")
        x32_ready = sem("x32_ready")
        vhi_ready = sem("vhi_ready")
        vlo_ready = sem("vlo_ready")
        t_done = sem("t_done")
        xt_ready = sem("xt_ready")
        xtc_ready = sem("xtc_ready")
        vc_ready = sem("vc_ready")
        qk_done = sem("qk_done")
        p_exp = sem("p_exp")
        p_lo = sem("p_lo")
        pv_done = sem("pv_done")
        rden_ready = sem("rden_ready")
        attn_added = sem("attn_added")
        hc_ready = sem("hc_ready")
        stat2_done = sem("stat2_done")
        mv2_ready = sem("mv2_ready")
        ve2_ready = sem("ve2_ready")
        rstd2_ready = sem("rstd2_ready")
        x2_ready = sem("x2_ready")
        v2hi_ready = sem("v2hi_ready")
        v2lo_ready = sem("v2lo_ready")
        h2b_ready = sem("h2b_ready")
        t2_done = sem("t2_done")
        xt2_ready = sem("xt2_ready")
        f1_done = sem("f1_done")
        gelu_done = sem("gelu_done")
        ghi_ready = sem("ghi_ready")
        glo_ready = sem("glo_ready")
        f2_done = sem("f2_done")
        y_ready = sem("y_ready")
        k_dve = sem("k_dve")
        k_ve = sem("k_ve")
        k_rstd = sem("k_rstd")
        k_rn = sem("k_rn")
        k_xcls = sem("k_xcls")
        k_turned = sem("k_turned")
        k_xct = sem("k_xct")
        k_hid = sem("k_hid")
        k_gelu = sem("k_gelu")
        k_cand = sem("k_cand")
        k_biased = sem("k_biased")
        k_back = sem("k_back")
        k_abs = sem("k_abs")
        k_tanh = sem("k_tanh")
        k_gates = sem("k_gates")
        k_out = sem("k_out")

        def slots(eng, slot, between=None):
            for i in range(-2, 2):
                slot(0, i)
                if between and i == 0:
                    between()
            with eng.Fori(0, (NB - 4) // 4) as t:
                for c in range(2, 6):
                    slot(t, c)
            for i in range(NB - 2, NB):
                slot(0, i)

        last_step = N_STEP + 2

        def steps(eng, step, between=None):
            for s in range(-2, 2):
                step(0, s)
                if between and s == 1:
                    between()
            with eng.Fori(0, (N_STEP - 4) // 2) as t:
                for c in range(2, 4):
                    step(t, c)
            for s in range(N_STEP - 2, last_step + 1):
                step(0, s)

        def tiles(s):
            if isinstance(s, int) and s >= N_STEP:
                return (4, PC) if s == N_STEP else (1, PCL)
            return 4, 128

        def rows(s, k):
            if isinstance(s, int) and s >= N_STEP:
                return hc[0:tiles(s)[1], 4 * (s - N_STEP) + k, :]
            return h[:, s * 4 + k, :]

        def rows_all(s):
            n, m = tiles(s)
            if isinstance(s, int) and s >= N_STEP:
                return hc[0:m, 4 * (s - N_STEP):4 * (s - N_STEP) + n, :]
            return h[:, bass.ds(s * 4, 4), :]

        def tiles_before(s):
            return s * 4 if not isinstance(s, int) or s <= N_STEP + 1 else 4 * (N_STEP + 1) + 1

        def pairs_before(s):
            return s * 2 if not isinstance(s, int) or s <= N_STEP + 1 else 2 * (N_STEP + 1) + 1

        block = ctx.enter_context(nc.Block())

        @block.sync
        def _(eng):
            eng.dma_start(hc[:, :, :], txtc).then_inc(ld_txtc, 16)
            eng.dma_start(wtok_sb[:, :, :], wtok).then_inc(ld_w, 16)
            eng.dma_start(x_sb[:, 0], x[0]).then_inc(ld_x[0], 16)
            eng.dma_start(btok_sb[:, :], btok).then_inc(ld_w, 16)
            eng.dma_start(x_sb[:, 1], x[1]).then_inc(ld_x[1], 16)
            for n in range(4):
                eng.dma_start(hs[MB:128, n, 1, :], txtb[n]).then_inc(ld_txtb[n], 16)
            eng.wait_ge(c_split, 2)
            eng.dma_start(split_c.rearrange("(c p) d -> p c d", p=PC), vcp[:, :, :]).then_inc(st_split, 16)
            eng.dma_start(x_sb[:, 2], x[2]).then_inc(ld_x[2], 16)
            eng.dma_start(x_sb[:, 3], x[3]).then_inc(ld_x[3], 16)
            eng.wait_ge(st_split, 16)
            eng.dma_start(vcall[:, :, :],
                          split_c[0:NB * MC, :].rearrange("(b p) d -> p b d", p=MC)).then_inc(ld_split, 16)
            eng.dma_start(w1st[:, :, :], fc1).then_inc(ld_ffn, 16)
            eng.dma_start(w2st[:, :, :], fc2).then_inc(ld_ffn, 16)
            eng.dma_start(b1_sb[:, :], b1).then_inc(ld_ffn, 16)
            eng.dma_start(b2_sb[:, :], b2).then_inc(ld_ffn, 16)

            def slot(t, c):
                i = t * 4 + c
                if valid(i, NB) and valid(i + 6, NB) or isinstance(i, int) and -2 <= i < 0:
                    eng.wait_ge(tokb_done, i + 3)
                    eng.dma_start(x_sb[:, (c + 2) % 4], x[i + 6]).then_inc(ld_x[(c + 2) % 4], 16)
                if valid(i, NB):
                    eng.wait_ge(attn_added, 3 * (i + 1))
                    eng.dma_start(attn_c[bass.ds(i * MC, MC), :], ac[:, c % 2, :]).then_inc(st_ac[c % 2], 16)
                    if valid(i + 4, NB):
                        eng.dma_start(hs[MB:128, c % 4, 1, :], txtb[i + 4]).then_inc(ld_txtb[c % 4], 16)

            for i in range(-2, 2):
                slot(0, i)
            with eng.Fori(0, 6) as t:
                for c in range(2, 6):
                    slot(t, c)
            for i in range(26, NB):
                slot(0, i)

            for b in range(2):
                eng.wait_ge(st_ac[b], 16 * NB // 2)
            eng.dma_start(acp[:, 0:NC - 1, :],
                          attn_c[0:(NC - 1) * PC, :].rearrange("(c p) d -> p c d", p=PC)).then_inc(ld_acp, 16)
            eng.dma_start(acp[0:PCL, NC - 1, :], attn_c[(NC - 1) * PC:NB * MC, :]).then_inc(ld_acp, 16)
            for n in range(NCLS):
                eng.dma_start(hcls[32 * (n % 3):32 * (n % 3) + 32, n // 3, :],
                              h[n:n + 1, 0:2 * NB:2, :]).then_inc(ld_hcls, 16)
            eng.dma_start(gw_sb[:, :, :, :], gatew).then_inc(ld_hcls, 16)
            eng.dma_start(gb_sb[:, :, :], gateb).then_inc(ld_hcls, 16)
            for dst, src in ((ain1_sb[:, :, :], ain1), (ain2_sb[:, :, :], ain2), (abin_sb[:, :, :], abin),
                             (aout_sb[:, :, :, :], aout), (about1_sb[:, :], about1), (about2_sb[:, :], about2)):
                eng.dma_start(dst, src).then_inc(ld_atom, 16)

            def step(t, c):
                s = t * 2 + c
                if valid(s - 1, last_step):
                    n, m = tiles(s - 1)
                    eng.wait_ge(y_ready, tiles_before(s - 1) + n)
                    if isinstance(s, int) and s - 1 >= N_STEP:
                        g = 4 * (s - 1 - N_STEP)
                        dst = out_c[0:m, g:g + n, :]
                    else:
                        dst = out_ab[s - 1]
                    eng.dma_start(dst, rows_all(s - 1)).then_inc(st_out, 16)

            def class_out():
                eng.wait_ge(k_out, 4)
                eng.dma_start(out_cls, hcls[:, :, :]).then_inc(st_out, 16)

            steps(eng, step, class_out)
            eng.wait_ge(st_out, 16 * (last_step + 1))

        @block.tensor
        def _(eng):
            def tokens(t, c, half):
                n, b, m = t * 4 + c, c % 4, (128, MB)[half]
                if not valid(n, NB):
                    return
                if half == 0:
                    if isinstance(n, int) and n == 0:
                        eng.wait_ge(ld_w, 32)
                    eng.wait_ge(ld_x[b], (t + (c // 4 + 1)) * 16)
                if after(n, 1):
                    eng.wait_ge((ha_ready, hb_ready)[half], n)
                for k in range(KP):
                    mm = eng.matmul(ps_tok[half][0:m, 0:D], x_sb[:, b, k, 128 * half:128 * half + m],
                                    wtok_sb[:, k, :], start=(k == 0), stop=(k == KP - 1))
                mm.then_inc((toka_done, tokb_done)[half], 1)

            def turn(t, c):
                n, b = t * 4 + c, c % 4
                if not valid(n, NB):
                    return
                eng.wait_ge(vhi_ready, 2 * (n + 1))
                eng.wait_ge(vlo_ready, 2 * (n + 1))
                if after(n, 1):
                    eng.wait_ge(xt_ready, 2 * n)
                for a in range(2):
                    for k, src in enumerate(split_columns(v[:, b, a, :])):
                        mm = eng.transpose(ps_t[a][:, k, :], src, ident[:, :])
                mm.then_inc(t_done, 1)

            def split_columns(r):
                return r[:, HI:HI + 128], r[:, LO1:LO1 + 128], r[:, HI2:HI2 + 128], r[:, HI + 128:HI2 + 64]

            def product(out, b, t0, t1, s0, s1):
                X = xt[:, b]
                eng.matmul(out, X[:, 0, t0:t1], X[:, 0, s0:s1], start=True, stop=False)
                eng.matmul(out, X[:, 0, t0:t1], X[:, 1, s0:s1], start=False, stop=False)
                eng.matmul(out, X[:, 1, t0:t1], X[:, 0, s0:s1], start=False, stop=False)
                eng.matmul(out, X[:, 3, t0:t1], X[:, 2, s0:s1], start=False, stop=False)
                eng.matmul(out, X[64:128, 2, t0:t1], X[64:128, 3, s0:s1], start=False, stop=False)

            def scores(t, c):
                n, b = t * 4 + c, c % 2
                if not valid(n, NB):
                    return
                eng.wait_ge(xt_ready, 2 * (n + 1))
                eng.wait_ge(xtc_ready, n + 1)
                if isinstance(n, int) and n == 0:
                    eng.wait_ge(masks_ready, 3)
                if after(n, 1):
                    eng.wait_ge(p_exp, 4 * n)
                for t0, t1, col, width in ((0, 128, 0, COLS_A), (128, 256, PCOL_B, COLS_B), (256, S, PCOL_C, MC)):
                    m = t1 - t0
                    product(ps_s[0:m, col:col + width], b, t0, t1, t0, S)
                    mm = eng.matmul(ps_s[0:m, col:col + m], ident[0:m, 0:m], never[0:m, 0:m],
                                    start=False, stop=True)
                mm.then_inc(qk_done, 1)

            def values(t, c):
                n, b, pb = t * 4 + c, c % 4, c % 2
                if not valid(n, NB):
                    return
                eng.wait_ge(p_exp, 4 * (n + 1))
                eng.wait_ge(p_lo, 2 * (n + 1))
                eng.wait_ge(vc_ready, n + 1)
                if after(n, 1):
                    eng.wait_ge(attn_added, 3 * n)
                blocks = ((128, 0), (128, PCOL_B - 128), (MC, PCOL_C - 256))
                for q, (s0, s1, out) in enumerate(((0, 128, ps_o[:, 0:D + 1]), (128, 256, ps_o[:, D + 1:2 * D + 2]),
                                                   (256, S, ps_oc[0:MC, 0:D + 1]))):
                    for r in range(q + 1):
                        m, col = blocks[r]
                        row = vc[:, pb, :] if r == 2 else v[:, b, r, :]
                        hi, lo = phi[0:m, pb, col + s0:col + s1], plo[0:m, pb, col + s0:col + s1]
                        eng.matmul(out, hi, row[:, ONE:HI2], start=(r == 0), stop=False)
                        eng.matmul(out, lo, row[:, ONE:HI2], start=False, stop=False)
                        eng.matmul(out[:, 129:D + 1], hi, row[:, LO2:LO1], start=False, stop=False)
                        mm = eng.matmul(out[:, 1:129], hi, row[:, LO1:VW], start=False, stop=(r == q))
                mm.then_inc(pv_done, 1)

            def turn_c():
                eng.wait_ge(masks_ready, 3)
                eng.wait_ge(c_split, 2)
                for g in range(NC):
                    if g:
                        eng.wait_ge(c_kept, g)
                    for k, src in enumerate(split_columns(vcp[:, g, :])):
                        mm = eng.transpose(ps_t[0][:, k, 0:PC], src, ident[0:PC, 0:PC])
                    mm.then_inc(c_turned, 1)
                eng.wait_ge(c_kept, NC)

            def slot(t, c):
                tokens(t, c + 2, 0)
                tokens(t, c + 2, 1)
                turn(t, c + 1)
                if isinstance(t, int) and c == -2:
                    turn_c()
                values(t, c)
                scores(t, c + 1)

            slots(eng, slot)

            def turn2(t, c):
                s, b = t * 2 + c, c % 2
                if not valid(s, last_step):
                    return
                n, m = tiles(s)
                eng.wait_ge(v2hi_ready, s + 1)
                eng.wait_ge(v2lo_ready, 2 * (s + 1))
                if isinstance(s, int) and s == 0:
                    eng.wait_ge(attn_added, 3 * NB)
                if after(s, 1):
                    eng.wait_ge(xt2_ready, pairs_before(s))
                for k in range(n):
                    for j, src in enumerate((v2[0:m, b, k, 0:128], v2[0:m, b, k, FLO1:FW], v2[0:m, b, k, 128:FLO1])):
                        mm = eng.transpose(ps_t2[k // 2][:, k % 2, j, 0:m], src, ident[0:m, 0:m])
                    if k % 2 or k == n - 1:
                        mm.then_inc(t2_done, 1)

            def fc1_products(t, c):
                s, b = t * 2 + c, c % 2
                if not valid(s, last_step):
                    return
                n, m = tiles(s)
                N = n * m
                eng.wait_ge(xt2_ready, pairs_before(s) + (n + 1) // 2)
                if isinstance(s, int) and s == 0:
                    eng.wait_ge(w_split, 4)
                X = xt2[:, b]
                for q in range(KH):
                    if after(s, 1) or q >= 3:
                        eng.wait_ge(gelu_done, s * KH + (q - 2))
                    out = ps_f1[q % 3][:, 0:N]
                    w = slice(128 * q, 128 * q + 128)
                    eng.matmul(out, w1hi[:, 0, w], X[:, 0, 0:N], start=True, stop=False)
                    eng.matmul(out, w1hi[:, 0, w], X[:, 1, 0:N], start=False, stop=False)
                    eng.matmul(out, w1lo[:, 0, w], X[:, 0, 0:N], start=False, stop=False)
                    eng.matmul(out, w1hi[:, 1, w], X[:, 2, 0:N], start=False, stop=False)
                    eng.matmul(out, w1lo[0:64, 1, w], X[0:64, 2, 0:N],
                               start=False, stop=True).then_inc(f1_done, 1)

            def fc2_products(t, c):
                s, b = t * 2 + c, c % 2
                if not valid(s, last_step):
                    return
                n, m = tiles(s)
                eng.wait_ge(ghi_ready, KH * (s + 1))
                eng.wait_ge(glo_ready, KH * (s + 1))
                if after(s, 1):
                    eng.wait_ge(y_ready, tiles_before(s))
                for k in range(n):
                    out = ps_f2[k // 2][0:m, D * (k % 2):D * (k % 2) + D]
                    for q in range(KH):
                        hi, lo = ghi[:, b, q, m * k:m * k + m], glo[:, b, q, m * k:m * k + m]
                        eng.matmul(out, hi, w2hi[:, q, :], start=(q == 0), stop=False)
                        eng.matmul(out, hi, w2lo[:, q, :], start=False, stop=False)
                        mm = eng.matmul(out, lo, w2hi[:, q, :], start=False, stop=(q == KH - 1))
                    if k % 2 or k == n - 1:
                        mm.then_inc(f2_done, 1)

            def step(t, c):
                turn2(t, c + 1)
                fc1_products(t, c)
                fc2_products(t, c - 1)

            def class_tokens():
                eng.wait_ge(k_xcls, 2)
                for j in range(2):
                    w = slice(96 * j, 96 * j + 96)
                    eng.transpose(ps_ct[:, w], xcls[:, j, 0:128], ident32[0:96, 0:96])
                    mm = eng.transpose(ps_ct[0:64, 192 + 96 * j:288 + 96 * j], xcls[:, j, 128:D],
                                       ident32[0:96, 0:96])
                mm.then_inc(k_turned, 1)
                eng.wait_ge(k_xct, 2)
                eng.wait_ge(ld_atom, 16 * 6)
                eng.wait_ge(gelu_done, 2 * KH)
                for a in range(NATOM):
                    n0, dn, n, _ = atom_tokens(a)
                    for q in range(KH):
                        u = 2 * a + q // 3
                        if q % 3 == 0 and u >= 3:
                            eng.wait_ge(k_gelu, 3 * (u - 2))
                        out = ps_f1[u % 3][:, 96 * (q % 3):96 * (q % 3) + NB * n]
                        w = slice(128 * q, 128 * q + 128)
                        eng.matmul(out, ain1_sb[:, a, w], xct1[:, n0:n0 + dn * (n - 1) + 1:dn, :],
                                   start=True, stop=False)
                        mm = eng.matmul(out, ain2_sb[:, a, w], xct2[:, n0:n0 + dn * (n - 1) + 1:dn, :],
                                        start=False, stop=True)
                        if q % 3 == 2:
                            mm.then_inc(k_hid, 1)
                eng.wait_ge(k_gelu, NATOM * KH)
                for a in range(NATOM):
                    n0, dn, n, r = atom_tokens(a)
                    for half, (m, out) in enumerate(((128, ps_f1[0]), (64, ps_f1[1]))):
                        out = out[0:m, 0:384].rearrange("p (r n b) -> p r n b", r=2, n=NCLS)
                        for q in range(KH):
                            mm = eng.matmul(out[:, 1 - r, n0:n0 + dn * (n - 1) + 1:dn, :],
                                            aout_sb[:, a, q, 128 * half:128 * half + m],
                                            gt[:, q, 1 - r, n0:n0 + dn * (n - 1) + 1:dn, :],
                                            start=(q == 0), stop=(q == KH - 1))
                        mm.then_inc(k_cand, 1)
                eng.wait_ge(k_biased, 2 * NATOM)
                for j in range(2):
                    for r in range(2):
                        out = (ps_f1[2], ps_ct)[j][0:96, D * r:D * r + D]
                        eng.transpose(out[:, 0:128], cand1[:, r, 3 * j:3 * j + 3, :], ident32[:, :])
                        mm = eng.transpose(out[:, 128:D], cand2[:, r, 3 * j:3 * j + 3, :], ident32[0:64, 0:64])
                    mm.then_inc(k_back, 1)
                eng.wait_ge(k_out, 4)

            steps(eng, step, class_tokens)

        @block.scalar
        def _(eng):
            eng.wait_ge(c_norm, NC)
            eng.copy(vcp[:, :, HI:HI2], xc32[:, :, :]).then_inc(c_hi, 1)
            eng.copy(vcp[:, :, HI2:LO2], xc32[:, :, 128:D]).then_inc(c_hi, 1)

            def keep_columns_b(t, c):
                n, b = t * 4 + c, c % 2
                if not valid(n, NB):
                    return
                eng.wait_ge(t_done, n + 1)
                if after(n, 2):
                    eng.wait_ge(qk_done, n - 1)
                eng.copy(xt[:, b, :, 128:256], ps_t[1][:, :, :]).then_inc(xt_ready, 1)

            def exponents(t, c):
                n, b = t * 4 + c, c % 2
                if valid(n, NB):
                    eng.wait_ge(qk_done, n + 1)
                    if after(n, 2):
                        eng.wait_ge(p_lo, 2 * (n - 1))
                        eng.wait_ge(pv_done, n - 1)
                    for dst in (p32, phi):
                        for m, c0, c1 in ((128, 0, PCOL_C), (MC, PCOL_C, PCOLS)):
                            eng.activation(dst[0:m, b, c0:c1], ps_s[0:m, c0:c1], ACT.Exp, bias=shift[0:m, 0:1],
                                           scale=SCALE).then_inc(p_exp, 1)

            def high_parts(t, c):
                n, b = t * 4 + c, c % 4
                if valid(n, NB):
                    eng.wait_ge(x32_ready, 2 * (n + 1))
                    if after(n, 4):
                        eng.wait_ge(pv_done, n - 3)
                    eng.copy(v[:, b, :, HI:HI2], x32[:, c % 2, :, :]).then_inc(vhi_ready, 1)
                    eng.copy(v[:, b, :, HI2:LO2], x32[:, c % 2, :, 128:D]).then_inc(vhi_ready, 1)

            def slot(t, c):
                keep_columns_b(t, c + 1)
                high_parts(t, c + 2)
                exponents(t, c + 1)

            slots(eng, slot)

            def gelu(t, c, q):
                s = t * 2 + c
                N = tiles(s)[0] * tiles(s)[1]
                eng.wait_ge(f1_done, s * KH + (q + 1))
                if after(s, 1) or q >= 3:
                    eng.wait_ge(glo_ready, s * KH + (q - 2))
                eng.activation(g32[:, q % 3, 0:N], ps_f1[q % 3][:, 0:N], ACT.Gelu, bias=b1_sb[:, q:q + 1],
                               scale=down[:, 0:1]).then_inc(gelu_done, 1)

            def gelu_hi(t, c, q):
                s = t * 2 + c
                N = tiles(s)[0] * tiles(s)[1]
                eng.wait_ge(gelu_done, s * KH + (q + 1))
                if q == 0 and after(s, 2):
                    eng.wait_ge(f2_done, pairs_before(s - 1))
                eng.activation(ghi[:, c % 2, q, 0:N], g32[:, q % 3, 0:N], ACT.Copy,
                               scale=up[:, 3:4]).then_inc(ghi_ready, 1)

            def step(t, c):
                s = t * 2 + c
                if valid(s, last_step):
                    for q in range(KH + 1):
                        if q < KH:
                            gelu(t, c, q)
                        if q:
                            gelu_hi(t, c, q - 1)
                n = t * 2 + (c + 2)
                if valid(n, last_step):
                    k, m = tiles(n)
                    eng.wait_ge(x2_ready, tiles_before(n) + k)
                    if after(n, 2):
                        eng.wait_ge(t2_done, pairs_before(n - 1))
                    eng.copy(v2[0:m, c % 2, 0:k, 0:D], x2[0:m, c % 2, 0:k, :]).then_inc(v2hi_ready, 1)

            def class_tokens():
                eng.wait_ge(ld_atom, 16 * 6)
                for a in range(NATOM):
                    n0, dn, n, r = atom_tokens(a)
                    for q in range(KH):
                        eng.wait_ge(k_hid, 2 * a + q // 3 + 1)
                        src = ps_f1[(2 * a + q // 3) % 3][:, 96 * (q % 3):96 * (q % 3) + NB * n]
                        eng.activation(gt[:, q, r, n0:n0 + dn * (n - 1) + 1:dn, :],
                                       src.rearrange("p (n b) -> p n b", b=NB), ACT.Gelu,
                                       bias=abin_sb[:, a, q:q + 1]).then_inc(k_gelu, 1)
                eng.wait_ge(k_abs, 2)
                eng.activation(lg[:, :, 3], lg[:, :, 2], ACT.Tanh, scale=0.5).then_inc(k_tanh, 1)
                for a in range(NATOM):
                    n0, dn, n, r = atom_tokens(a)
                    for half, (m, src, dst, bias) in enumerate(((128, ps_f1[0], cand1, about1_sb),
                                                                (64, ps_f1[1], cand2, about2_sb))):
                        eng.wait_ge(k_cand, 2 * NATOM)
                        src = src[0:m, 0:384].rearrange("p (r n b) -> p r n b", r=2, n=NCLS)
                        eng.activation(dst[:, 1 - r, n0:n0 + dn * (n - 1) + 1:dn, :],
                                       src[:, 1 - r, n0:n0 + dn * (n - 1) + 1:dn, :], ACT.Identity,
                                       bias=bias[:, a:a + 1]).then_inc(k_biased, 1)

            steps(eng, step, class_tokens)

        @block.gpsimd
        def _(eng):
            eng.memset(half_neg[:, :], -0.5).then_inc(const_ready, 1)
            eng.memset(eps[:, :], EPS).then_inc(const_ready, 1)
            eng.memset(shift[:, :], SHIFT).then_inc(const_ready, 1)
            eng.memset(ident[:, :], 0.0).then_inc(const_ready, 1)
            eng.memset(ident32[:, :], 0.0).then_inc(const_ready, 1)
            eng.memset(never[:, :], 0.0).then_inc(const_ready, 1)
            eng.memset(v[:, :, :, ONE:HI], 1.0).then_inc(const_ready, 1)
            eng.memset(v[:, :, :, 0:ONE], 0.0).then_inc(const_ready, 1)
            eng.memset(vcp[:, :, ONE:HI], 1.0).then_inc(const_ready, 1)
            eng.memset(vcp[:, :, 0:ONE], 0.0).then_inc(const_ready, 1)
            eng.wait_ge(const_ready, 10)
            eng.affine_select(out=ident[:, :], in_=ident[:, :], compare_op=ALU.not_equal, fill=1.0,
                              base=0, pattern=[[-1, 128]], channel_multiplier=1).then_inc(masks_ready, 1)
            eng.affine_select(out=ident32[:, :], in_=ident32[:, :], compare_op=ALU.not_equal, fill=1.0,
                              base=0, pattern=[[-1, 128]], channel_multiplier=1).then_inc(masks_ready, 1)
            eng.affine_select(out=never[:, :], in_=never[:, :], compare_op=ALU.is_ge, fill=MASKED,
                              base=0, pattern=[[1, 128]], channel_multiplier=-1).then_inc(masks_ready, 1)

            eng.wait_ge(c_mv, NC)
            eng.tensor_tensor(vec[:, :], mvc[:, :, 1], eps[0:PC, 0:NC], ALU.add).then_inc(c_ve, 1)
            eng.wait_ge(c_ve, 1)
            eng.tensor_tensor(rstdc[:, :], vec[:, :], half_neg[0:PC, 0:NC], ALU.pow).then_inc(c_rstd, 1)
            eng.wait_ge(c_hi, 2)
            eng.tensor_tensor(vcp[:, :, LO1:VW], xc32[:, :, 0:128], vcp[:, :, HI:HI + 128],
                              ALU.subtract).then_inc(c_split, 1)
            eng.tensor_tensor(vcp[:, :, LO2:LO1], xc32[:, :, 128:D], vcp[:, :, HI2:LO2],
                              ALU.subtract).then_inc(c_split, 1)

            def slot(t, c):
                n, b = t * 4 + (c + 1), (c + 1) % 2
                if valid(n, NB):
                    if isinstance(n, int) and n == 0:
                        eng.wait_ge(c_kept, NC)
                        eng.wait_ge(ld_split, 16)
                    if after(n, 2):
                        eng.wait_ge(qk_done, n - 1)
                    eng.tensor_copy(xt[:, b, :, 256:S], ct[:, :, bass.ds(n * MC, MC)]).then_inc(xtc_ready, 1)
                    if after(n, 2):
                        eng.wait_ge(pv_done, n - 1)
                    eng.tensor_copy(vc[:, b, :], vcall[:, n, :]).then_inc(vc_ready, 1)
                n, b = t * 4 + (c + 2), (c + 2) % 4
                if valid(n, NB):
                    eng.wait_ge(mv_ready, 2 * (n + 1))
                    eng.tensor_tensor(ve[:, :], mv[:, :, 1], eps[:, 0:2], ALU.add).then_inc(ve_ready, 1)
                    eng.wait_ge(ve_ready, n + 1)
                    eng.tensor_tensor(rstd[:, :], ve[:, :], half_neg[:, 0:2], ALU.pow).then_inc(rstd_ready, 1)
                    eng.wait_ge(vhi_ready, 2 * (n + 1))
                    eng.tensor_tensor(v[:, b, :, LO1:VW], x32[:, c % 2, :, 0:128], v[:, b, :, HI:HI + 128],
                                      ALU.subtract).then_inc(vlo_ready, 1)
                    eng.tensor_tensor(v[:, b, :, LO2:LO1], x32[:, c % 2, :, 128:D], v[:, b, :, HI2:LO2],
                                      ALU.subtract).then_inc(vlo_ready, 1)

            def weight_peaks():
                eng.wait_ge(w_peak, 3)
                eng.partition_all_reduce(peaks[:, 0:3], peak[:, :], 128, ABSMAX).then_inc(w_peaks, 1)

            slots(eng, slot, weight_peaks)

            def step(t, c):
                n, b = t * 2 + (c + 2), c % 2
                if not valid(n, last_step):
                    return
                k, m = tiles(n)
                eng.wait_ge(mv2_ready, tiles_before(n) + k)
                eng.tensor_tensor(ve2[0:m, 0:k], mv2[0:m, 0:k, 1], eps[0:m, 0:k], ALU.add).then_inc(ve2_ready, 1)
                eng.wait_ge(ve2_ready, n + 1)
                eng.tensor_tensor(rstd2[0:m, 0:k], ve2[0:m, 0:k], half_neg[0:m, 0:k], ALU.pow).then_inc(rstd2_ready, 1)
                eng.wait_ge(v2hi_ready, n + 1)
                eng.tensor_tensor(v2[0:m, b, 0:k, FLO1:FW], x2[0:m, b, 0:k, 0:128], v2[0:m, b, 0:k, 0:128],
                                  ALU.subtract).then_inc(v2lo_ready, 1)
                eng.tensor_tensor(v2[0:m, b, 0:k, FLO2:FLO1], x2[0:m, b, 0:k, 128:D], v2[0:m, b, 0:k, 128:D],
                                  ALU.subtract).then_inc(v2lo_ready, 1)
                if isinstance(n, int) and n == 0:
                    eng.wait_ge(ld_hcls, 16 * (NCLS + 2))
                r = rows_all(n)
                eng.tensor_tensor(r, r, b2_sb[0:m, :].unsqueeze(1).to_broadcast([m, k, D]),
                                  ALU.add).then_inc(h2b_ready, 1)

            def class_rows():
                eng.wait_ge(k_dve, 4)
                eng.tensor_tensor(lg[:, :, 0], mvk[:, :, 1], eps[0:96, 0:2], ALU.add).then_inc(k_ve, 1)
                eng.wait_ge(k_ve, 1)
                eng.tensor_tensor(lg[:, :, 1], lg[:, :, 0], half_neg[0:96, 0:2], ALU.pow).then_inc(k_rstd, 1)
                eng.wait_ge(k_gates, 1)
                eng.tensor_tensor(rn[:, :, :], sq[:, :, :],
                                  half_neg[0:96, 0:6].rearrange("p (a b) -> p a b", a=2), ALU.pow).then_inc(k_rn, 1)

            steps(eng, step, class_rows)

        @block.vector
        def _(eng):
            eng.wait_ge(ld_txtc, 16)
            for g in range(NC):
                eng.bn_stats(stc[:, g, :], hc[:, g, :]).then_inc(c_stat, 1)
            for g in range(NC):
                eng.wait_ge(c_stat, g + 1)
                eng.bn_aggr(mvc[:, g, :], stc[:, g, :]).then_inc(c_mv, 1)
            eng.wait_ge(c_rstd, 1)
            for g in range(NC):
                eng.tensor_scalar(xc32[:, g, :], hc[:, g, :], mvc[:, g, 0:1], rstdc[:, g:g + 1],
                                  ALU.subtract, ALU.mult).then_inc(c_norm, 1)

            def keep_c():
                for g in range(NC):
                    eng.wait_ge(c_turned, g + 1)
                    eng.tensor_copy(ct[:, :, PC * g:PC * g + PC], ps_t[0][:, :, 0:PC]).then_inc(c_kept, 1)

            def low_probs(t, c):
                n, b = t * 4 + c, c % 2
                if not valid(n, NB):
                    return
                eng.wait_ge(p_exp, 4 * (n + 1))
                if after(n, 2):
                    eng.wait_ge(pv_done, n - 1)
                for m, c0, c1 in ((128, 0, PCOL_C), (MC, PCOL_C, PCOLS)):
                    eng.tensor_tensor(plo[0:m, b, c0:c1], p32[0:m, b, c0:c1], phi[0:m, b, c0:c1],
                                      ALU.subtract).then_inc(p_lo, 1)

            def add_bias(t, c, half):
                n, b, m = t * 4 + c, c % 4, (128, MB)[half]
                if not valid(n, NB):
                    return
                done, ready = ((toka_done, ha_ready), (tokb_done, hb_ready))[half]
                eng.wait_ge(done, n + 1)
                eng.tensor_tensor(hs[0:m, b, half, :], ps_tok[half][0:m, 0:D], btok_sb[0:m, :],
                                  ALU.add).then_inc(ready, 1)

            def statistics1(t, c, half):
                n, b = t * 4 + c, c % 4
                if not valid(n, NB):
                    return
                if half:
                    eng.wait_ge(ld_txtb[b], (t + (c // 4 + 1)) * 16)
                eng.wait_ge((ha_ready, hb_ready)[half], n + 1)
                eng.bn_stats(st[:, half, :], hs[:, b, half, :]).then_inc(stat_done, 1)

            def aggregate(t, c, half):
                if valid(t * 4 + c, NB):
                    eng.bn_aggr(mv[:, half, :], st[:, half, :]).then_inc(mv_ready, 1)

            def statistics_there(t, c, half):
                n = t * 4 + c
                if valid(n, NB):
                    eng.wait_ge(stat_done, n * 2 + (half + 1))

            def keep_columns(t, c):
                n, b = t * 4 + c, c % 2
                if not valid(n, NB):
                    return
                eng.wait_ge(t_done, n + 1)
                if after(n, 2):
                    eng.wait_ge(qk_done, n - 1)
                eng.tensor_copy(xt[:, b, :, 0:128], ps_t[0][:, :, :]).then_inc(xt_ready, 1)

            def normalise(t, c):
                n, b = t * 4 + c, c % 2
                if not valid(n, NB):
                    return
                eng.wait_ge(mv_ready, 2 * (n + 1))
                eng.wait_ge(rstd_ready, n + 1)
                if after(n, 2):
                    eng.wait_ge(vlo_ready, 2 * (n - 1))
                for a in range(2):
                    eng.tensor_scalar(x32[:, b, a, :], hs[:, c % 4, a, :], mv[:, a, 0:1], rstd[:, a:a + 1],
                                      ALU.subtract, ALU.mult).then_inc(x32_ready, 1)

            def denominators(t, c):
                n = t * 4 + c
                if not valid(n, NB):
                    return
                eng.wait_ge(pv_done, n + 1)
                eng.reciprocal(rden[:, 0:2], ps_o[:, 0:D + 2:D + 1]).then_inc(rden_ready, 1)
                eng.reciprocal(rden[0:MC, 2:3], ps_oc[0:MC, 0:1]).then_inc(rden_ready, 1)

            def add_attention(t, c):
                n, b = t * 4 + c, c % 2
                if not valid(n, NB):
                    return
                eng.wait_ge(rden_ready, 2 * (n + 1))
                for a in range(2):
                    eng.scalar_tensor_tensor(h[:, n * 2 + a, :], ps_o[:, (D + 1) * a + 1:(D + 1) * (a + 1)],
                                             rden[:, a:a + 1], hs[:, c % 4, a, :],
                                             ALU.mult, ALU.add).then_inc(attn_added, 1)
                if after(n, 2):
                    eng.wait_ge(st_ac[b], (t * 2 + c // 2) * 16)
                eng.tensor_scalar(ac[:, b, :], ps_oc[0:MC, 1:D + 1], rden[0:MC, 2:3], None,
                                  ALU.mult).then_inc(attn_added, 1)

            def slot(t, c):
                low_probs(t, c)
                add_bias(t, c + 2, 0)
                statistics1(t, c + 2, 0)
                statistics_there(t, c + 2, 0)
                add_bias(t, c + 2, 1)
                aggregate(t, c + 2, 0)
                statistics1(t, c + 2, 1)
                if isinstance(t, int) and c == -2:
                    keep_c()
                statistics_there(t, c + 2, 1)
                keep_columns(t, c + 1)
                aggregate(t, c + 2, 1)
                denominators(t, c)
                normalise(t, c + 2)
                add_attention(t, c)

            def split_weights():
                eng.wait_ge(ld_ffn, 64)
                eng.tensor_reduce(peak[:, 0:1], w1st[:, :, :], AX.XY, ALU.max, apply_absolute_value=True).then_inc(w_peak, 1)
                eng.tensor_reduce(peak[:, 1:2], b1_sb[:, :], AX.X, ALU.max, apply_absolute_value=True).then_inc(w_peak, 1)
                eng.tensor_reduce(peak[:, 2:3], w2st[:, :, :], AX.XY, ALU.max, apply_absolute_value=True).then_inc(w_peak, 1)
                eng.wait_ge(w_peaks, 1)
                eng.scalar_tensor_tensor(peaks[:, 3:4], peaks[:, 0:1], float(D), peaks[:, 1:2],
                                         ALU.mult, ALU.add).then_inc(w_pow, 1)
                eng.wait_ge(w_pow, 1)
                eng.tensor_scalar(peaks[:, :], peaks[:, :], 2.0 ** -60, None, ALU.max).then_inc(w_pow, 1)
                eng.wait_ge(w_pow, 2)
                eng.tensor_scalar(pow2[:, :].bitcast(U32), peaks[:, :].bitcast(U32), 0x7F800000, None,
                                  ALU.bitwise_and).then_inc(w_pow, 1)
                eng.wait_ge(w_pow, 3)
                eng.tensor_scalar(down[:, :], pow2[:, :], 1 / TOP, None, ALU.mult).then_inc(w_pow, 1)
                eng.wait_ge(w_pow, 4)
                eng.reciprocal(up[:, :], down[:, :]).then_inc(w_pow, 1)
                eng.wait_ge(w_pow, 5)
                eng.tensor_tensor(down[:, 1:2], down[:, 2:3], down[:, 3:4], ALU.mult).then_inc(w_pow, 1)
                eng.wait_ge(w_pow, 6)
                for src, hi, lo, k in ((w1st, w1hi, w1lo, 0), (w2st, w2hi, w2lo, 2)):
                    eng.tensor_scalar(hi[:, :, :], src[:, :, :], up[:, k:k + 1], None, ALU.mult).then_inc(w_split, 1)
                for n, (src, hi, lo, k) in enumerate(((w1st, w1hi, w1lo, 0), (w2st, w2hi, w2lo, 2))):
                    eng.wait_ge(w_split, n + 1)
                    eng.scalar_tensor_tensor(lo[:, :, :], src[:, :, :], up[:, k:k + 1], hi[:, :, :],
                                             ALU.mult, ALU.subtract).then_inc(w_split, 1)

            slots(eng, slot, split_weights)
            eng.wait_ge(attn_added, 3 * NB)

            def statistics(t, c):
                s = t * 2 + c
                if not valid(s, last_step):
                    return
                n, m = tiles(s)
                if isinstance(s, int) and s == N_STEP:
                    eng.wait_ge(ld_acp, 32)
                    eng.tensor_tensor(hc[:, 0:NC - 1, :], hc[:, 0:NC - 1, :], acp[:, 0:NC - 1, :],
                                      ALU.add).then_inc(hc_ready, 1)
                    eng.tensor_tensor(hc[0:PCL, NC - 1, :], hc[0:PCL, NC - 1, :], acp[0:PCL, NC - 1, :],
                                      ALU.add).then_inc(hc_ready, 1)
                    eng.wait_ge(hc_ready, 2)
                for k in range(n):
                    eng.bn_stats(st2[0:m, k, :], rows(s, k)).then_inc(stat2_done, 1)
                eng.wait_ge(stat2_done, tiles_before(s) + n)

            def aggregate2(t, c):
                s = t * 2 + c
                if not valid(s, last_step):
                    return
                n, m = tiles(s)
                for k in range(n):
                    eng.bn_aggr(mv2[0:m, k, :], st2[0:m, k, :]).then_inc(mv2_ready, 1)

            def normalise2(t, c):
                s, b = t * 2 + c, c % 2
                if not valid(s, last_step):
                    return
                n, m = tiles(s)
                eng.wait_ge(mv2_ready, tiles_before(s) + n)
                eng.wait_ge(rstd2_ready, s + 1)
                if after(s, 2):
                    eng.wait_ge(v2lo_ready, 2 * (s - 1))
                for k in range(n):
                    eng.tensor_scalar(x2[0:m, b, k, :], rows(s, k), mv2[0:m, k, 0:1], rstd2[0:m, k:k + 1],
                                      ALU.subtract, ALU.mult).then_inc(x2_ready, 1)

            def keep_columns2(t, c):
                s, b = t * 2 + c, c % 2
                if not valid(s, last_step):
                    return
                n, m = tiles(s)
                if after(s, 2):
                    eng.wait_ge(f1_done, (s - 1) * KH)
                for j in range((n + 1) // 2):
                    w = min(2, n - 2 * j)
                    eng.wait_ge(t2_done, pairs_before(s) + (j + 1))
                    eng.tensor_copy(xt2[:, b, :, 2 * m * j:2 * m * j + w * m].rearrange("p k (a n) -> p a k n", a=w),
                                    ps_t2[j][:, 0:w, :, 0:m]).then_inc(xt2_ready, 1)

            def low_gelu(t, c, q):
                s = t * 2 + c
                if not valid(s, last_step):
                    return
                N = tiles(s)[0] * tiles(s)[1]
                eng.wait_ge(ghi_ready, s * KH + (q + 1))
                if q == 0 and after(s, 2):
                    eng.wait_ge(f2_done, pairs_before(s - 1))
                eng.scalar_tensor_tensor(glo[:, c % 2, q, 0:N], g32[:, q % 3, 0:N], up[:, 3:4],
                                         ghi[:, c % 2, q, 0:N], ALU.mult, ALU.subtract).then_inc(glo_ready, 1)

            def outputs(t, c):
                s = t * 2 + c
                if not valid(s, last_step):
                    return
                n, m = tiles(s)
                eng.wait_ge(h2b_ready, s + 1)
                for k in range(n):
                    if k % 2 == 0:
                        eng.wait_ge(f2_done, pairs_before(s) + (k // 2 + 1))
                    eng.scalar_tensor_tensor(rows(s, k), ps_f2[k // 2][0:m, D * (k % 2):D * (k % 2) + D],
                                             down[0:m, 1:2], rows(s, k), ALU.mult, ALU.add).then_inc(y_ready, 1)

            def step(t, c):
                statistics(t, c + 2)
                keep_columns2(t, c + 1)
                aggregate2(t, c + 2)
                for q in range(3):
                    low_gelu(t, c, q)
                normalise2(t, c + 2)
                for q in range(3, KH):
                    low_gelu(t, c, q)
                outputs(t, c - 1)

            def class_rows():
                eng.wait_ge(ld_hcls, 16 * (NCLS + 2))
                for j in range(2):
                    eng.bn_stats(stk[:, j, :], hcls[:, j, :]).then_inc(k_dve, 1)
                eng.wait_ge(k_dve, 2)
                for j in range(2):
                    eng.bn_aggr(mvk[:, j, :], stk[:, j, :]).then_inc(k_dve, 1)
                eng.wait_ge(k_dve, 4)
                eng.wait_ge(k_rstd, 1)
                for j in range(2):
                    eng.tensor_scalar(xcls[:, j, :], hcls[:, j, :], mvk[:, j, 0:1], lg[:, j, 1:2],
                                      ALU.subtract, ALU.mult).then_inc(k_xcls, 1)
                eng.wait_ge(k_xcls, 2)
                count = 4
                for j in range(2):
                    w0, w1, xr = gw_sb[:, j, 0, :], gw_sb[:, j, 1, :], xcls[:, j, :]
                    for k, (a, b) in enumerate(((xr, w0), (xr, w1), (xr, xr), (w0, w0), (w1, w1))):
                        eng.wait_ge(k_dve, count)
                        eng.tensor_tensor_reduce(scr[:, :], a, b, 1.0, 0.0, ALU.mult, ALU.add,
                                                 dots[:, j, k:k + 1]).then_inc(k_dve, 1)
                        count += 1
                eng.wait_ge(k_dve, count)
                eng.tensor_scalar(sq[:, :, :], dots[:, :, 2:5], 1e-24, None, ALU.max).then_inc(k_gates, 1)
                eng.wait_ge(k_turned, 1)
                eng.tensor_copy(xct1[:, :, :], ps_ct[:, 0:192].rearrange("p (n b) -> p n b", b=NB)).then_inc(k_xct, 1)
                eng.tensor_copy(xct2[:, :, :],
                                ps_ct[0:64, 192:384].rearrange("p (n b) -> p n b", b=NB)).then_inc(k_xct, 1)
                eng.wait_ge(k_rn, 1)
                link = [count]

                def linked(ins):
                    link[0] += 1
                    ins.then_inc(k_dve, 1)
                    eng.wait_ge(k_dve, link[0])

                linked(eng.tensor_tensor(dots[:, :, 0:2], dots[:, :, 0:2], rn[:, :, 1:3], ALU.mult))
                linked(eng.tensor_tensor(lg[:, :, 4], dots[:, :, 1], dots[:, :, 0], ALU.subtract))
                linked(eng.tensor_tensor(lg[:, :, 4], lg[:, :, 4], rn[:, :, 0], ALU.mult))
                linked(eng.tensor_tensor(lg[:, :, 5], gb_sb[:, :, 1], gb_sb[:, :, 0], ALU.subtract))
                linked(eng.tensor_tensor(lg[:, :, 6], lg[:, :, 4], lg[:, :, 5], ALU.add))
                eng.scalar_tensor_tensor(lg[:, :, 2], lg[:, :, 6], -1.0, lg[:, :, 6], ALU.mult, ALU.max).then_inc(k_abs, 1)
                eng.tensor_scalar(lg[:, :, 7], lg[:, :, 6], 0.0, None, ALU.is_gt).then_inc(k_abs, 1)
                eng.wait_ge(k_abs, 2)
                eng.wait_ge(k_tanh, 1)
                linked(eng.tensor_scalar(lg[:, :, 4], lg[:, :, 3], 0.5, 0.5, ALU.mult, ALU.add))
                linked(eng.tensor_tensor(lg[:, :, 5], lg[:, :, 4], lg[:, :, 7], ALU.mult))
                linked(eng.tensor_tensor(lg[:, :, 6], lg[:, :, 4], lg[:, :, 5], ALU.subtract))
                eng.wait_ge(k_back, 2)
                for r in range(2):
                    for j in range(2):
                        src = (ps_f1[2], ps_ct)[j][0:96, D * r:D * r + D]
                        eng.scalar_tensor_tensor(hcls[:, j, :], src, lg[:, j, 6 - r:7 - r], hcls[:, j, :],
                                                 ALU.mult, ALU.add).then_inc(k_out, 1)
                    if r == 0:
                        eng.wait_ge(k_out, 2)

            steps(eng, step, class_rows)


_OUT_AB = (N_STEP, 128, 4, D)
_OUT_C = (PC, NC, D)
_OUT_CLS = (96, 2, D)


def kernel(**inputs):
    import numpy as np
    import concourse.bacc as bacc
    from concourse import mybir as mb
    from concourse.bass_utils import run_bass_kernel_spmd as run

    a = {k: np.asarray(val) for k, val in inputs.items()}
    x = a["x"].reshape(NB, 3, 14, 16, 14, 16).transpose(0, 1, 3, 5, 2, 4).reshape(NB, KP, 128, NI)
    txt = a["txt"]
    txtc = np.zeros((NC * PC, D), txt.dtype)
    txtc[:NB * MC] = txt[:, 77 - MC:].reshape(NB * MC, D)
    fc1 = a["L0_ffn_fc1_w"].T
    ain = a["L0_ffn_atom_in_w"].transpose(2, 0, 1)
    aout = a["L0_ffn_atom_out_w"].transpose(0, 2, 1).reshape(NATOM, KH, 128, D)
    about = a["L0_ffn_atom_out_b"].T

    def per_class(w):
        w = w.reshape(2, 3, 1, *w.shape[1:]).swapaxes(0, 1)
        w = np.broadcast_to(w, (3, 2, NB) + w.shape[3:])
        return w.swapaxes(1, 2).reshape(96, 2, *w.shape[3:])

    laid = {
        "x": x.transpose(0, 2, 1, 3),
        "wtok": a["L0_tok_W"].T.reshape(KP, 128, D).transpose(1, 0, 2),
        "btok": np.broadcast_to(a["L0_tok_b"], (128, D)),
        "txtb": txt[:, :77 - MC],
        "txtc": txtc.reshape(NC, PC, D).transpose(1, 0, 2),
        "fc1": np.stack([fc1[:128], np.concatenate([fc1[128:], fc1[128:]])], 1),
        "b1": a["L0_ffn_fc1_b"].reshape(KH, 128).T,
        "fc2": a["L0_ffn_fc2_w"].T.reshape(KH, 128, D).transpose(1, 0, 2),
        "b2": np.broadcast_to(a["L0_ffn_fc2_b"], (128, D)),
        "gatew": per_class(a["L0_ffn_gate_pair"]),
        "gateb": per_class(a["L0_ffn_balance_bias"]),
        "ain1": ain[:128],
        "ain2": ain[128:],
        "abin": a["L0_ffn_atom_in_b"].reshape(NATOM, KH, 128).transpose(2, 0, 1),
        "aout": aout.transpose(2, 0, 1, 3),
        "about1": about[:128],
        "about2": about[128:],
    }
    nc = bacc.Bacc("TRN2", target_bir_lowering=False, num_devices=1)
    arrays, args = {}, []
    for name, val in laid.items():
        val = np.ascontiguousarray(val)
        arrays[f"in_{name}"] = val
        args.append(nc.dram_tensor(f"in_{name}", val.shape, mb.dt.from_np(val.dtype), kind="ExternalInput").ap())
    for name, shape in (("ab", _OUT_AB), ("c", _OUT_C), ("cls", _OUT_CLS)):
        args.append(nc.dram_tensor(f"out_{name}", shape, F32, kind="ExternalOutput").ap())
    build(nc, *args)
    r = run(nc, [arrays], core_ids=[0]).results[0]
    out = np.empty((NB, S, D), np.float32)
    out[:, :256] = np.asarray(r["out_ab"]).reshape(N_STEP, 128, 2, 2, D).transpose(0, 2, 3, 1, 4).reshape(NB, 256, D)
    out[:, 256:] = np.asarray(r["out_c"]).transpose(1, 0, 2).reshape(NC * PC, D)[:NB * MC].reshape(NB, MC, D)
    cls = np.asarray(r["out_cls"]).reshape(3, NB, 2, D).transpose(1, 2, 0, 3)
    out[:, :NCLS] = cls.reshape(NB, NCLS, D)
    return out
```

```python
from contextlib import ExitStack

import concourse.bass as bass
import concourse.mybir as mybir

ALU = mybir.AluOpType
ACT = mybir.ActivationFunctionType
AX = mybir.AxisListType
F32 = mybir.dt.float32
F16 = mybir.dt.float16
U32 = mybir.dt.uint32
ABSMAX = bass.bass_isa.ReduceOp.absmax

NB = 32
D = 192
NI = 196
S = 273
PD = 768
KP = PD // 128
HID = 768
KH = HID // 128
NCLS, NATOM = 6, 5
EPS = 1e-5
MB = NI - 128
MC = S - 256
GC = 7
PC = GC * MC
NC = -(-NB // GC)
PCL = (NB - (NC - 1) * GC) * MC
ONE, HI, HI2, LO2, LO1, VW = 1, 2, 194, 258, 322, 450
FLO2, FLO1, FW = 192, 256, 384
SCALE = D ** -0.5
SHIFT = 15 * 0.6931471805599453 - D ** 0.5
MASKED = -30000.0
TOP = 2.0 ** 14
COLS_A, COLS_B = S, S - 128
PCOL_B, PCOL_C, PCOLS = COLS_A, COLS_A + COLS_B, COLS_A + COLS_B + MC
LOOPED = NB - 10
LN_SLOT = LOOPED + 2
WARM_UP = 24
N_STEP = NB * 2 // 4

PAIRS = [(0, 3), (0, 4), (1, 3), (1, 4), (2, 3), (2, 4)]


def atom_tokens(a):
    return (2 * a, 1, 2, 0) if a < 3 else (a - 3, 2, 3, 1)


def valid(n, last):
    return not isinstance(n, int) or 0 <= n < last


def after(n, least):
    return not isinstance(n, int) or n >= least


def build(nc, x, wtok, btok, txtb, txtc, fc1, b1, fc2, b2, gatew, gateb, ain1, ain2, abin,
          aout, about1, about2, out_ab, out_c, out_cls):
    split_c = nc.dram_tensor("split_c", [NC * PC, VW], F16).ap()
    attn_c = nc.dram_tensor("attn_c", [NC * PC, D], F32).ap()
    rows_cls = nc.dram_tensor("rows_cls", [NCLS, NB, D], F32).ap()
    ctx = ExitStack()
    with ctx:
        def sb(name, shape, dt, within=ctx):
            return within.enter_context(nc.sbuf_tensor(name, shape, dt))

        def sem(name):
            return ctx.enter_context(nc.semaphore(name))

        bank = [ctx.enter_context(nc.psum_tensor(f"bank{b}", [128, 512], F32)) for b in range(8)]

        h = sb("h", [128, 2 * NB, D], F32)
        hc = sb("hc", [PC, NC, D], F32)
        b2_sb = sb("b2_sb", [128, D], F32)
        ident = sb("ident", [128, 128], F16)
        ident32 = sb("ident32", [128, 128], F32)
        w1hi = sb("w1hi", [128, 2, HID], F16)
        w1lo = sb("w1lo", [128, 2, HID], F16)
        w2hi = sb("w2hi", [128, KH, D], F16)
        w2lo = sb("w2lo", [128, KH, D], F16)
        b1_sb = sb("b1_sb", [128, KH], F32)
        peak = sb("peak", [128, 3], F32)
        peaks = sb("peaks", [128, 4], F32)
        pow2 = sb("pow2", [128, 4], F32)
        up = sb("up", [128, 4], F32)
        down = sb("down", [128, 4], F32)
        shift = sb("shift", [128, 1], F32)
        eps = sb("eps", [128, 8], F32)
        half_neg = sb("half_neg", [128, 8], F32)
        x2 = sb("x2", [128, 2, 4, D], F32)
        v2 = sb("v2", [128, 2, 4, FW], F16)
        xt2 = sb("xt2", [128, 2, 3, 512], F16)
        st2 = sb("st2", [128, 4, 6], F32)
        mv2 = sb("mv2", [128, 4, 2], F32)
        ve2 = sb("ve2", [128, 4], F32)
        rstd2 = sb("rstd2", [128, 4], F32)

        actx = ctx.enter_context(ExitStack())
        x_sb = sb("x_sb", [128, 4, KP, NI], F32, actx)
        wtok_sb = sb("wtok_sb", [128, KP, D], F32, actx)
        w1st = sb("w1st", [128, 2, HID], F32, actx)
        w2st = sb("w2st", [128, KH, D], F32, actx)
        hs = sb("hs", [128, 4, 2, D], F32, actx)
        btok_sb = sb("btok_sb", [128, D], F32, actx)
        never = sb("never", [128, 128], F16, actx)
        v = sb("v", [128, 4, 2, VW], F16, actx)
        vc = sb("vc", [MC, 4, VW], F16, actx)
        xt = sb("xt", [128, 2, 4, S + 1], F16, actx)
        ct = sb("ct", [128, 4, NC * PC], F16, actx)
        x32 = sb("x32", [128, 2, 2, D], F32, actx)
        p32 = sb("p32", [128, 2, PCOLS], F32, actx)
        phi = sb("phi", [128, 2, PCOLS], F16, actx)
        plo = sb("plo", [128, 2, PCOLS], F16, actx)
        xc32 = sb("xc32", [PC, NC, D], F32, actx)
        vcp = sb("vcp", [PC, NC, VW], F16, actx)
        ac = sb("ac", [MC, 2, D], F32, actx)
        st = sb("st", [128, 2, 6], F32, actx)
        mv = sb("mv", [128, 2, 2], F32, actx)
        ve = sb("ve", [128, 2], F32, actx)
        rstd = sb("rstd", [128, 2], F32, actx)
        stc = sb("stc", [PC, NC, 6], F32, actx)
        mvc = sb("mvc", [PC, NC, 2], F32, actx)
        vec = sb("vec", [PC, NC], F32, actx)
        rstdc = sb("rstdc", [PC, NC], F32, actx)
        rden = sb("rden", [128, 3], F32, actx)
        actx.close()

        bctx = ctx.enter_context(ExitStack())
        g32 = sb("g32", [128, 3, 512], F32, bctx)
        ghi = sb("ghi", [128, 2, KH, 512], F16, bctx)
        glo = sb("glo", [128, 2, KH, 512], F16, bctx)
        acp = sb("acp", [PC, NC, D], F32, bctx)
        ain1_sb = sb("ain1_sb", [128, NATOM, HID], F32, bctx)
        ain2_sb = sb("ain2_sb", [64, NATOM, HID], F32, bctx)
        aout_sb = sb("aout_sb", [128, NATOM, KH, D], F32, bctx)
        abin_sb = sb("abin_sb", [128, NATOM, KH], F32, bctx)
        about1_sb = sb("about1_sb", [128, NATOM], F32, bctx)
        about2_sb = sb("about2_sb", [64, NATOM], F32, bctx)
        hcls = sb("hcls", [96, 2, D], F32, bctx)
        xcls = sb("xcls", [96, 2, D], F32, bctx)
        gw_sb = sb("gw_sb", [96, 2, 2, D], F32, bctx)
        gb_sb = sb("gb_sb", [96, 2, 2], F32, bctx)
        scr = sb("scr", [96, D], F32, bctx)
        dots = sb("dots", [96, 2, 5], F32, bctx)
        sq = sb("sq", [96, 2, 3], F32, bctx)
        rn = sb("rn", [96, 2, 3], F32, bctx)
        lg = sb("lg", [96, 2, 8], F32, bctx)
        stk = sb("stk", [96, 2, 6], F32, bctx)
        mvk = sb("mvk", [96, 2, 2], F32, bctx)
        xct1 = sb("xct1", [128, NCLS, NB], F32, bctx)
        xct2 = sb("xct2", [64, NCLS, NB], F32, bctx)
        gt = sb("gt", [128, KH, 2, NCLS, NB], F32, bctx)
        cand1 = sb("cand1", [128, 2, NCLS, NB], F32, bctx)
        cand2 = sb("cand2", [64, 2, NCLS, NB], F32, bctx)

        ps_tok = [bank[0], bank[1]]
        ps_t = [bank[b][:, :].bitcast(F16)[:, 0:512].rearrange("p (k n) -> p k n", k=4) for b in (2, 6)]
        ps_tc = [bank[b][:, :].bitcast(F16)[:, 0:512].rearrange("p (k n) -> p k n", k=4) for b in (6, 7, 3, 4, 5)]
        ps_s = bank[3]
        ps_o, ps_oc = bank[4], bank[5]
        ps_t2 = [bank[b][:, :].bitcast(F16)[:, 0:768].rearrange("p (a k n) -> p a k n", a=2, k=3) for b in (0, 1)]
        ps_f1 = [bank[2], bank[6], bank[7]]
        ps_f2 = [bank[4], bank[5]]
        ps_ct = bank[3]

        ld_w = sem("ld_w")
        ld_x = [sem(f"ld_x{b}") for b in range(4)]
        ld_txtc = sem("ld_txtc")
        ld_txtb = [sem(f"ld_txtb{b}") for b in range(4)]
        ld_ffn = sem("ld_ffn")
        ld_vc = [sem(f"ld_vc{b}") for b in range(4)]
        st_split = sem("st_split")
        st_ac = [sem(f"st_ac{b}") for b in range(2)]
        ld_acp = sem("ld_acp")
        st_cls = sem("st_cls")
        ld_ain = sem("ld_ain")
        ld_aout = sem("ld_aout")
        ld_hcls = sem("ld_hcls")
        ld_gate = sem("ld_gate")
        ld_first = sem("ld_first")
        st_out = sem("st_out")
        const_ready = sem("const_ready")
        masks_ready = sem("masks_ready")
        c_stat = sem("c_stat")
        c_mv = sem("c_mv")
        c_ve = sem("c_ve")
        c_rstd = sem("c_rstd")
        c_norm = sem("c_norm")
        c_hi = sem("c_hi")
        c_split = sem("c_split")
        c_turned = sem("c_turned")
        c_kept = sem("c_kept")
        w_peak = sem("w_peak")
        w_peaks = sem("w_peaks")
        w_pow = sem("w_pow")
        w_split = sem("w_split")
        warmed = sem("warmed")
        toka_done = sem("toka_done")
        tokb_done = sem("tokb_done")
        ha_ready = sem("ha_ready")
        hb_ready = sem("hb_ready")
        stat_done = sem("stat_done")
        mv_ready = sem("mv_ready")
        ve_ready = sem("ve_ready")
        rstd_ready = sem("rstd_ready")
        x32_ready = sem("x32_ready")
        vhi_ready = sem("vhi_ready")
        vlo_ready = sem("vlo_ready")
        t_done = sem("t_done")
        xt_ready = sem("xt_ready")
        xtc_ready = sem("xtc_ready")
        qk_done = sem("qk_done")
        p_exp = sem("p_exp")
        p_lo = sem("p_lo")
        pv_done = sem("pv_done")
        rden_ready = sem("rden_ready")
        attn_added = sem("attn_added")
        hc_ready = sem("hc_ready")
        stat2_done = sem("stat2_done")
        mv2_ready = sem("mv2_ready")
        ve2_ready = sem("ve2_ready")
        rstd2_ready = sem("rstd2_ready")
        x2_ready = sem("x2_ready")
        v2hi_ready = sem("v2hi_ready")
        v2lo_ready = sem("v2lo_ready")
        h2b_ready = sem("h2b_ready")
        t2_done = sem("t2_done")
        xt2_ready = sem("xt2_ready")
        f1_done = sem("f1_done")
        gelu_done = sem("gelu_done")
        ghi_ready = sem("ghi_ready")
        glo_ready = sem("glo_ready")
        f2_done = sem("f2_done")
        y_ready = sem("y_ready")
        k_dve = sem("k_dve")
        k_ve = sem("k_ve")
        k_rstd = sem("k_rstd")
        k_rn = sem("k_rn")
        k_xcls = sem("k_xcls")
        k_turned = sem("k_turned")
        k_xct = sem("k_xct")
        k_hid = sem("k_hid")
        k_gelu = sem("k_gelu")
        k_cand = sem("k_cand")
        k_biased = sem("k_biased")
        k_back = sem("k_back")
        k_abs = sem("k_abs")
        k_tanh = sem("k_tanh")
        k_gates = sem("k_gates")
        k_out = sem("k_out")

        last_step = N_STEP + 2

        def schedule(eng, slot, step, slot_stages=None, step_stages=None):
            slot_stages, step_stages = slot_stages or {}, step_stages or {}

            def one_slot(i):
                slot(0, i)
                if i in slot_stages:
                    slot_stages[i]()

            def one_step(s):
                step(0, s)
                if s in step_stages:
                    step_stages[s]()

            for i in range(-2, 2):
                one_slot(i)
            with eng.Fori(0, (LOOPED - 2) // 4) as t:
                for c in range(2, 6):
                    slot(t, c)
            for i in range(LOOPED, NB - 3):
                one_slot(i)
            for s in range(-2, 1):
                one_step(s)
                one_slot(NB - 1 + s)
            for s in range(1, 8):
                one_step(s)
            with eng.Fori(0, (N_STEP - 10) // 2) as t:
                for c in range(8, 10):
                    step(t, c)
            for s in range(N_STEP - 2, last_step + 1):
                one_step(s)

        def early(s):
            return isinstance(s, int) and s < 3

        def tiles(s):
            if isinstance(s, int) and s >= N_STEP:
                return (4, PC) if s == N_STEP else (1, PCL)
            return 4, 128

        def sums(s, k):
            return ps_ct if isinstance(s, int) and s == N_STEP + 1 else ps_f2[k // 2]

        def rows(s, k):
            if isinstance(s, int) and s >= N_STEP:
                return hc[0:tiles(s)[1], 4 * (s - N_STEP) + k, :]
            return h[:, s * 4 + k, :]

        def rows_all(s):
            n, m = tiles(s)
            if isinstance(s, int) and s >= N_STEP:
                return hc[0:m, 4 * (s - N_STEP):4 * (s - N_STEP) + n, :]
            return h[:, bass.ds(s * 4, 4), :]

        def tiles_before(s):
            return s * 4 if not isinstance(s, int) or s <= N_STEP + 1 else 4 * (N_STEP + 1) + 1

        def pairs_before(s):
            return s * 2 if not isinstance(s, int) or s <= N_STEP + 1 else 2 * (N_STEP + 1) + 1

        block = ctx.enter_context(nc.Block())

        @block.sync
        def _(eng):
            half = KP // 2
            eng.dma_start(wtok_sb[:, 0:half, :], wtok[:, 0:half, :]).then_inc(ld_first, 16)
            eng.dma_start(x_sb[:, 0, 0:half], x[0, :, 0:half]).then_inc(ld_first, 16)
            eng.dma_start(wtok_sb[:, half:KP, :], wtok[:, half:KP, :]).then_inc(ld_w, 16)
            eng.dma_start(x_sb[:, 0, half:KP], x[0, :, half:KP]).then_inc(ld_x[0], 16)
            eng.dma_start(hc[:, :, :], txtc).then_inc(ld_txtc, 16)
            eng.dma_start(btok_sb[:, :], btok).then_inc(ld_w, 16)
            eng.dma_start(hs[MB:128, 0, 1, :], txtb[0]).then_inc(ld_txtb[0], 16)
            eng.dma_start(x_sb[:, 1], x[1]).then_inc(ld_x[1], 16)
            for n in range(1, 4):
                eng.dma_start(hs[MB:128, n, 1, :], txtb[n]).then_inc(ld_txtb[n], 16)
            eng.dma_start(x_sb[:, 2], x[2]).then_inc(ld_x[2], 16)
            eng.wait_ge(c_split, 2)
            eng.dma_start(split_c.rearrange("(c p) d -> p c d", p=PC), vcp[:, :, :]).then_inc(st_split, 16)
            eng.dma_start(x_sb[:, 3], x[3]).then_inc(ld_x[3], 16)
            eng.wait_ge(st_split, 16)
            for n in range(4):
                eng.dma_start(vc[:, n, :], split_c[n * MC:(n + 1) * MC, :]).then_inc(ld_vc[n], 16)
            eng.dma_start(w1st[:, :, :], fc1).then_inc(ld_ffn, 16)
            eng.dma_start(w2st[:, :, :], fc2).then_inc(ld_ffn, 16)
            eng.dma_start(b1_sb[:, :], b1).then_inc(ld_ffn, 16)
            eng.dma_start(b2_sb[:, :], b2).then_inc(ld_ffn, 16)

            def slot(t, c):
                i = t * 4 + c
                if valid(i, NB) and valid(i + 6, NB) or isinstance(i, int) and -2 <= i < 0:
                    eng.wait_ge(tokb_done, i + 3)
                    eng.dma_start(x_sb[:, (c + 2) % 4], x[i + 6]).then_inc(ld_x[(c + 2) % 4], 16)
                if valid(i, NB):
                    eng.wait_ge(attn_added, 3 * (i + 1))
                    eng.dma_start(attn_c[bass.ds(i * MC, MC), :], ac[:, c % 2, :]).then_inc(st_ac[c % 2], 16)
                    if after(i, 1):
                        eng.wait_ge(st_cls, 16 * i)
                    eng.dma_start(rows_cls[:, bass.ds(i, 1), :], h[0:NCLS, bass.ds(i * 2, 1), :]).then_inc(st_cls, 16)
                    if valid(i + 4, NB):
                        eng.dma_start(hs[MB:128, c % 4, 1, :], txtb[i + 4]).then_inc(ld_txtb[c % 4], 16)
                        eng.dma_start(vc[:, c % 4, :],
                                      split_c[bass.ds((i + 4) * MC, MC), :]).then_inc(ld_vc[c % 4], 16)

            def load_classes():
                eng.wait_ge(st_cls, 16 * NB)
                for j in range(2):
                    eng.dma_start(hcls[:, j, :],
                                  rows_cls[3 * j:3 * j + 3].rearrange("n b d -> (n b) d")).then_inc(ld_hcls, 16)
                eng.dma_start(gw_sb[:, :, :, :], gatew).then_inc(ld_gate, 16)
                eng.dma_start(gb_sb[:, :, :], gateb).then_inc(ld_gate, 16)
                for dst, src in ((ain1_sb[:, :, :], ain1), (ain2_sb[:, :, :], ain2), (abin_sb[:, :, :], abin)):
                    eng.dma_start(dst, src).then_inc(ld_ain, 16)
                for dst, src in ((aout_sb[:, :, :, :], aout), (about1_sb[:, :], about1), (about2_sb[:, :], about2)):
                    eng.dma_start(dst, src).then_inc(ld_aout, 16)
                for b in range(2):
                    eng.wait_ge(st_ac[b], 16 * NB // 2)
                eng.dma_start(acp[:, 0:NC - 1, :],
                              attn_c[0:(NC - 1) * PC, :].rearrange("(c p) d -> p c d", p=PC)).then_inc(ld_acp, 16)
                eng.dma_start(acp[0:PCL, NC - 1, :], attn_c[(NC - 1) * PC:NB * MC, :]).then_inc(ld_acp, 16)

            def step(t, c):
                s = t * 2 + c
                if valid(s - 1, last_step):
                    n, m = tiles(s - 1)
                    eng.wait_ge(y_ready, tiles_before(s - 1) + n)
                    if isinstance(s, int) and s - 1 >= N_STEP:
                        g = 4 * (s - 1 - N_STEP)
                        dst = out_c[0:m, g:g + n, :]
                    else:
                        dst = out_ab[s - 1]
                    eng.dma_start(dst, rows_all(s - 1)).then_inc(st_out, 16)

            def class_out():
                eng.wait_ge(k_out, 4)
                eng.dma_start(out_cls, hcls[:, :, :]).then_inc(st_out, 16)

            schedule(eng, slot, step, {NB - 1: load_classes}, {N_STEP - 1: class_out})
            eng.wait_ge(st_out, 16 * (last_step + 1))

        @block.tensor
        def _(eng):
            eng.wait_ge(masks_ready, 1)
            for _ in range(WARM_UP):
                warm = eng.transpose(ps_t[0][:, 0, :], ident[:, :], ident[:, :])
            warm.then_inc(warmed, 1)
            eng.wait_ge(warmed, 1)

            def tokens(t, c, half):
                n, b, m = t * 4 + c, c % 4, (128, MB)[half]
                if not valid(n, NB):
                    return
                if half == 0:
                    if isinstance(n, int) and n == 0:
                        eng.wait_ge(ld_first, 32)
                    else:
                        eng.wait_ge(ld_x[b], (t + (c // 4 + 1)) * 16)
                if after(n, 1):
                    eng.wait_ge((ha_ready, hb_ready)[half], n)
                for k in range(KP):
                    if isinstance(n, int) and n == 0 and half == 0 and k == KP // 2:
                        eng.wait_ge(ld_w, 32)
                        eng.wait_ge(ld_x[0], 16)
                    mm = eng.matmul(ps_tok[half][0:m, 0:D], x_sb[:, b, k, 128 * half:128 * half + m],
                                    wtok_sb[:, k, :], start=(k == 0), stop=(k == KP - 1))
                mm.then_inc((toka_done, tokb_done)[half], 1)

            def turn(t, c):
                n, b = t * 4 + c, c % 4
                if not valid(n, NB):
                    return
                eng.wait_ge(vhi_ready, 2 * (n + 1))
                eng.wait_ge(vlo_ready, 2 * (n + 1))
                if isinstance(n, int) and n == 0:
                    eng.wait_ge(c_kept, 1)
                if after(n, 1):
                    eng.wait_ge(xt_ready, 2 * n)
                for a in range(2):
                    for k, src in enumerate(split_columns(v[:, b, a, :])):
                        mm = eng.transpose(ps_t[a][:, k, :], src, ident[:, :])
                mm.then_inc(t_done, 1)

            def split_columns(r):
                return r[:, HI:HI + 128], r[:, LO1:LO1 + 128], r[:, HI2:HI2 + 128], r[:, HI + 128:HI2 + 64]

            def product(out, b, t0, t1, s0, s1):
                X = xt[:, b]
                eng.matmul(out, X[:, 0, t0:t1], X[:, 0, s0:s1], start=True, stop=False)
                eng.matmul(out, X[:, 0, t0:t1], X[:, 1, s0:s1], start=False, stop=False)
                eng.matmul(out, X[:, 1, t0:t1], X[:, 0, s0:s1], start=False, stop=False)
                eng.matmul(out, X[:, 3, t0:t1], X[:, 2, s0:s1], start=False, stop=False)
                eng.matmul(out, X[64:128, 2, t0:t1], X[64:128, 3, s0:s1], start=False, stop=False)

            def scores(t, c):
                n, b = t * 4 + c, c % 2
                if not valid(n, NB):
                    return
                eng.wait_ge(xt_ready, 2 * (n + 1))
                eng.wait_ge(xtc_ready, n + 1)
                if isinstance(n, int) and n == 0:
                    eng.wait_ge(masks_ready, 3)
                if after(n, 1):
                    eng.wait_ge(p_exp, 4 * n)
                for t0, t1, col, width in ((0, 128, 0, COLS_A), (128, 256, PCOL_B, COLS_B), (256, S, PCOL_C, MC)):
                    m = t1 - t0
                    product(ps_s[0:m, col:col + width], b, t0, t1, t0, S)
                    mm = eng.matmul(ps_s[0:m, col:col + m], ident[0:m, 0:m], never[0:m, 0:m],
                                    start=False, stop=True)
                mm.then_inc(qk_done, 1)

            def values(t, c):
                n, b, pb = t * 4 + c, c % 4, c % 2
                if not valid(n, NB):
                    return
                eng.wait_ge(p_exp, 4 * (n + 1))
                eng.wait_ge(p_lo, 2 * (n + 1))
                eng.wait_ge(ld_vc[b], (t + (c // 4 + 1)) * 16)
                if after(n, 1):
                    eng.wait_ge(attn_added, 3 * n)
                blocks = ((128, 0), (128, PCOL_B - 128), (MC, PCOL_C - 256))
                for q, (s0, s1, out) in enumerate(((0, 128, ps_o[:, 0:D + 1]), (128, 256, ps_o[:, D + 1:2 * D + 2]),
                                                   (256, S, ps_oc[0:MC, 0:D + 1]))):
                    for r in range(q + 1):
                        m, col = blocks[r]
                        row = vc[:, b, :] if r == 2 else v[:, b, r, :]
                        hi, lo = phi[0:m, pb, col + s0:col + s1], plo[0:m, pb, col + s0:col + s1]
                        eng.matmul(out, hi, row[:, ONE:HI2], start=(r == 0), stop=False)
                        eng.matmul(out, lo, row[:, ONE:HI2], start=False, stop=False)
                        eng.matmul(out[:, 129:D + 1], hi, row[:, LO2:LO1], start=False, stop=False)
                        mm = eng.matmul(out[:, 1:129], hi, row[:, LO1:VW], start=False, stop=(r == q))
                mm.then_inc(pv_done, 1)

            def turn_c():
                eng.wait_ge(masks_ready, 3)
                eng.wait_ge(c_split, 2)
                for g in range(NC):
                    for k, src in enumerate(split_columns(vcp[:, g, :])):
                        mm = eng.transpose(ps_tc[g][:, k, 0:PC], src, ident[0:PC, 0:PC])
                    mm.then_inc(c_turned, 1)

            def slot(t, c):
                tokens(t, c + 2, 0)
                if isinstance(t, int) and c == -1:
                    turn_c()
                tokens(t, c + 2, 1)
                turn(t, c + 1)
                values(t, c)
                scores(t, c + 1)

            def turn2(t, c):
                s, b = t * 2 + c, c % 2
                if not valid(s, last_step):
                    return
                n, m = tiles(s)
                eng.wait_ge(v2hi_ready, s + 1)
                eng.wait_ge(v2lo_ready, 2 * (s + 1))
                if isinstance(s, int) and s == 0:
                    eng.wait_ge(ha_ready, NB)
                    eng.wait_ge(hb_ready, NB)
                if after(s, 1):
                    eng.wait_ge(xt2_ready, pairs_before(s))
                for k in range(n):
                    for j, src in enumerate((v2[0:m, b, k, 0:128], v2[0:m, b, k, FLO1:FW], v2[0:m, b, k, 128:FLO1])):
                        mm = eng.transpose(ps_t2[k // 2][:, k % 2, j, 0:m], src, ident[0:m, 0:m])
                    if k % 2 or k == n - 1:
                        mm.then_inc(t2_done, 1)

            def fc1_products(t, c):
                s, b = t * 2 + c, c % 2
                if not valid(s, last_step):
                    return
                n, m = tiles(s)
                N = n * m
                eng.wait_ge(xt2_ready, pairs_before(s) + (n + 1) // 2)
                if isinstance(s, int) and s == 0:
                    eng.wait_ge(w_split, 4)
                    eng.wait_ge(xt_ready, 2 * NB)
                X = xt2[:, b]
                for q in range(KH):
                    if after(s, 1) or q >= 3:
                        eng.wait_ge(gelu_done, s * KH + (q - 2))
                    if isinstance(s, int) and s in (4, 5) and q < 3:
                        eng.wait_ge(k_gelu, 3 * ((4, 5, 6) if s == 4 else (10, 8, 9))[q])
                    out = ps_f1[q % 3][:, 0:N]
                    w = slice(128 * q, 128 * q + 128)
                    eng.matmul(out, w1hi[:, 0, w], X[:, 0, 0:N], start=True, stop=False)
                    eng.matmul(out, w1hi[:, 0, w], X[:, 1, 0:N], start=False, stop=False)
                    eng.matmul(out, w1lo[:, 0, w], X[:, 0, 0:N], start=False, stop=False)
                    eng.matmul(out, w1hi[:, 1, w], X[:, 2, 0:N], start=False, stop=False)
                    eng.matmul(out, w1lo[0:64, 1, w], X[0:64, 2, 0:N],
                               start=False, stop=True).then_inc(f1_done, 1)

            def fc2_products(t, c):
                s, b = t * 2 + c, c % 2
                if not valid(s, last_step):
                    return
                n, m = tiles(s)
                eng.wait_ge(ghi_ready, KH * (s + 1))
                eng.wait_ge(glo_ready, KH * (s + 1))
                if isinstance(s, int) and s == 0:
                    eng.wait_ge(attn_added, 3 * NB)
                if after(s, 1) and not (isinstance(s, int) and s == N_STEP + 1):
                    eng.wait_ge(y_ready, tiles_before(s))
                for k in range(n):
                    out = sums(s, k)[0:m, D * (k % 2):D * (k % 2) + D]
                    for q in range(KH):
                        hi, lo = ghi[:, b, q, m * k:m * k + m], glo[:, b, q, m * k:m * k + m]
                        eng.matmul(out, hi, w2hi[:, q, :], start=(q == 0), stop=False)
                        eng.matmul(out, hi, w2lo[:, q, :], start=False, stop=False)
                        mm = eng.matmul(out, lo, w2hi[:, q, :], start=False, stop=(q == KH - 1))
                    if k % 2 or k == n - 1:
                        mm.then_inc(f2_done, 1)

            def step(t, c):
                turn2(t, c + 1)
                fc1_products(t, c)
                fc2_products(t, c - 1)

            def turn_classes():
                eng.wait_ge(k_xcls, 2)
                for j in range(2):
                    w = slice(96 * j, 96 * j + 96)
                    eng.transpose(ps_ct[:, w], xcls[:, j, 0:128], ident32[0:96, 0:96])
                    mm = eng.transpose(ps_ct[0:64, 192 + 96 * j:288 + 96 * j], xcls[:, j, 128:D],
                                       ident32[0:96, 0:96])
                mm.then_inc(k_turned, 1)

            def class_hidden(first, last):
                if first == 0:
                    eng.wait_ge(k_xct, 2)
                    eng.wait_ge(ld_ain, 16 * 3)
                eng.wait_ge(gelu_done, (4 if first == 0 else 5) * KH)
                for a in range(first, last):
                    n0, dn, n, _ = atom_tokens(a)
                    for q in range(KH):
                        u = 2 * a + q // 3
                        if q % 3 == 0 and u >= 3:
                            eng.wait_ge(k_gelu, 3 * (u - 2))
                        out = ps_f1[u % 3][:, 96 * (q % 3):96 * (q % 3) + NB * n]
                        w = slice(128 * q, 128 * q + 128)
                        eng.matmul(out, ain1_sb[:, a, w], xct1[:, n0:n0 + dn * (n - 1) + 1:dn, :],
                                   start=True, stop=False)
                        mm = eng.matmul(out, ain2_sb[:, a, w], xct2[:, n0:n0 + dn * (n - 1) + 1:dn, :],
                                        start=False, stop=True)
                        if q % 3 == 2:
                            mm.then_inc(k_hid, 1)

            def class_outputs(half):
                if half == 0:
                    eng.wait_ge(k_gelu, NATOM * KH)
                    eng.wait_ge(ld_aout, 16 * 3)
                else:
                    eng.wait_ge(k_biased, NATOM)
                m, d0 = ((64, 128), (128, 0))[half]
                out = ps_ct[0:m, 0:384].rearrange("p (r n b) -> p r n b", r=2, n=NCLS)
                for a in range(NATOM):
                    n0, dn, n, r = atom_tokens(a)
                    for q in range(KH):
                        mm = eng.matmul(out[:, 1 - r, n0:n0 + dn * (n - 1) + 1:dn, :],
                                        aout_sb[:, a, q, d0:d0 + m],
                                        gt[:, q, 1 - r, n0:n0 + dn * (n - 1) + 1:dn, :],
                                        start=(q == 0), stop=(q == KH - 1))
                    mm.then_inc(k_cand, 1)

            def class_back(j):
                if j:
                    eng.wait_ge(k_out, 2)
                else:
                    eng.wait_ge(k_biased, 2 * NATOM)
                for r in range(2):
                    out = ps_ct[0:96, D * r:D * r + D]
                    eng.transpose(out[:, 0:128], cand1[:, r, 3 * j:3 * j + 3, :], ident32[:, :])
                    mm = eng.transpose(out[:, 128:D], cand2[:, r, 3 * j:3 * j + 3, :], ident32[0:64, 0:64])
                mm.then_inc(k_back, 1)

            schedule(eng, slot, step, None,
                     {2: turn_classes, 3: lambda: class_hidden(0, 3), 4: lambda: class_hidden(3, NATOM),
                      5: lambda: class_outputs(0), 6: lambda: class_outputs(1), 7: lambda: class_back(0),
                      N_STEP - 2: lambda: class_back(1),
                      N_STEP: lambda: eng.wait_ge(k_out, 4)})

        @block.scalar
        def _(eng):
            eng.wait_ge(c_norm, NC)
            eng.copy(vcp[:, :, HI:HI2], xc32[:, :, :]).then_inc(c_hi, 1)
            eng.copy(vcp[:, :, HI2:LO2], xc32[:, :, 128:D]).then_inc(c_hi, 1)

            def keep_columns_b(t, c):
                n, b = t * 4 + c, c % 2
                if not valid(n, NB):
                    return
                eng.wait_ge(t_done, n + 1)
                if after(n, 2):
                    eng.wait_ge(qk_done, n - 1)
                eng.copy(xt[:, b, :, 128:256], ps_t[1][:, :, :]).then_inc(xt_ready, 1)

            def exponents(t, c):
                n, b = t * 4 + c, c % 2
                if valid(n, NB):
                    eng.wait_ge(qk_done, n + 1)
                    if after(n, 2):
                        eng.wait_ge(p_lo, 2 * (n - 1))
                        eng.wait_ge(pv_done, n - 1)
                    for dst in (p32, phi):
                        for m, c0, c1 in ((128, 0, PCOL_C), (MC, PCOL_C, PCOLS)):
                            eng.activation(dst[0:m, b, c0:c1], ps_s[0:m, c0:c1], ACT.Exp, bias=shift[0:m, 0:1],
                                           scale=SCALE).then_inc(p_exp, 1)

            def high_parts(t, c):
                n, b = t * 4 + c, c % 4
                if valid(n, NB):
                    eng.wait_ge(x32_ready, 2 * (n + 1))
                    if after(n, 4):
                        eng.wait_ge(pv_done, n - 3)
                    eng.copy(v[:, b, :, HI:HI2], x32[:, c % 2, :, :]).then_inc(vhi_ready, 1)
                    eng.copy(v[:, b, :, HI2:LO2], x32[:, c % 2, :, 128:D]).then_inc(vhi_ready, 1)

            def slot(t, c):
                keep_columns_b(t, c + 1)
                high_parts(t, c + 2)
                exponents(t, c + 1)

            def high_weights():
                eng.wait_ge(w_pow, 6)
                eng.activation(w1hi[:, :, :], w1st[:, :, :], ACT.Copy, scale=up[:, 0:1]).then_inc(w_split, 1)
                eng.activation(w2hi[:, :, :], w2st[:, :, :], ACT.Copy, scale=up[:, 2:3]).then_inc(w_split, 1)

            def high_rows(n, b):
                k, m = tiles(n)
                eng.wait_ge(x2_ready, tiles_before(n) + k)
                if after(n, 2):
                    eng.wait_ge(t2_done, pairs_before(n - 1))
                eng.copy(v2[0:m, b, 0:k, 0:D], x2[0:m, b, 0:k, :]).then_inc(v2hi_ready, 1)

            def gelu(t, c, q):
                s = t * 2 + c
                N = tiles(s)[0] * tiles(s)[1]
                eng.wait_ge(f1_done, s * KH + (q + 1))
                if after(s, 1) or q >= 3:
                    eng.wait_ge(glo_ready, s * KH + (q - 2))
                eng.activation(g32[:, q % 3, 0:N], ps_f1[q % 3][:, 0:N], ACT.Gelu, bias=b1_sb[:, q:q + 1],
                               scale=down[:, 0:1]).then_inc(gelu_done, 1)

            def gelu_hi(t, c, q):
                s = t * 2 + c
                N = tiles(s)[0] * tiles(s)[1]
                eng.wait_ge(gelu_done, s * KH + (q + 1))
                if q == 0 and after(s, 2):
                    eng.wait_ge(f2_done, pairs_before(s - 1))
                eng.activation(ghi[:, c % 2, q, 0:N], g32[:, q % 3, 0:N], ACT.Copy,
                               scale=up[:, 3:4]).then_inc(ghi_ready, 1)

            def step(t, c):
                s = t * 2 + c
                if valid(s, last_step):
                    for q in range(KH + 1):
                        if q < KH:
                            gelu(t, c, q)
                        if q:
                            gelu_hi(t, c, q - 1)
                n = t * 2 + (c + 2)
                if valid(n, last_step) and not early(n):
                    high_rows(n, c % 2)

            def class_hidden(first, last):
                eng.wait_ge(ld_ain, 16 * 3)
                for a in range(first, last):
                    n0, dn, n, r = atom_tokens(a)
                    for q in range(KH):
                        u = 2 * a + q // 3
                        eng.wait_ge(k_hid, u + 1)
                        src = ps_f1[u % 3][:, 96 * (q % 3):96 * (q % 3) + NB * n]
                        eng.activation(gt[:, q, r, n0:n0 + dn * (n - 1) + 1:dn, :],
                                       src.rearrange("p (n b) -> p n b", b=NB), ACT.Gelu,
                                       bias=abin_sb[:, a, q:q + 1]).then_inc(k_gelu, 1)

            def class_outputs(half):
                eng.wait_ge(ld_aout, 16 * 3)
                m, dst, bias = ((64, cand2, about2_sb), (128, cand1, about1_sb))[half]
                src = ps_ct[0:m, 0:384].rearrange("p (r n b) -> p r n b", r=2, n=NCLS)
                for a in range(NATOM):
                    n0, dn, n, r = atom_tokens(a)
                    eng.wait_ge(k_cand, NATOM * (half + 1))
                    eng.activation(dst[:, 1 - r, n0:n0 + dn * (n - 1) + 1:dn, :],
                                   src[:, 1 - r, n0:n0 + dn * (n - 1) + 1:dn, :], ACT.Identity,
                                   bias=bias[:, a:a + 1]).then_inc(k_biased, 1)
                if half == 0:
                    eng.wait_ge(k_abs, 2)
                    eng.activation(lg[:, :, 3], lg[:, :, 2], ACT.Tanh, scale=0.5).then_inc(k_tanh, 1)

            schedule(eng, slot, step,
                     {1: high_weights, LN_SLOT + 1: lambda: high_rows(0, 0), LN_SLOT + 3: lambda: high_rows(1, 1),
                      LN_SLOT + 6: lambda: high_rows(2, 0)},
                     {3: lambda: class_hidden(0, 3), 4: lambda: class_hidden(3, NATOM),
                      5: lambda: class_outputs(0), 6: lambda: class_outputs(1)})

        @block.gpsimd
        def _(eng):
            eng.memset(half_neg[:, :], -0.5).then_inc(const_ready, 1)
            eng.memset(eps[:, :], EPS).then_inc(const_ready, 1)
            eng.memset(shift[:, :], SHIFT).then_inc(const_ready, 1)
            eng.memset(ident[:, :], 0.0).then_inc(const_ready, 1)
            eng.memset(ident32[:, :], 0.0).then_inc(const_ready, 1)
            eng.memset(never[:, :], 0.0).then_inc(const_ready, 1)
            eng.memset(v[:, :, :, ONE:HI], 1.0).then_inc(const_ready, 1)
            eng.memset(v[:, :, :, 0:ONE], 0.0).then_inc(const_ready, 1)
            eng.memset(vcp[:, :, ONE:HI], 1.0).then_inc(const_ready, 1)
            eng.memset(vcp[:, :, 0:ONE], 0.0).then_inc(const_ready, 1)
            eng.wait_ge(const_ready, 10)
            eng.affine_select(out=ident[:, :], in_=ident[:, :], compare_op=ALU.not_equal, fill=1.0,
                              base=0, pattern=[[-1, 128]], channel_multiplier=1).then_inc(masks_ready, 1)
            eng.affine_select(out=ident32[:, :], in_=ident32[:, :], compare_op=ALU.not_equal, fill=1.0,
                              base=0, pattern=[[-1, 128]], channel_multiplier=1).then_inc(masks_ready, 1)
            eng.affine_select(out=never[:, :], in_=never[:, :], compare_op=ALU.is_ge, fill=MASKED,
                              base=0, pattern=[[1, 128]], channel_multiplier=-1).then_inc(masks_ready, 1)

            eng.wait_ge(c_mv, NC)
            eng.tensor_tensor(vec[:, :], mvc[:, :, 1], eps[0:PC, 0:NC], ALU.add).then_inc(c_ve, 1)
            eng.wait_ge(c_ve, 1)
            eng.tensor_tensor(rstdc[:, :], vec[:, :], half_neg[0:PC, 0:NC], ALU.pow).then_inc(c_rstd, 1)

            def slot(t, c):
                n, b = t * 4 + (c + 1), (c + 1) % 2
                if valid(n, NB):
                    if isinstance(n, int) and n == 0:
                        eng.wait_ge(c_kept, NC)
                    if after(n, 2):
                        eng.wait_ge(qk_done, n - 1)
                    eng.tensor_copy(xt[:, b, :, 256:S], ct[:, :, bass.ds(n * MC, MC)]).then_inc(xtc_ready, 1)
                n, b = t * 4 + (c + 2), (c + 2) % 4
                if valid(n, NB):
                    eng.wait_ge(mv_ready, 2 * (n + 1))
                    eng.tensor_tensor(ve[:, :], mv[:, :, 1], eps[:, 0:2], ALU.add).then_inc(ve_ready, 1)
                    eng.wait_ge(ve_ready, n + 1)
                    eng.tensor_tensor(rstd[:, :], ve[:, :], half_neg[:, 0:2], ALU.pow).then_inc(rstd_ready, 1)
                    eng.wait_ge(vhi_ready, 2 * (n + 1))
                    eng.tensor_tensor(v[:, b, :, LO1:VW], x32[:, c % 2, :, 0:128], v[:, b, :, HI:HI + 128],
                                      ALU.subtract).then_inc(vlo_ready, 1)
                    eng.tensor_tensor(v[:, b, :, LO2:LO1], x32[:, c % 2, :, 128:D], v[:, b, :, HI2:LO2],
                                      ALU.subtract).then_inc(vlo_ready, 1)

            def weight_peaks():
                eng.wait_ge(w_peak, 3)
                eng.partition_all_reduce(peaks[:, 0:3], peak[:, :], 128, ABSMAX).then_inc(w_peaks, 1)

            def scale_rows(n):
                k, m = tiles(n)
                eng.wait_ge(mv2_ready, tiles_before(n) + k)
                eng.tensor_tensor(ve2[0:m, 0:k], mv2[0:m, 0:k, 1], eps[0:m, 0:k], ALU.add).then_inc(ve2_ready, 1)
                eng.wait_ge(ve2_ready, n + 1)
                eng.tensor_tensor(rstd2[0:m, 0:k], ve2[0:m, 0:k], half_neg[0:m, 0:k], ALU.pow).then_inc(rstd2_ready, 1)

            def low_rows(n, b):
                k, m = tiles(n)
                eng.wait_ge(v2hi_ready, n + 1)
                eng.tensor_tensor(v2[0:m, b, 0:k, FLO1:FW], x2[0:m, b, 0:k, 0:128], v2[0:m, b, 0:k, 0:128],
                                  ALU.subtract).then_inc(v2lo_ready, 1)
                eng.tensor_tensor(v2[0:m, b, 0:k, FLO2:FLO1], x2[0:m, b, 0:k, 128:D], v2[0:m, b, 0:k, 128:D],
                                  ALU.subtract).then_inc(v2lo_ready, 1)

            def bias_rows(n):
                k, m = tiles(n)
                if isinstance(n, int) and n <= 3:
                    eng.wait_ge(st_cls, 16 * (2 * n + 2 if early(n) else NB))
                r = rows_all(n)
                eng.tensor_tensor(r, r, b2_sb[0:m, :].unsqueeze(1).to_broadcast([m, k, D]),
                                  ALU.add).then_inc(h2b_ready, 1)

            def step(t, c):
                n = t * 2 + (c + 2)
                if valid(n, last_step) and not early(n):
                    scale_rows(n)
                    low_rows(n, c % 2)
                    bias_rows(n)

            def scale_and_bias(n):
                scale_rows(n)
                if n:
                    bias_rows(n - 1)

            def last_low_rows():
                low_rows(2, 0)
                bias_rows(2)

            def class_scale():
                eng.wait_ge(k_dve, 4)
                eng.tensor_tensor(lg[:, :, 0], mvk[:, :, 1], eps[0:96, 0:2], ALU.add).then_inc(k_ve, 1)
                eng.wait_ge(k_ve, 1)
                eng.tensor_tensor(lg[:, :, 1], lg[:, :, 0], half_neg[0:96, 0:2], ALU.pow).then_inc(k_rstd, 1)

            def class_norms():
                eng.wait_ge(k_gates, 1)
                eng.tensor_tensor(rn[:, :, :], sq[:, :, :],
                                  half_neg[0:96, 0:6].rearrange("p (a b) -> p a b", a=2), ALU.pow).then_inc(k_rn, 1)

            schedule(eng, slot, step,
                     {0: weight_peaks,
                      LN_SLOT: lambda: scale_and_bias(0), LN_SLOT + 1: lambda: low_rows(0, 0),
                      LN_SLOT + 2: lambda: scale_and_bias(1), LN_SLOT + 3: lambda: low_rows(1, 1),
                      LN_SLOT + 4: lambda: scale_and_bias(2), LN_SLOT + 6: last_low_rows},
                     {1: class_scale, 3: class_norms})

        @block.vector
        def _(eng):
            eng.wait_ge(ld_txtc, 16)
            for g in range(NC):
                eng.bn_stats(stc[:, g, :], hc[:, g, :]).then_inc(c_stat, 1)
            for g in range(NC):
                eng.wait_ge(c_stat, g + 1)
                eng.bn_aggr(mvc[:, g, :], stc[:, g, :]).then_inc(c_mv, 1)
            eng.wait_ge(c_rstd, 1)
            for g in range(NC):
                eng.tensor_scalar(xc32[:, g, :], hc[:, g, :], mvc[:, g, 0:1], rstdc[:, g:g + 1],
                                  ALU.subtract, ALU.mult).then_inc(c_norm, 1)

            def split_rows_c():
                eng.wait_ge(c_hi, 2)
                eng.tensor_tensor(vcp[:, :, LO1:VW], xc32[:, :, 0:128], vcp[:, :, HI:HI + 128],
                                  ALU.subtract).then_inc(c_split, 1)
                eng.tensor_tensor(vcp[:, :, LO2:LO1], xc32[:, :, 128:D], vcp[:, :, HI2:LO2],
                                  ALU.subtract).then_inc(c_split, 1)

            def keep_c():
                for g in range(NC):
                    eng.wait_ge(c_turned, g + 1)
                    eng.tensor_copy(ct[:, :, PC * g:PC * g + PC], ps_tc[g][:, :, 0:PC]).then_inc(c_kept, 1)

            def low_probs(t, c):
                n, b = t * 4 + c, c % 2
                if not valid(n, NB):
                    return
                eng.wait_ge(p_exp, 4 * (n + 1))
                if after(n, 2):
                    eng.wait_ge(pv_done, n - 1)
                for m, c0, c1 in ((128, 0, PCOL_C), (MC, PCOL_C, PCOLS)):
                    eng.tensor_tensor(plo[0:m, b, c0:c1], p32[0:m, b, c0:c1], phi[0:m, b, c0:c1],
                                      ALU.subtract).then_inc(p_lo, 1)

            def add_bias(t, c, half):
                n, b, m = t * 4 + c, c % 4, (128, MB)[half]
                if not valid(n, NB):
                    return
                done, ready = ((toka_done, ha_ready), (tokb_done, hb_ready))[half]
                eng.wait_ge(done, n + 1)
                eng.tensor_tensor(hs[0:m, b, half, :], ps_tok[half][0:m, 0:D], btok_sb[0:m, :],
                                  ALU.add).then_inc(ready, 1)

            def statistics1(t, c, half):
                n, b = t * 4 + c, c % 4
                if not valid(n, NB):
                    return
                if half:
                    eng.wait_ge(ld_txtb[b], (t + (c // 4 + 1)) * 16)
                eng.wait_ge((ha_ready, hb_ready)[half], n + 1)
                eng.bn_stats(st[:, half, :], hs[:, b, half, :]).then_inc(stat_done, 1)

            def aggregate(t, c, half):
                if valid(t * 4 + c, NB):
                    eng.bn_aggr(mv[:, half, :], st[:, half, :]).then_inc(mv_ready, 1)

            def statistics_there(t, c, half):
                n = t * 4 + c
                if valid(n, NB):
                    eng.wait_ge(stat_done, n * 2 + (half + 1))

            def keep_columns(t, c):
                n, b = t * 4 + c, c % 2
                if not valid(n, NB):
                    return
                eng.wait_ge(t_done, n + 1)
                if after(n, 2):
                    eng.wait_ge(qk_done, n - 1)
                eng.tensor_copy(xt[:, b, :, 0:128], ps_t[0][:, :, :]).then_inc(xt_ready, 1)

            def normalise(t, c):
                n, b = t * 4 + c, c % 2
                if not valid(n, NB):
                    return
                eng.wait_ge(mv_ready, 2 * (n + 1))
                eng.wait_ge(rstd_ready, n + 1)
                if after(n, 2):
                    eng.wait_ge(vlo_ready, 2 * (n - 1))
                for a in range(2):
                    eng.tensor_scalar(x32[:, b, a, :], hs[:, c % 4, a, :], mv[:, a, 0:1], rstd[:, a:a + 1],
                                      ALU.subtract, ALU.mult).then_inc(x32_ready, 1)

            def denominators(t, c):
                n = t * 4 + c
                if not valid(n, NB):
                    return
                eng.wait_ge(pv_done, n + 1)
                eng.reciprocal(rden[:, 0:2], ps_o[:, 0:D + 2:D + 1]).then_inc(rden_ready, 1)
                eng.reciprocal(rden[0:MC, 2:3], ps_oc[0:MC, 0:1]).then_inc(rden_ready, 1)

            def add_attention(t, c):
                n, b = t * 4 + c, c % 2
                if not valid(n, NB):
                    return
                eng.wait_ge(rden_ready, 2 * (n + 1))
                for a in range(2):
                    eng.scalar_tensor_tensor(h[:, n * 2 + a, :], ps_o[:, (D + 1) * a + 1:(D + 1) * (a + 1)],
                                             rden[:, a:a + 1], hs[:, c % 4, a, :],
                                             ALU.mult, ALU.add).then_inc(attn_added, 1)
                if after(n, 2):
                    eng.wait_ge(st_ac[b], (t * 2 + c // 2) * 16)
                eng.tensor_scalar(ac[:, b, :], ps_oc[0:MC, 1:D + 1], rden[0:MC, 2:3], None,
                                  ALU.mult).then_inc(attn_added, 1)

            def slot(t, c):
                if not (isinstance(t, int) and c == NB - 1):
                    low_probs(t, c)
                add_bias(t, c + 2, 0)
                statistics1(t, c + 2, 0)
                if isinstance(t, int) and c == -1:
                    keep_c()
                statistics_there(t, c + 2, 0)
                add_bias(t, c + 2, 1)
                aggregate(t, c + 2, 0)
                statistics1(t, c + 2, 1)
                statistics_there(t, c + 2, 1)
                keep_columns(t, c + 1)
                aggregate(t, c + 2, 1)
                if isinstance(t, int) and c == -2:
                    split_rows_c()
                denominators(t, c)
                normalise(t, c + 2)
                add_attention(t, c)
                if isinstance(t, int) and c == NB - 2:
                    low_probs(t, c + 1)

            def weight_maxima():
                eng.wait_ge(ld_ffn, 64)
                eng.tensor_reduce(peak[:, 0:1], w1st[:, :, :], AX.XY, ALU.max, apply_absolute_value=True).then_inc(w_peak, 1)
                eng.tensor_reduce(peak[:, 1:2], b1_sb[:, :], AX.X, ALU.max, apply_absolute_value=True).then_inc(w_peak, 1)
                eng.tensor_reduce(peak[:, 2:3], w2st[:, :, :], AX.XY, ALU.max, apply_absolute_value=True).then_inc(w_peak, 1)

            def weight_scales():
                eng.wait_ge(w_peaks, 1)
                eng.scalar_tensor_tensor(peaks[:, 3:4], peaks[:, 0:1], float(D), peaks[:, 1:2],
                                         ALU.mult, ALU.add).then_inc(w_pow, 1)
                eng.wait_ge(w_pow, 1)
                eng.tensor_scalar(peaks[:, :], peaks[:, :], 2.0 ** -60, None, ALU.max).then_inc(w_pow, 1)
                eng.wait_ge(w_pow, 2)
                eng.tensor_scalar(pow2[:, :].bitcast(U32), peaks[:, :].bitcast(U32), 0x7F800000, None,
                                  ALU.bitwise_and).then_inc(w_pow, 1)
                eng.wait_ge(w_pow, 3)
                eng.tensor_scalar(down[:, :], pow2[:, :], 1 / TOP, None, ALU.mult).then_inc(w_pow, 1)
                eng.wait_ge(w_pow, 4)
                eng.reciprocal(up[:, :], down[:, :]).then_inc(w_pow, 1)
                eng.wait_ge(w_pow, 5)
                eng.tensor_tensor(down[:, 1:2], down[:, 2:3], down[:, 3:4], ALU.mult).then_inc(w_pow, 1)

            def low_weights(n):
                src, hi, lo, k = ((w1st, w1hi, w1lo, 0), (w2st, w2hi, w2lo, 2))[n]
                eng.wait_ge(w_split, 2)
                eng.scalar_tensor_tensor(lo[:, :, :], src[:, :, :], up[:, k:k + 1], hi[:, :, :],
                                         ALU.mult, ALU.subtract).then_inc(w_split, 1)

            def statistics(s):
                n, m = tiles(s)
                if isinstance(s, int) and s == N_STEP:
                    eng.wait_ge(ld_acp, 32)
                    eng.tensor_tensor(hc[:, 0:NC - 1, :], hc[:, 0:NC - 1, :], acp[:, 0:NC - 1, :],
                                      ALU.add).then_inc(hc_ready, 1)
                    eng.tensor_tensor(hc[0:PCL, NC - 1, :], hc[0:PCL, NC - 1, :], acp[0:PCL, NC - 1, :],
                                      ALU.add).then_inc(hc_ready, 1)
                    eng.wait_ge(hc_ready, 2)
                if isinstance(s, int) and s <= 3:
                    eng.wait_ge(attn_added, 3 * (LN_SLOT + 2 * s + 1 if early(s) else NB))
                for k in range(n):
                    eng.bn_stats(st2[0:m, k, :], rows(s, k)).then_inc(stat2_done, 1)
                eng.wait_ge(stat2_done, tiles_before(s) + n)

            def aggregate2(s):
                n, m = tiles(s)
                for k in range(n):
                    eng.bn_aggr(mv2[0:m, k, :], st2[0:m, k, :]).then_inc(mv2_ready, 1)

            def normalise2(s, b):
                n, m = tiles(s)
                eng.wait_ge(mv2_ready, tiles_before(s) + n)
                eng.wait_ge(rstd2_ready, s + 1)
                if after(s, 2):
                    eng.wait_ge(v2lo_ready, 2 * (s - 1))
                for k in range(n):
                    eng.tensor_scalar(x2[0:m, b, k, :], rows(s, k), mv2[0:m, k, 0:1], rstd2[0:m, k:k + 1],
                                      ALU.subtract, ALU.mult).then_inc(x2_ready, 1)

            def keep_columns2(t, c):
                s, b = t * 2 + c, c % 2
                if not valid(s, last_step):
                    return
                n, m = tiles(s)
                if after(s, 2):
                    eng.wait_ge(f1_done, (s - 1) * KH)
                for j in range((n + 1) // 2):
                    w = min(2, n - 2 * j)
                    eng.wait_ge(t2_done, pairs_before(s) + (j + 1))
                    eng.tensor_copy(xt2[:, b, :, 2 * m * j:2 * m * j + w * m].rearrange("p k (a n) -> p a k n", a=w),
                                    ps_t2[j][:, 0:w, :, 0:m]).then_inc(xt2_ready, 1)

            def low_gelu(t, c, q):
                s = t * 2 + c
                if not valid(s, last_step):
                    return
                N = tiles(s)[0] * tiles(s)[1]
                eng.wait_ge(ghi_ready, s * KH + (q + 1))
                if q == 0 and after(s, 2):
                    eng.wait_ge(f2_done, pairs_before(s - 1))
                eng.scalar_tensor_tensor(glo[:, c % 2, q, 0:N], g32[:, q % 3, 0:N], up[:, 3:4],
                                         ghi[:, c % 2, q, 0:N], ALU.mult, ALU.subtract).then_inc(glo_ready, 1)

            def outputs(t, c):
                s = t * 2 + c
                if not valid(s, last_step):
                    return
                n, m = tiles(s)
                eng.wait_ge(h2b_ready, s + 1)
                for k in range(n):
                    if k % 2 == 0:
                        eng.wait_ge(f2_done, pairs_before(s) + (k // 2 + 1))
                    eng.scalar_tensor_tensor(rows(s, k), sums(s, k)[0:m, D * (k % 2):D * (k % 2) + D],
                                             down[0:m, 1:2], rows(s, k), ALU.mult, ALU.add).then_inc(y_ready, 1)

            def step(t, c):
                n = t * 2 + (c + 2)
                coming = valid(n, last_step) and not early(n)
                if coming:
                    statistics(n)
                keep_columns2(t, c + 1)
                if coming:
                    aggregate2(n)
                for q in range(3):
                    low_gelu(t, c, q)
                if coming:
                    normalise2(n, c % 2)
                for q in range(3, KH):
                    low_gelu(t, c, q)
                outputs(t, c - 1)

            def class_rows():
                eng.wait_ge(ld_hcls, 16 * 2)
                for j in range(2):
                    eng.bn_stats(stk[:, j, :], hcls[:, j, :]).then_inc(k_dve, 1)
                eng.wait_ge(k_dve, 2)
                for j in range(2):
                    eng.bn_aggr(mvk[:, j, :], stk[:, j, :]).then_inc(k_dve, 1)
                eng.wait_ge(k_dve, 4)
                eng.wait_ge(k_rstd, 1)
                for j in range(2):
                    eng.tensor_scalar(xcls[:, j, :], hcls[:, j, :], mvk[:, j, 0:1], lg[:, j, 1:2],
                                      ALU.subtract, ALU.mult).then_inc(k_xcls, 1)

            def class_columns():
                eng.wait_ge(k_turned, 1)
                eng.tensor_copy(xct1[:, :, :], ps_ct[:, 0:192].rearrange("p (n b) -> p n b", b=NB)).then_inc(k_xct, 1)
                eng.tensor_copy(xct2[:, :, :],
                                ps_ct[0:64, 192:384].rearrange("p (n b) -> p n b", b=NB)).then_inc(k_xct, 1)

            def class_dots(j):
                eng.wait_ge(k_xcls, 2)
                eng.wait_ge(ld_gate, 16 * 2)
                w0, w1, xr = gw_sb[:, j, 0, :], gw_sb[:, j, 1, :], xcls[:, j, :]
                for k, (a, b) in enumerate(((xr, w0), (xr, w1), (xr, xr), (w0, w0), (w1, w1))):
                    eng.wait_ge(k_dve, 4 + 5 * j + k)
                    eng.tensor_tensor_reduce(scr[:, :], a, b, 1.0, 0.0, ALU.mult, ALU.add,
                                             dots[:, j, k:k + 1]).then_inc(k_dve, 1)

            def class_squares():
                class_dots(1)
                eng.wait_ge(k_dve, 14)
                eng.tensor_scalar(sq[:, :, :], dots[:, :, 2:5], 1e-24, None, ALU.max).then_inc(k_gates, 1)

            def class_gates():
                eng.wait_ge(k_rn, 1)
                eng.tensor_tensor(dots[:, :, 0:2], dots[:, :, 0:2], rn[:, :, 1:3], ALU.mult).then_inc(k_dve, 1)
                eng.wait_ge(k_dve, 15)
                eng.tensor_tensor(lg[:, :, 4], dots[:, :, 1], dots[:, :, 0], ALU.subtract).then_inc(k_dve, 1)
                eng.wait_ge(k_dve, 16)
                eng.tensor_tensor(lg[:, :, 4], lg[:, :, 4], rn[:, :, 0], ALU.mult).then_inc(k_dve, 1)
                eng.wait_ge(k_dve, 17)
                eng.tensor_tensor(lg[:, :, 5], gb_sb[:, :, 1], gb_sb[:, :, 0], ALU.subtract).then_inc(k_dve, 1)
                eng.wait_ge(k_dve, 18)
                eng.tensor_tensor(lg[:, :, 6], lg[:, :, 4], lg[:, :, 5], ALU.add).then_inc(k_dve, 1)
                eng.wait_ge(k_dve, 19)
                eng.scalar_tensor_tensor(lg[:, :, 2], lg[:, :, 6], -1.0, lg[:, :, 6], ALU.mult, ALU.max).then_inc(k_abs, 1)
                eng.tensor_scalar(lg[:, :, 7], lg[:, :, 6], 0.0, None, ALU.is_gt).then_inc(k_abs, 1)

            def class_weights():
                eng.wait_ge(k_abs, 2)
                eng.wait_ge(k_tanh, 1)
                eng.tensor_scalar(lg[:, :, 4], lg[:, :, 3], 0.5, 0.5, ALU.mult, ALU.add).then_inc(k_dve, 1)
                eng.wait_ge(k_dve, 20)
                eng.tensor_tensor(lg[:, :, 5], lg[:, :, 4], lg[:, :, 7], ALU.mult).then_inc(k_dve, 1)
                eng.wait_ge(k_dve, 21)
                eng.tensor_tensor(lg[:, :, 6], lg[:, :, 4], lg[:, :, 5], ALU.subtract).then_inc(k_dve, 1)
                eng.wait_ge(k_dve, 22)
                class_sum(0)

            def class_sum(j):
                eng.wait_ge(k_back, j + 1)
                for r in range(2):
                    if r:
                        eng.wait_ge(k_out, 2 * j + 1)
                    eng.scalar_tensor_tensor(hcls[:, j, :], ps_ct[0:96, D * r:D * r + D], lg[:, j, 6 - r:7 - r],
                                             hcls[:, j, :], ALU.mult, ALU.add).then_inc(k_out, 1)

            def moments(s):
                statistics(s)
                aggregate2(s)

            def columns_and_dots():
                class_columns()
                class_dots(0)

            schedule(eng, slot, step,
                     {0: weight_maxima, 1: weight_scales, LOOPED: lambda: low_weights(0),
                      LOOPED + 1: lambda: low_weights(1),
                      LN_SLOT: lambda: moments(0), LN_SLOT + 1: lambda: normalise2(0, 0),
                      LN_SLOT + 2: lambda: moments(1), LN_SLOT + 3: lambda: normalise2(1, 1),
                      LN_SLOT + 4: lambda: moments(2), LN_SLOT + 5: lambda: normalise2(2, 0)},
                     {1: class_rows, 2: columns_and_dots, 3: class_squares, 4: class_gates, 7: class_weights,
                      N_STEP - 2: lambda: class_sum(1)})


_OUT_AB = (N_STEP, 128, 4, D)
_OUT_C = (PC, NC, D)
_OUT_CLS = (96, 2, D)


def kernel(**inputs):
    import numpy as np
    import concourse.bacc as bacc
    from concourse import mybir as mb
    from concourse.bass_utils import run_bass_kernel_spmd as run

    a = {k: np.asarray(val) for k, val in inputs.items()}
    x = a["x"].reshape(NB, 3, 14, 16, 14, 16).transpose(0, 1, 3, 5, 2, 4).reshape(NB, KP, 128, NI)
    txt = a["txt"]
    txtc = np.zeros((NC * PC, D), txt.dtype)
    txtc[:NB * MC] = txt[:, 77 - MC:].reshape(NB * MC, D)
    fc1 = a["L0_ffn_fc1_w"].T
    ain = a["L0_ffn_atom_in_w"].transpose(2, 0, 1)
    aout = a["L0_ffn_atom_out_w"].transpose(0, 2, 1).reshape(NATOM, KH, 128, D)
    about = a["L0_ffn_atom_out_b"].T

    def per_class(w):
        w = w.reshape(2, 3, 1, *w.shape[1:]).swapaxes(0, 1)
        w = np.broadcast_to(w, (3, 2, NB) + w.shape[3:])
        return w.swapaxes(1, 2).reshape(96, 2, *w.shape[3:])

    laid = {
        "x": x.transpose(0, 2, 1, 3),
        "wtok": a["L0_tok_W"].T.reshape(KP, 128, D).transpose(1, 0, 2),
        "btok": np.broadcast_to(a["L0_tok_b"], (128, D)),
        "txtb": txt[:, :77 - MC],
        "txtc": txtc.reshape(NC, PC, D).transpose(1, 0, 2),
        "fc1": np.stack([fc1[:128], np.concatenate([fc1[128:], fc1[128:]])], 1),
        "b1": a["L0_ffn_fc1_b"].reshape(KH, 128).T,
        "fc2": a["L0_ffn_fc2_w"].T.reshape(KH, 128, D).transpose(1, 0, 2),
        "b2": np.broadcast_to(a["L0_ffn_fc2_b"], (128, D)),
        "gatew": per_class(a["L0_ffn_gate_pair"]),
        "gateb": per_class(a["L0_ffn_balance_bias"]),
        "ain1": ain[:128],
        "ain2": ain[128:],
        "abin": a["L0_ffn_atom_in_b"].reshape(NATOM, KH, 128).transpose(2, 0, 1),
        "aout": aout.transpose(2, 0, 1, 3),
        "about1": about[:128],
        "about2": about[128:],
    }
    nc = bacc.Bacc("TRN2", target_bir_lowering=False, num_devices=1)
    arrays, args = {}, []
    for name, val in laid.items():
        val = np.ascontiguousarray(val)
        arrays[f"in_{name}"] = val
        args.append(nc.dram_tensor(f"in_{name}", val.shape, mb.dt.from_np(val.dtype), kind="ExternalInput").ap())
    for name, shape in (("ab", _OUT_AB), ("c", _OUT_C), ("cls", _OUT_CLS)):
        args.append(nc.dram_tensor(f"out_{name}", shape, F32, kind="ExternalOutput").ap())
    build(nc, *args)
    r = run(nc, [arrays], core_ids=[0]).results[0]
    out = np.empty((NB, S, D), np.float32)
    out[:, :256] = np.asarray(r["out_ab"]).reshape(N_STEP, 128, 2, 2, D).transpose(0, 2, 3, 1, 4).reshape(NB, 256, D)
    out[:, 256:] = np.asarray(r["out_c"]).transpose(1, 0, 2).reshape(NC * PC, D)[:NB * MC].reshape(NB, MC, D)
    cls = np.asarray(r["out_cls"]).reshape(3, NB, 2, D).transpose(1, 2, 0, 3)
    out[:, :NCLS] = cls.reshape(NB, NCLS, D)
    return out
```

```python
from contextlib import ExitStack

import concourse.bass as bass
import concourse.mybir as mybir

ALU = mybir.AluOpType
ACT = mybir.ActivationFunctionType
AX = mybir.AxisListType
F32 = mybir.dt.float32
F16 = mybir.dt.float16
U32 = mybir.dt.uint32
ABSMAX = bass.bass_isa.ReduceOp.absmax

NB = 32
D = 192
NI = 196
S = 273
PD = 768
KP = PD // 128
HID = 768
KH = HID // 128
NCLS, NATOM = 6, 5
EPS = 1e-5
HB = 64
NL = NI - 128 - HB
NT = HB - NL
NP = NB // 2
MC = S - 256
GC = 7
PC = GC * MC
NC = -(-NB // GC)
PCL = (NB - (NC - 1) * GC) * MC
ONE, HI, HI2, LO2, LO1, VW = 1, 2, 194, 258, 322, 450
FLO2, FLO1, FW = 192, 256, 384
SCALE = D ** -0.5
SHIFT = 15 * 0.6931471805599453 - D ** 0.5
MASKED = -30000.0
TOP = 2.0 ** 14
COLS_A, COLS_B = S, S - 128
PCOL_B, PCOL_C, PCOLS = COLS_A, COLS_A + COLS_B, COLS_A + COLS_B + MC
LOOPED = NB - 10
LN_SLOT = LOOPED + 1
WARM_UP = 36
N_STEP = NB * 2 // 4



def atom_tokens(a):
    return (2 * a, 1, 2, 0) if a < 3 else (a - 3, 2, 3, 1)


def valid(n, last):
    return not isinstance(n, int) or 0 <= n < last


def after(n, least):
    return not isinstance(n, int) or n >= least


def build(nc, xa, xb, xl, wtok, btok, txtb, txtc, fc1, b1, fc2, b2, gatew, gateb, ain1, ain2, abin,
          aout, about1, about2, out_ab, out_c, out_cls):
    split_c = nc.dram_tensor("split_c", [NC * PC, VW], F16).ap()
    attn_c = nc.dram_tensor("attn_c", [NC * PC, D], F32).ap()
    left = nc.dram_tensor("left", [NB, NL, D], F32).ap()
    rows_cls = nc.dram_tensor("rows_cls", [NCLS, NB, D], F32).ap()
    ctx = ExitStack()
    with ctx:
        def sb(name, shape, dt, within=ctx):
            return within.enter_context(nc.sbuf_tensor(name, shape, dt))

        def sem(name):
            return ctx.enter_context(nc.semaphore(name))

        bank = [ctx.enter_context(nc.psum_tensor(f"bank{b}", [128, 512], F32)) for b in range(8)]

        h = sb("h", [128, 2 * NB, D], F32)
        hc = sb("hc", [PC, NC, D], F32)
        b2_sb = sb("b2_sb", [128, D], F32)
        ident = sb("ident", [128, 128], F16)
        ident32 = sb("ident32", [128, 128], F32)
        w1hi = sb("w1hi", [128, 2, HID], F16)
        w1lo = sb("w1lo", [128, 2, HID], F16)
        w2hi = sb("w2hi", [128, KH, D], F16)
        w2lo = sb("w2lo", [128, KH, D], F16)
        b1_sb = sb("b1_sb", [128, KH], F32)
        peak = sb("peak", [128, 3], F32)
        peaks = sb("peaks", [128, 4], F32)
        pow2 = sb("pow2", [128, 4], F32)
        up = sb("up", [128, 4], F32)
        down = sb("down", [128, 4], F32)
        shift = sb("shift", [128, 1], F32)
        eps = sb("eps", [128, 8], F32)
        half_neg = sb("half_neg", [128, 8], F32)
        x2 = sb("x2", [128, 2, 4, D], F32)
        v2 = sb("v2", [128, 2, 4, FW], F16)
        xt2 = sb("xt2", [128, 2, 3, 512], F16)
        st2 = sb("st2", [128, 4, 6], F32)
        mv2 = sb("mv2", [128, 4, 2], F32)
        ve2 = sb("ve2", [128, 4], F32)
        rstd2 = sb("rstd2", [128, 4], F32)

        actx = ctx.enter_context(ExitStack())
        xa_sb = sb("xa_sb", [128, 4, KP, 128], F32, actx)
        xb_sb = sb("xb_sb", [128, 2, KP, 128], F32, actx)
        xl_sb = sb("xl_sb", [128, KP, 128], F32, actx)
        left_sb = sb("left_sb", [128, D], F32, actx)
        wtok_sb = sb("wtok_sb", [128, KP, D], F32, actx)
        w1st = sb("w1st", [128, 2, HID], F32, actx)
        w2st = sb("w2st", [128, KH, D], F32, actx)
        hs = sb("hs", [128, 4, 2, D], F32, actx)
        btok_sb = sb("btok_sb", [128, D], F32, actx)
        never = sb("never", [128, 128], F16, actx)
        never_odd = sb("never_odd", [128, 128], F16, actx)
        v = sb("v", [128, 4, 2, VW], F16, actx)
        vc = sb("vc", [MC, 4, VW], F16, actx)
        xt = sb("xt", [128, 2, 4, S + 1], F16, actx)
        ct = sb("ct", [128, 4, NC * PC], F16, actx)
        x32 = sb("x32", [128, 2, 2, D], F32, actx)
        p32 = sb("p32", [128, 2, PCOLS], F32, actx)
        phi = sb("phi", [128, 2, PCOLS], F16, actx)
        plo = sb("plo", [128, 2, PCOLS], F16, actx)
        xc32 = sb("xc32", [PC, NC, D], F32, actx)
        vcp = sb("vcp", [PC, NC, VW], F16, actx)
        ac = sb("ac", [MC, 2, D], F32, actx)
        st = sb("st", [128, 2, 6], F32, actx)
        mv = sb("mv", [128, 2, 2], F32, actx)
        ve = sb("ve", [128, 2], F32, actx)
        rstd = sb("rstd", [128, 2], F32, actx)
        stc = sb("stc", [PC, NC, 6], F32, actx)
        mvc = sb("mvc", [PC, NC, 2], F32, actx)
        vec = sb("vec", [PC, NC], F32, actx)
        rstdc = sb("rstdc", [PC, NC], F32, actx)
        rden = sb("rden", [128, 3], F32, actx)
        actx.close()

        bctx = ctx.enter_context(ExitStack())
        g32 = sb("g32", [128, 3, 512], F32, bctx)
        ghi = sb("ghi", [128, 2, KH, 512], F16, bctx)
        glo = sb("glo", [128, 2, KH, 512], F16, bctx)
        acp = sb("acp", [PC, NC, D], F32, bctx)
        ain1_sb = sb("ain1_sb", [128, NATOM, HID], F32, bctx)
        ain2_sb = sb("ain2_sb", [64, NATOM, HID], F32, bctx)
        aout_sb = sb("aout_sb", [128, NATOM, KH, D], F32, bctx)
        abin_sb = sb("abin_sb", [128, NATOM, KH], F32, bctx)
        about1_sb = sb("about1_sb", [128, NATOM], F32, bctx)
        about2_sb = sb("about2_sb", [64, NATOM], F32, bctx)
        hcls = sb("hcls", [96, 2, D], F32, bctx)
        xcls = sb("xcls", [96, 2, D], F32, bctx)
        gw_sb = sb("gw_sb", [96, 2, 2, D], F32, bctx)
        gb_sb = sb("gb_sb", [96, 2, 2], F32, bctx)
        scr = sb("scr", [96, D], F32, bctx)
        dots = sb("dots", [96, 2, 5], F32, bctx)
        sq = sb("sq", [96, 2, 3], F32, bctx)
        rn = sb("rn", [96, 2, 3], F32, bctx)
        lg = sb("lg", [96, 2, 8], F32, bctx)
        stk = sb("stk", [96, 2, 6], F32, bctx)
        mvk = sb("mvk", [96, 2, 2], F32, bctx)
        xct1 = sb("xct1", [128, NCLS, NB], F32, bctx)
        xct2 = sb("xct2", [64, NCLS, NB], F32, bctx)
        gt = sb("gt", [128, KH, 2, NCLS, NB], F32, bctx)
        cand1 = sb("cand1", [128, 2, NCLS, NB], F32, bctx)
        cand2 = sb("cand2", [64, 2, NCLS, NB], F32, bctx)

        ps_a, ps_b, ps_left = bank[0], [bank[1], bank[7]], bank[5]
        ps_t = [bank[b][:, :].bitcast(F16)[:, 0:512].rearrange("p (k n) -> p k n", k=4) for b in (2, 6)]
        ps_tc = [bank[b][:, :].bitcast(F16)[:, 0:512].rearrange("p (k n) -> p k n", k=4) for b in (6, 2, 3, 4, 5)]
        ps_s = bank[3]
        ps_o, ps_oc = bank[4], bank[5]
        ps_t2 = [bank[b][:, :].bitcast(F16)[:, 0:768].rearrange("p (a k n) -> p a k n", a=2, k=3) for b in (0, 1)]
        ps_f1 = [bank[2], bank[6], bank[7]]
        ps_f2 = [bank[4], bank[5]]
        ps_ct = bank[3]

        ld_w = sem("ld_w")
        ld_xa = [sem(f"ld_xa{b}") for b in range(4)]
        ld_xb = [sem(f"ld_xb{b}") for b in range(2)]
        ld_xl = sem("ld_xl")
        st_left = sem("st_left")
        left_done = sem("left_done")
        left_ready = sem("left_ready")
        ld_txtc = sem("ld_txtc")
        ld_txtb = [sem(f"ld_txtb{b}") for b in range(4)]
        ld_fc1 = sem("ld_fc1")
        ld_fc2 = sem("ld_fc2")
        ld_vc = [sem(f"ld_vc{b}") for b in range(4)]
        st_split = sem("st_split")
        st_ac = [sem(f"st_ac{b}") for b in range(2)]
        ld_acp = sem("ld_acp")
        st_cls = sem("st_cls")
        ld_ain = sem("ld_ain")
        ld_aout = sem("ld_aout")
        ld_hcls = sem("ld_hcls")
        ld_gate = sem("ld_gate")
        ld_wfirst = sem("ld_wfirst")
        st_out = sem("st_out")
        const_ready = sem("const_ready")
        masks_ready = sem("masks_ready")
        c_stat = sem("c_stat")
        c_mv = sem("c_mv")
        c_ve = sem("c_ve")
        c_rstd = sem("c_rstd")
        c_norm = sem("c_norm")
        c_hi = sem("c_hi")
        c_split = sem("c_split")
        c_turned = sem("c_turned")
        c_kept = sem("c_kept")
        w_peak = sem("w_peak")
        w_peaks = sem("w_peaks")
        w_pow = sem("w_pow")
        w_scaled = sem("w_scaled")
        w_high = sem("w_high")
        w_low = sem("w_low")
        warmed = sem("warmed")
        toka_done = sem("toka_done")
        tokb_done = sem("tokb_done")
        ha_ready = sem("ha_ready")
        hb_ready = sem("hb_ready")
        stat_done = sem("stat_done")
        mv_ready = sem("mv_ready")
        ve_ready = sem("ve_ready")
        rstd_ready = sem("rstd_ready")
        x32_ready = sem("x32_ready")
        vhi_ready = sem("vhi_ready")
        vlo_ready = sem("vlo_ready")
        t_done = sem("t_done")
        xt_ready = sem("xt_ready")
        xtc_ready = sem("xtc_ready")
        qk_done = sem("qk_done")
        p_exp = sem("p_exp")
        p_lo = sem("p_lo")
        pv_done = sem("pv_done")
        rden_ready = sem("rden_ready")
        attn_added = sem("attn_added")
        hc_ready = sem("hc_ready")
        stat2_done = sem("stat2_done")
        mv2_ready = sem("mv2_ready")
        ve2_ready = sem("ve2_ready")
        rstd2_ready = sem("rstd2_ready")
        x2_ready = sem("x2_ready")
        v2hi_ready = sem("v2hi_ready")
        v2lo_ready = sem("v2lo_ready")
        h2b_ready = sem("h2b_ready")
        t2_done = sem("t2_done")
        xt2_ready = sem("xt2_ready")
        f1_done = sem("f1_done")
        gelu_done = sem("gelu_done")
        ghi_ready = sem("ghi_ready")
        glo_ready = sem("glo_ready")
        f2_done = sem("f2_done")
        y_ready = sem("y_ready")
        k_dve = sem("k_dve")
        k_ve = sem("k_ve")
        k_rstd = sem("k_rstd")
        k_rn = sem("k_rn")
        k_xcls = sem("k_xcls")
        k_turned = sem("k_turned")
        k_xct = sem("k_xct")
        k_hid = sem("k_hid")
        k_gelu = sem("k_gelu")
        k_cand = sem("k_cand")
        k_biased = sem("k_biased")
        k_back = sem("k_back")
        k_abs = sem("k_abs")
        k_tanh = sem("k_tanh")
        k_gates = sem("k_gates")
        k_out = sem("k_out")

        last_step = N_STEP + 2

        def schedule(eng, slot, step, slot_stages=None, step_stages=None):
            slot_stages, step_stages = slot_stages or {}, step_stages or {}

            def one_slot(i):
                slot(0, i)
                if i in slot_stages:
                    slot_stages[i]()

            def one_step(s):
                step(0, s)
                if s in step_stages:
                    step_stages[s]()

            for i in range(-2, 2):
                one_slot(i)
            with eng.Fori(0, (LOOPED - 2) // 4) as t:
                for c in range(2, 6):
                    slot(t, c)
            for i in range(LOOPED, NB - 3):
                one_slot(i)
            for s in range(-2, 1):
                one_step(s)
                one_slot(NB - 1 + s)
            for s in range(1, 8):
                one_step(s)
            with eng.Fori(0, (N_STEP - 10) // 2) as t:
                for c in range(8, 10):
                    step(t, c)
            for s in range(N_STEP - 2, last_step + 1):
                one_step(s)

        def early(s):
            return isinstance(s, int) and s < 3

        def tiles(s):
            if isinstance(s, int) and s >= N_STEP:
                return (4, PC) if s == N_STEP else (1, PCL)
            return 4, 128

        def sums(s, k):
            return ps_ct if isinstance(s, int) and s == N_STEP + 1 else ps_f2[k // 2]

        def rows(s, k):
            if isinstance(s, int) and s >= N_STEP:
                return hc[0:tiles(s)[1], 4 * (s - N_STEP) + k, :]
            return h[:, s * 4 + k, :]

        def rows_all(s):
            n, m = tiles(s)
            if isinstance(s, int) and s >= N_STEP:
                return hc[0:m, 4 * (s - N_STEP):4 * (s - N_STEP) + n, :]
            return h[:, bass.ds(s * 4, 4), :]

        def tiles_before(s):
            return s * 4 if not isinstance(s, int) or s <= N_STEP + 1 else 4 * (N_STEP + 1) + 1

        def pairs_before(s):
            return s * 2 if not isinstance(s, int) or s <= N_STEP + 1 else 2 * (N_STEP + 1) + 1

        block = ctx.enter_context(nc.Block())

        @block.sync
        def _(eng):
            half = KP // 2
            eng.dma_start(wtok_sb[:, 0:half, :], wtok[:, 0:half, :]).then_inc(ld_wfirst, 16)
            eng.dma_start(xl_sb[:, :, :], xl).then_inc(ld_xl, 16)
            eng.dma_start(wtok_sb[:, half:KP, :], wtok[:, half:KP, :]).then_inc(ld_w, 16)
            eng.dma_start(btok_sb[:, :], btok).then_inc(ld_w, 16)
            eng.dma_start(xb_sb[:, 0], xb[0]).then_inc(ld_xb[0], 16)
            eng.dma_start(xa_sb[:, 0], xa[0]).then_inc(ld_xa[0], 16)
            eng.dma_start(hc[:, :, :], txtc).then_inc(ld_txtc, 16)
            eng.dma_start(xa_sb[:, 1], xa[1]).then_inc(ld_xa[1], 16)
            eng.wait_ge(left_ready, 1)
            eng.dma_start(left.rearrange("b n d -> (b n) d"), left_sb[:, :]).then_inc(st_left, 16)
            eng.dma_start(xb_sb[:, 1], xb[1]).then_inc(ld_xb[1], 16)

            def load_rows(n, c):
                at = HB * (1 - c % 2)
                eng.dma_start(hs[at:at + NL, c % 4, 1, :], left[n]).then_inc(ld_txtb[c % 4], 16)
                eng.dma_start(hs[at + NL:at + HB, c % 4, 1, :], txtb[n]).then_inc(ld_txtb[c % 4], 16)

            eng.wait_ge(st_left, 16)
            load_rows(0, 0)
            load_rows(1, 1)
            eng.dma_start(xa_sb[:, 2], xa[2]).then_inc(ld_xa[2], 16)
            load_rows(2, 2)
            load_rows(3, 3)
            eng.dma_start(w2st[:, :, :], fc2).then_inc(ld_fc2, 16)
            eng.dma_start(b1_sb[:, :], b1).then_inc(ld_fc2, 16)
            eng.wait_ge(c_split, 2)
            eng.dma_start(split_c.rearrange("(c p) d -> p c d", p=PC), vcp[:, :, :]).then_inc(st_split, 16)
            eng.dma_start(xa_sb[:, 3], xa[3]).then_inc(ld_xa[3], 16)
            eng.wait_ge(st_split, 16)
            for n in range(4):
                eng.dma_start(vc[:, n, :], split_c[n * MC:(n + 1) * MC, :]).then_inc(ld_vc[n], 16)
            eng.dma_start(w1st[:, :, :], fc1).then_inc(ld_fc1, 16)
            eng.dma_start(b2_sb[:, :], b2).then_inc(ld_fc1, 16)

            def slot(t, c):
                i = t * 4 + c
                if valid(i, NB) and valid(i + 6, NB) or isinstance(i, int) and -2 <= i < 0:
                    eng.wait_ge(toka_done, i + 3)
                    eng.dma_start(xa_sb[:, (c + 2) % 4], xa[i + 6]).then_inc(ld_xa[(c + 2) % 4], 16)
                if isinstance(i, int) and i == -2:
                    eng.wait_ge(tokb_done, 1)
                    eng.dma_start(xb_sb[:, 0], xb[2]).then_inc(ld_xb[0], 16)
                if c % 2 and (not isinstance(i, int) or i + 8 < NB):
                    p = (c + 3) // 2
                    eng.wait_ge(tokb_done, t * 2 + (p + 1))
                    eng.dma_start(xb_sb[:, p % 2], xb[t * 2 + (p + 2)]).then_inc(ld_xb[p % 2], 16)
                if valid(i, NB):
                    eng.wait_ge(attn_added, 3 * (i + 1))
                    eng.dma_start(attn_c[bass.ds(i * MC, MC), :], ac[:, c % 2, :]).then_inc(st_ac[c % 2], 16)
                    if after(i, 1):
                        eng.wait_ge(st_cls, 16 * i)
                    eng.dma_start(rows_cls[:, bass.ds(i, 1), :], h[0:NCLS, bass.ds(i * 2, 1), :]).then_inc(st_cls, 16)
                    if valid(i + 4, NB):
                        load_rows(i + 4, c)
                        eng.dma_start(vc[:, c % 4, :],
                                      split_c[bass.ds((i + 4) * MC, MC), :]).then_inc(ld_vc[c % 4], 16)

            def load_classes():
                eng.wait_ge(st_cls, 16 * NB)
                for j in range(2):
                    eng.dma_start(hcls[:, j, :],
                                  rows_cls[3 * j:3 * j + 3].rearrange("n b d -> (n b) d")).then_inc(ld_hcls, 16)
                eng.dma_start(gw_sb[:, :, :, :], gatew).then_inc(ld_gate, 16)
                eng.dma_start(gb_sb[:, :, :], gateb).then_inc(ld_gate, 16)
                eng.wait_ge(w_low, 4)
                for dst, src in ((ain1_sb[:, :, :], ain1), (ain2_sb[:, :, :], ain2), (abin_sb[:, :, :], abin)):
                    eng.dma_start(dst, src).then_inc(ld_ain, 16)
                for dst, src in ((aout_sb[:, :, :, :], aout), (about1_sb[:, :], about1), (about2_sb[:, :], about2)):
                    eng.dma_start(dst, src).then_inc(ld_aout, 16)
                for b in range(2):
                    eng.wait_ge(st_ac[b], 16 * NB // 2)
                eng.dma_start(acp[:, 0:NC - 1, :],
                              attn_c[0:(NC - 1) * PC, :].rearrange("(c p) d -> p c d", p=PC)).then_inc(ld_acp, 16)
                eng.dma_start(acp[0:PCL, NC - 1, :], attn_c[(NC - 1) * PC:NB * MC, :]).then_inc(ld_acp, 16)

            def step(t, c):
                s = t * 2 + c
                if valid(s - 1, last_step):
                    n, m = tiles(s - 1)
                    eng.wait_ge(y_ready, tiles_before(s - 1) + n)
                    if isinstance(s, int) and s - 1 >= N_STEP:
                        g = 4 * (s - 1 - N_STEP)
                        dst = out_c[0:m, g:g + n, :]
                    else:
                        dst = out_ab[s - 1]
                    eng.dma_start(dst, rows_all(s - 1)).then_inc(st_out, 16)

            def class_out():
                eng.wait_ge(k_out, 4)
                eng.dma_start(out_cls, hcls[:, :, :]).then_inc(st_out, 16)

            schedule(eng, slot, step, {NB - 1: load_classes}, {N_STEP: class_out})
            eng.wait_ge(st_out, 16 * (last_step + 1))

        @block.tensor
        def _(eng):
            eng.wait_ge(masks_ready, 1)
            for _ in range(WARM_UP):
                warm = eng.transpose(ps_t[0][:, 0, :], ident[:, :], ident[:, :])
            warm.then_inc(warmed, 1)
            eng.wait_ge(warmed, 1)

            def patch_products(out, patches):
                for k in range(KP):
                    mm = eng.matmul(out[:, 0:D], patches[:, k, :], wtok_sb[:, k, :], start=(k == 0), stop=(k == KP - 1))
                return mm

            def last_tokens():
                eng.wait_ge(ld_wfirst, 16)
                eng.wait_ge(ld_xl, 16)
                eng.wait_ge(ld_w, 32)
                patch_products(ps_left, xl_sb).then_inc(left_done, 1)

            def tokens_a(t, c):
                n, b = t * 4 + c, c % 4
                if not valid(n, NB):
                    return
                eng.wait_ge(ld_xa[b], (t + (c // 4 + 1)) * 16)
                if after(n, 1):
                    eng.wait_ge(ha_ready, n)
                patch_products(ps_a, xa_sb[:, b]).then_inc(toka_done, 1)

            def tokens_b(t, c):
                n, b = t * 2 + c, c % 2
                if not valid(n, NP):
                    return
                eng.wait_ge(ld_xb[b], (t + (c // 2 + 1)) * 16)
                if after(n, 2):
                    eng.wait_ge(hb_ready, n * 2 - 2)
                patch_products(ps_b[b], xb_sb[:, b]).then_inc(tokb_done, 1)

            def turn(t, c):
                n, b = t * 4 + c, c % 4
                if not valid(n, NB):
                    return
                eng.wait_ge(vhi_ready, 2 * (n + 1))
                eng.wait_ge(vlo_ready, 2 * (n + 1))
                if isinstance(n, int) and n == 0:
                    eng.wait_ge(c_kept, 2)
                if after(n, 1):
                    eng.wait_ge(xt_ready, 2 * n)
                for a in range(2):
                    for k, src in enumerate(split_columns(v[:, b, a, :])):
                        mm = eng.transpose(ps_t[a][:, k, :], src, ident[:, :])
                mm.then_inc(t_done, 1)

            def split_columns(r):
                return r[:, HI:HI + 128], r[:, LO1:LO1 + 128], r[:, HI2:HI2 + 128], r[:, HI + 128:HI2 + 64]

            def product(out, b, t0, t1, s0, s1):
                X = xt[:, b]
                eng.matmul(out, X[:, 0, t0:t1], X[:, 0, s0:s1], start=True, stop=False)
                eng.matmul(out, X[:, 0, t0:t1], X[:, 1, s0:s1], start=False, stop=False)
                eng.matmul(out, X[:, 1, t0:t1], X[:, 0, s0:s1], start=False, stop=False)
                eng.matmul(out, X[:, 3, t0:t1], X[:, 2, s0:s1], start=False, stop=False)
                eng.matmul(out, X[64:128, 2, t0:t1], X[64:128, 3, s0:s1], start=False, stop=False)

            def scores(t, c):
                n, b = t * 4 + c, c % 2
                if not valid(n, NB):
                    return
                eng.wait_ge(xt_ready, 2 * (n + 1))
                eng.wait_ge(xtc_ready, n + 1)
                if isinstance(n, int) and n == 0:
                    eng.wait_ge(masks_ready, 6)
                if after(n, 1):
                    eng.wait_ge(p_exp, 4 * n)
                for t0, t1, col, width in ((0, 128, 0, COLS_A), (128, 256, PCOL_B, COLS_B), (256, S, PCOL_C, MC)):
                    m = t1 - t0
                    product(ps_s[0:m, col:col + width], b, t0, t1, t0, S)
                    mask = never_odd if t0 == 128 and c % 2 else never
                    mm = eng.matmul(ps_s[0:m, col:col + m], ident[0:m, 0:m], mask[0:m, 0:m],
                                    start=False, stop=True)
                mm.then_inc(qk_done, 1)

            def values(t, c):
                n, b, pb = t * 4 + c, c % 4, c % 2
                if not valid(n, NB):
                    return
                eng.wait_ge(p_exp, 4 * (n + 1))
                eng.wait_ge(p_lo, 2 * (n + 1))
                eng.wait_ge(ld_vc[b], (t + (c // 4 + 1)) * 16)
                if after(n, 1):
                    eng.wait_ge(attn_added, 3 * n)
                blocks = ((128, 0), (128, PCOL_B - 128), (MC, PCOL_C - 256))
                for q, (s0, s1, out) in enumerate(((0, 128, ps_o[:, 0:D + 1]), (128, 256, ps_o[:, D + 1:2 * D + 2]),
                                                   (256, S, ps_oc[0:MC, 0:D + 1]))):
                    for r in range(q + 1):
                        m, col = blocks[r]
                        row = vc[:, b, :] if r == 2 else v[:, b, r, :]
                        hi, lo = phi[0:m, pb, col + s0:col + s1], plo[0:m, pb, col + s0:col + s1]
                        eng.matmul(out, hi, row[:, ONE:HI2], start=(r == 0), stop=False)
                        eng.matmul(out, lo, row[:, ONE:HI2], start=False, stop=False)
                        eng.matmul(out[:, 129:D + 1], hi, row[:, LO2:LO1], start=False, stop=False)
                        mm = eng.matmul(out[:, 1:129], hi, row[:, LO1:VW], start=False, stop=(r == q))
                mm.then_inc(pv_done, 1)

            def turn_c():
                eng.wait_ge(masks_ready, 3)
                eng.wait_ge(c_split, 2)
                for g in range(NC):
                    for k, src in enumerate(split_columns(vcp[:, g, :])):
                        if g == NC - 1 and k == 0:
                            eng.wait_ge(left_ready, 1)
                        mm = eng.transpose(ps_tc[g][:, k, 0:PC], src, ident[0:PC, 0:PC])
                    mm.then_inc(c_turned, 1)

            def slot(t, c):
                if isinstance(t, int) and c == -2:
                    last_tokens()
                    tokens_b(0, 0)
                tokens_a(t, c + 2)
                if isinstance(t, int) and c == -1:
                    tokens_b(0, 1)
                    turn_c()
                turn(t, c + 1)
                if c % 2 and not (isinstance(t, int) and c == -1):
                    tokens_b(t, (c + 3) // 2)
                values(t, c)
                scores(t, c + 1)

            def turn2(t, c):
                s, b = t * 2 + c, c % 2
                if not valid(s, last_step):
                    return
                n, m = tiles(s)
                eng.wait_ge(v2hi_ready, s + 1)
                eng.wait_ge(v2lo_ready, 2 * (s + 1))
                if isinstance(s, int) and s == 0:
                    eng.wait_ge(ha_ready, NB)
                    eng.wait_ge(hb_ready, NB)
                if after(s, 1):
                    eng.wait_ge(xt2_ready, pairs_before(s))
                for k in range(n):
                    for j, src in enumerate((v2[0:m, b, k, 0:128], v2[0:m, b, k, FLO1:FW], v2[0:m, b, k, 128:FLO1])):
                        mm = eng.transpose(ps_t2[k // 2][:, k % 2, j, 0:m], src, ident[0:m, 0:m])
                    if k % 2 or k == n - 1:
                        mm.then_inc(t2_done, 1)

            def fc1_products(t, c):
                s, b = t * 2 + c, c % 2
                if not valid(s, last_step):
                    return
                n, m = tiles(s)
                N = n * m
                eng.wait_ge(xt2_ready, pairs_before(s) + (n + 1) // 2)
                if isinstance(s, int) and s == 0:
                    eng.wait_ge(w_high, 1)
                    eng.wait_ge(w_low, 2)
                    eng.wait_ge(xt_ready, 2 * NB)
                X = xt2[:, b]
                for q in range(KH):
                    if after(s, 1) or q >= 3:
                        eng.wait_ge(gelu_done, s * KH + (q - 2))
                    if isinstance(s, int) and s in (4, 5, 6) and q < 3:
                        eng.wait_ge(k_gelu, 3 * {4: (4, 2, 3), 5: (7, 8, 6), 6: (10, 8, 9)}[s][q])
                    out = ps_f1[q % 3][:, 0:N]
                    w = slice(128 * q, 128 * q + 128)
                    eng.matmul(out, w1hi[:, 0, w], X[:, 0, 0:N], start=True, stop=False)
                    eng.matmul(out, w1hi[:, 0, w], X[:, 1, 0:N], start=False, stop=False)
                    eng.matmul(out, w1lo[:, 0, w], X[:, 0, 0:N], start=False, stop=False)
                    eng.matmul(out, w1hi[:, 1, w], X[:, 2, 0:N], start=False, stop=False)
                    eng.matmul(out, w1lo[0:64, 1, w], X[0:64, 2, 0:N],
                               start=False, stop=True).then_inc(f1_done, 1)

            def fc2_products(t, c):
                s, b = t * 2 + c, c % 2
                if not valid(s, last_step):
                    return
                n, m = tiles(s)
                eng.wait_ge(ghi_ready, KH * (s + 1))
                eng.wait_ge(glo_ready, KH * (s + 1))
                if isinstance(s, int) and s == 0:
                    eng.wait_ge(w_high, 2)
                    eng.wait_ge(w_low, 4)
                if isinstance(s, int) and s == 0:
                    eng.wait_ge(attn_added, 3 * NB)
                if after(s, 1) and not (isinstance(s, int) and s == N_STEP + 1):
                    eng.wait_ge(y_ready, tiles_before(s))
                for k in range(n):
                    out = sums(s, k)[0:m, D * (k % 2):D * (k % 2) + D]
                    for q in range(KH):
                        hi, lo = ghi[:, b, q, m * k:m * k + m], glo[:, b, q, m * k:m * k + m]
                        eng.matmul(out, hi, w2hi[:, q, :], start=(q == 0), stop=False)
                        eng.matmul(out, hi, w2lo[:, q, :], start=False, stop=False)
                        mm = eng.matmul(out, lo, w2hi[:, q, :], start=False, stop=(q == KH - 1))
                    if k % 2 or k == n - 1:
                        mm.then_inc(f2_done, 1)

            def step(t, c):
                turn2(t, c + 1)
                fc1_products(t, c)
                fc2_products(t, c - 1)

            def turn_classes():
                eng.wait_ge(k_xcls, 2)
                for j in range(2):
                    w = slice(96 * j, 96 * j + 96)
                    eng.transpose(ps_ct[:, w], xcls[:, j, 0:128], ident32[0:96, 0:96])
                    mm = eng.transpose(ps_ct[0:64, 192 + 96 * j:288 + 96 * j], xcls[:, j, 128:D],
                                       ident32[0:96, 0:96])
                mm.then_inc(k_turned, 1)

            def class_hidden(first, last):
                if first == 0:
                    eng.wait_ge(k_xct, 2)
                    eng.wait_ge(ld_ain, 16 * 3)
                eng.wait_ge(gelu_done, (4 + first // 2) * KH)
                for a in range(first, last):
                    n0, dn, n, _ = atom_tokens(a)
                    for q in range(KH):
                        u = 2 * a + q // 3
                        if q % 3 == 0 and u >= 3:
                            eng.wait_ge(k_gelu, 3 * (u - 2))
                        out = ps_f1[u % 3][:, 96 * (q % 3):96 * (q % 3) + NB * n]
                        w = slice(128 * q, 128 * q + 128)
                        eng.matmul(out, ain1_sb[:, a, w], xct1[:, n0:n0 + dn * (n - 1) + 1:dn, :],
                                   start=True, stop=False)
                        mm = eng.matmul(out, ain2_sb[:, a, w], xct2[:, n0:n0 + dn * (n - 1) + 1:dn, :],
                                        start=False, stop=True)
                        if q % 3 == 2:
                            mm.then_inc(k_hid, 1)

            def class_outputs(half):
                if half == 0:
                    eng.wait_ge(k_gelu, NATOM * KH)
                    eng.wait_ge(ld_aout, 16 * 3)
                else:
                    eng.wait_ge(k_biased, NATOM)
                m, d0 = ((64, 128), (128, 0))[half]
                out = ps_ct[0:m, 0:384].rearrange("p (r n b) -> p r n b", r=2, n=NCLS)
                for a in range(NATOM):
                    n0, dn, n, r = atom_tokens(a)
                    for q in range(KH):
                        mm = eng.matmul(out[:, 1 - r, n0:n0 + dn * (n - 1) + 1:dn, :],
                                        aout_sb[:, a, q, d0:d0 + m],
                                        gt[:, q, 1 - r, n0:n0 + dn * (n - 1) + 1:dn, :],
                                        start=(q == 0), stop=(q == KH - 1))
                    mm.then_inc(k_cand, 1)

            def class_back(j):
                if j:
                    eng.wait_ge(k_out, 2)
                else:
                    eng.wait_ge(k_biased, 2 * NATOM)
                for r in range(2):
                    out = ps_ct[0:96, D * r:D * r + D]
                    eng.transpose(out[:, 0:128], cand1[:, r, 3 * j:3 * j + 3, :], ident32[:, :])
                    mm = eng.transpose(out[:, 128:D], cand2[:, r, 3 * j:3 * j + 3, :], ident32[0:64, 0:64])
                mm.then_inc(k_back, 1)

            schedule(eng, slot, step, None,
                     {2: turn_classes, 3: lambda: class_hidden(0, 2), 4: lambda: class_hidden(2, 4),
                      5: lambda: class_hidden(4, NATOM), 6: lambda: class_outputs(0), 7: lambda: class_outputs(1),
                      N_STEP - 2: lambda: class_back(0), N_STEP - 1: lambda: class_back(1),
                      N_STEP: lambda: eng.wait_ge(k_out, 4)})

        @block.scalar
        def _(eng):
            eng.wait_ge(c_norm, NC)
            eng.copy(vcp[:, :, HI:HI2], xc32[:, :, :]).then_inc(c_hi, 1)
            eng.copy(vcp[:, :, HI2:LO2], xc32[:, :, 128:D]).then_inc(c_hi, 1)

            def keep_columns_b(t, c):
                n, b = t * 4 + c, c % 2
                if not valid(n, NB):
                    return
                eng.wait_ge(t_done, n + 1)
                if after(n, 2):
                    eng.wait_ge(qk_done, n - 1)
                eng.copy(xt[:, b, :, 128:256], ps_t[1][:, :, :]).then_inc(xt_ready, 1)

            def exponents(t, c):
                n, b = t * 4 + c, c % 2
                if valid(n, NB):
                    eng.wait_ge(qk_done, n + 1)
                    if after(n, 2):
                        eng.wait_ge(p_lo, 2 * (n - 1))
                        eng.wait_ge(pv_done, n - 1)
                    for dst in (p32, phi):
                        for m, c0, c1 in ((128, 0, PCOL_C), (MC, PCOL_C, PCOLS)):
                            eng.activation(dst[0:m, b, c0:c1], ps_s[0:m, c0:c1], ACT.Exp, bias=shift[0:m, 0:1],
                                           scale=SCALE).then_inc(p_exp, 1)

            def high_parts(t, c):
                n, b = t * 4 + c, c % 4
                if valid(n, NB):
                    eng.wait_ge(x32_ready, 2 * (n + 1))
                    if after(n, 4):
                        eng.wait_ge(pv_done, n - 3)
                    eng.copy(v[:, b, :, HI:HI2], x32[:, c % 2, :, :]).then_inc(vhi_ready, 1)
                    eng.copy(v[:, b, :, HI2:LO2], x32[:, c % 2, :, 128:D]).then_inc(vhi_ready, 1)

            mid_slot = {LN_SLOT: lambda: scale_weights(0), LN_SLOT + 1: lambda: high_weights(0),
                        LN_SLOT + 2: lambda: high_rows(0, 0), LN_SLOT + 3: lambda: scale_weights(1),
                        LN_SLOT + 4: lambda: high_rows(1, 1), LN_SLOT + 5: lambda: high_weights(1)}

            def slot(t, c):
                keep_columns_b(t, c + 1)
                if isinstance(t, int) and c in mid_slot:
                    mid_slot[c]()
                high_parts(t, c + 2)
                exponents(t, c + 1)

            def scale_weights(n):
                eng.wait_ge(w_pow, 6)
                w, k = ((w1st, 0), (w2st, 2))[n]
                eng.activation(w[:, :, :], w[:, :, :], ACT.Copy, scale=up[:, k:k + 1]).then_inc(w_scaled, 1)

            def high_weights(n):
                w, hi = ((w1st, w1hi), (w2st, w2hi))[n]
                eng.wait_ge(w_scaled, n + 1)
                eng.activation(hi[:, :, :], w[:, :, :], ACT.Copy).then_inc(w_high, 1)

            def high_rows(n, b):
                k, m = tiles(n)
                eng.wait_ge(x2_ready, tiles_before(n) + k)
                if after(n, 2):
                    eng.wait_ge(t2_done, pairs_before(n - 1))
                eng.copy(v2[0:m, b, 0:k, 0:D], x2[0:m, b, 0:k, :]).then_inc(v2hi_ready, 1)

            def gelu(t, c, q):
                s = t * 2 + c
                N = tiles(s)[0] * tiles(s)[1]
                eng.wait_ge(f1_done, s * KH + (q + 1))
                if after(s, 1) or q >= 3:
                    eng.wait_ge(glo_ready, s * KH + (q - 2))
                eng.activation(g32[:, q % 3, 0:N], ps_f1[q % 3][:, 0:N], ACT.Gelu, bias=b1_sb[:, q:q + 1],
                               scale=down[:, 0:1]).then_inc(gelu_done, 1)

            def gelu_hi(t, c, q):
                s = t * 2 + c
                N = tiles(s)[0] * tiles(s)[1]
                eng.wait_ge(gelu_done, s * KH + (q + 1))
                if q == 0 and after(s, 2):
                    eng.wait_ge(f2_done, pairs_before(s - 1))
                eng.activation(ghi[:, c % 2, q, 0:N], g32[:, q % 3, 0:N], ACT.Copy,
                               scale=up[:, 3:4]).then_inc(ghi_ready, 1)

            def step(t, c):
                s = t * 2 + c
                n = t * 2 + (c + 2)
                for q in range(KH + 1):
                    if q == KH and valid(n, last_step) and not early(n):
                        high_rows(n, c % 2)
                    if q < KH and valid(s, last_step):
                        gelu(t, c, q)
                    if q and valid(s, last_step):
                        gelu_hi(t, c, q - 1)

            def class_hidden(first, last):
                eng.wait_ge(ld_ain, 16 * 3)
                for a in range(first, last):
                    n0, dn, n, r = atom_tokens(a)
                    for q in range(KH):
                        u = 2 * a + q // 3
                        eng.wait_ge(k_hid, u + 1)
                        src = ps_f1[u % 3][:, 96 * (q % 3):96 * (q % 3) + NB * n]
                        eng.activation(gt[:, q, r, n0:n0 + dn * (n - 1) + 1:dn, :],
                                       src.rearrange("p (n b) -> p n b", b=NB), ACT.Gelu,
                                       bias=abin_sb[:, a, q:q + 1]).then_inc(k_gelu, 1)

            def class_outputs(half):
                eng.wait_ge(ld_aout, 16 * 3)
                m, dst, bias = ((64, cand2, about2_sb), (128, cand1, about1_sb))[half]
                src = ps_ct[0:m, 0:384].rearrange("p (r n b) -> p r n b", r=2, n=NCLS)
                for a in range(NATOM):
                    n0, dn, n, r = atom_tokens(a)
                    eng.wait_ge(k_cand, NATOM * (half + 1))
                    eng.activation(dst[:, 1 - r, n0:n0 + dn * (n - 1) + 1:dn, :],
                                   src[:, 1 - r, n0:n0 + dn * (n - 1) + 1:dn, :], ACT.Identity,
                                   bias=bias[:, a:a + 1]).then_inc(k_biased, 1)
                if half == 0:
                    eng.wait_ge(k_abs, 2)
                    eng.activation(lg[:, :, 3], lg[:, :, 2], ACT.Tanh, scale=0.5).then_inc(k_tanh, 1)

            schedule(eng, slot, step,
                     {NB - 3: lambda: high_rows(2, 0)},
                     {3: lambda: class_hidden(0, 2), 4: lambda: class_hidden(2, 4),
                      5: lambda: class_hidden(4, NATOM), 6: lambda: class_outputs(0), 7: lambda: class_outputs(1)})

        @block.gpsimd
        def _(eng):
            eng.memset(half_neg[:, :], -0.5).then_inc(const_ready, 1)
            eng.memset(eps[:, :], EPS).then_inc(const_ready, 1)
            eng.memset(shift[:, :], SHIFT).then_inc(const_ready, 1)
            eng.memset(ident[:, :], 0.0).then_inc(const_ready, 1)
            eng.memset(ident32[:, :], 0.0).then_inc(const_ready, 1)
            eng.memset(never[:, :], 0.0).then_inc(const_ready, 1)
            eng.memset(never_odd[:, :], 0.0).then_inc(const_ready, 1)
            eng.memset(v[:, :, :, ONE:HI], 1.0).then_inc(const_ready, 1)
            eng.memset(v[:, :, :, 0:ONE], 0.0).then_inc(const_ready, 1)
            eng.memset(vcp[:, :, ONE:HI], 1.0).then_inc(const_ready, 1)
            eng.memset(vcp[:, :, 0:ONE], 0.0).then_inc(const_ready, 1)
            eng.wait_ge(const_ready, 11)
            eng.affine_select(out=ident[:, :], in_=ident[:, :], compare_op=ALU.not_equal, fill=1.0,
                              base=0, pattern=[[-1, 128]], channel_multiplier=1).then_inc(masks_ready, 1)
            eng.affine_select(out=ident32[:, :], in_=ident32[:, :], compare_op=ALU.not_equal, fill=1.0,
                              base=0, pattern=[[-1, 128]], channel_multiplier=1).then_inc(masks_ready, 1)
            eng.affine_select(out=never[:, :], in_=never[:, :], compare_op=ALU.is_ge, fill=MASKED,
                              base=0, pattern=[[1, 128]], channel_multiplier=-1).then_inc(masks_ready, 1)
            eng.affine_select(out=never_odd[:, :], in_=never_odd[:, :], compare_op=ALU.is_ge, fill=MASKED,
                              base=0, pattern=[[1, 128]], channel_multiplier=-1).then_inc(masks_ready, 1)
            eng.wait_ge(masks_ready, 4)
            eng.memset(never_odd[0:HB, HB:128], MASKED).then_inc(masks_ready, 1)
            eng.memset(never_odd[HB:128, 0:HB], 0.0).then_inc(masks_ready, 1)
            eng.wait_ge(masks_ready, 6)

            eng.wait_ge(c_mv, NC)
            eng.tensor_tensor(vec[:, :], mvc[:, :, 1], eps[0:PC, 0:NC], ALU.add).then_inc(c_ve, 1)
            eng.wait_ge(c_ve, 1)
            eng.tensor_tensor(rstdc[:, :], vec[:, :], half_neg[0:PC, 0:NC], ALU.pow).then_inc(c_rstd, 1)

            def columns_c(t, c):
                n, b = t * 4 + c, c % 2
                if not valid(n, NB):
                    return
                if isinstance(n, int) and n == 0:
                    eng.wait_ge(c_kept, NC)
                if after(n, 2):
                    eng.wait_ge(qk_done, n - 1)
                eng.tensor_copy(xt[:, b, :, 256:S], ct[:, :, bass.ds(n * MC, MC)]).then_inc(xtc_ready, 1)

            def scales(t, c):
                n = t * 4 + c
                if not valid(n, NB):
                    return
                eng.wait_ge(mv_ready, 2 * (n + 1))
                eng.tensor_tensor(ve[:, :], mv[:, :, 1], eps[:, 0:2], ALU.add).then_inc(ve_ready, 1)
                eng.wait_ge(ve_ready, n + 1)
                eng.tensor_tensor(rstd[:, :], ve[:, :], half_neg[:, 0:2], ALU.pow).then_inc(rstd_ready, 1)

            def low_parts(t, c):
                n, b = t * 4 + c, c % 4
                if not valid(n, NB):
                    return
                eng.wait_ge(vhi_ready, 2 * (n + 1))
                eng.tensor_tensor(v[:, b, :, LO1:VW], x32[:, c % 2, :, 0:128], v[:, b, :, HI:HI + 128],
                                  ALU.subtract).then_inc(vlo_ready, 1)
                eng.tensor_tensor(v[:, b, :, LO2:LO1], x32[:, c % 2, :, 128:D], v[:, b, :, HI2:LO2],
                                  ALU.subtract).then_inc(vlo_ready, 1)

            def slot(t, c):
                if isinstance(t, int) and c == -1:
                    scales(t, c + 2)
                    columns_c(t, c + 1)
                else:
                    columns_c(t, c + 1)
                    scales(t, c + 2)
                low_parts(t, c + 2)

            def weight_peaks():
                eng.wait_ge(w_peak, 3)
                eng.partition_all_reduce(peaks[:, 0:3], peak[:, :], 128, ABSMAX).then_inc(w_peaks, 1)

            def scale_rows(n):
                k, m = tiles(n)
                eng.wait_ge(mv2_ready, tiles_before(n) + k)
                eng.tensor_tensor(ve2[0:m, 0:k], mv2[0:m, 0:k, 1], eps[0:m, 0:k], ALU.add).then_inc(ve2_ready, 1)
                eng.wait_ge(ve2_ready, n + 1)
                eng.tensor_tensor(rstd2[0:m, 0:k], ve2[0:m, 0:k], half_neg[0:m, 0:k], ALU.pow).then_inc(rstd2_ready, 1)

            def low_rows(n, b):
                k, m = tiles(n)
                eng.wait_ge(v2hi_ready, n + 1)
                eng.tensor_tensor(v2[0:m, b, 0:k, FLO1:FW], x2[0:m, b, 0:k, 0:128], v2[0:m, b, 0:k, 0:128],
                                  ALU.subtract).then_inc(v2lo_ready, 1)
                eng.tensor_tensor(v2[0:m, b, 0:k, FLO2:FLO1], x2[0:m, b, 0:k, 128:D], v2[0:m, b, 0:k, 128:D],
                                  ALU.subtract).then_inc(v2lo_ready, 1)

            def bias_rows(n):
                k, m = tiles(n)
                if isinstance(n, int) and n <= 3:
                    eng.wait_ge(st_cls, 16 * (2 * n + 2 if early(n) else NB))
                r = rows_all(n)
                eng.tensor_tensor(r, r, b2_sb[0:m, :].unsqueeze(1).to_broadcast([m, k, D]),
                                  ALU.add).then_inc(h2b_ready, 1)

            def step(t, c):
                n = t * 2 + (c + 2)
                if valid(n, last_step) and not early(n):
                    scale_rows(n)
                    low_rows(n, c % 2)
                    bias_rows(n)

            def low_weights(n, half):
                w, hi, lo = ((w1st, w1hi, w1lo), (w2st, w2hi, w2lo))[n]
                k = w.shape[1] // 2
                part = slice(k * half, k * half + k)
                eng.wait_ge(w_high, n + 1)
                eng.tensor_tensor(lo[:, part, :], w[:, part, :], hi[:, part, :], ALU.subtract).then_inc(w_low, 1)

            def scales_and_low_rows(n):
                scale_rows(n + 1)
                low_rows(n, n)

            def last_low_rows():
                low_rows(2, 0)
                low_weights(1, 0)

            def last_biases():
                low_weights(1, 1)
                bias_rows(1)
                bias_rows(2)

            def class_scale():
                eng.wait_ge(k_dve, 4)
                eng.tensor_tensor(lg[:, :, 0], mvk[:, :, 1], eps[0:96, 0:2], ALU.add).then_inc(k_ve, 1)
                eng.wait_ge(k_ve, 1)
                eng.tensor_tensor(lg[:, :, 1], lg[:, :, 0], half_neg[0:96, 0:2], ALU.pow).then_inc(k_rstd, 1)

            def class_norms():
                eng.wait_ge(k_gates, 1)
                eng.tensor_tensor(rn[:, :, :], sq[:, :, :],
                                  half_neg[0:96, 0:6].rearrange("p (a b) -> p a b", a=2), ALU.pow).then_inc(k_rn, 1)

            schedule(eng, slot, step,
                     {1: weight_peaks,
                      LN_SLOT: lambda: scale_rows(0), LN_SLOT + 1: lambda: low_weights(0, 0),
                      LN_SLOT + 2: lambda: scales_and_low_rows(0), LN_SLOT + 3: lambda: low_weights(0, 1),
                      LN_SLOT + 4: lambda: scales_and_low_rows(1), LN_SLOT + 5: lambda: bias_rows(0),
                      NB - 2: last_low_rows, NB - 1: last_biases},
                     {1: class_scale, 3: class_norms})

        @block.vector
        def _(eng):
            eng.wait_ge(left_done, 1)
            eng.wait_ge(ld_w, 32)
            eng.tensor_tensor(left_sb[:, :], ps_left[:, 0:D], btok_sb[:, :], ALU.add).then_inc(left_ready, 1)
            eng.wait_ge(ld_txtc, 16)
            for g in range(NC):
                eng.bn_stats(stc[:, g, :], hc[:, g, :]).then_inc(c_stat, 1)
            for g in range(NC):
                eng.wait_ge(c_stat, g + 1)
                eng.bn_aggr(mvc[:, g, :], stc[:, g, :]).then_inc(c_mv, 1)

            mid_slot = {}

            def normalise_c():
                eng.wait_ge(c_rstd, 1)
                for g in range(NC):
                    eng.tensor_scalar(xc32[:, g, :], hc[:, g, :], mvc[:, g, 0:1], rstdc[:, g:g + 1],
                                      ALU.subtract, ALU.mult).then_inc(c_norm, 1)

            def split_rows_c(part):
                low, cols, high = ((slice(LO1, VW), slice(0, 128), slice(HI, HI + 128)),
                                   (slice(LO2, LO1), slice(128, D), slice(HI2, LO2)))[part]
                eng.wait_ge(c_hi, 2)
                eng.tensor_tensor(vcp[:, :, low], xc32[:, :, cols], vcp[:, :, high], ALU.subtract).then_inc(c_split, 1)

            def keep_c():
                for g in range(NC):
                    eng.wait_ge(c_turned, g + 1)
                    eng.tensor_copy(ct[:, :, PC * g:PC * g + PC], ps_tc[g][:, :, 0:PC]).then_inc(c_kept, 1)

            def low_probs(t, c):
                n, b = t * 4 + c, c % 2
                if not valid(n, NB):
                    return
                eng.wait_ge(p_exp, 4 * (n + 1))
                if after(n, 2):
                    eng.wait_ge(pv_done, n - 1)
                for m, c0, c1 in ((128, 0, PCOL_C), (MC, PCOL_C, PCOLS)):
                    eng.tensor_tensor(plo[0:m, b, c0:c1], p32[0:m, b, c0:c1], phi[0:m, b, c0:c1],
                                      ALU.subtract).then_inc(p_lo, 1)

            def add_bias(t, c, half):
                n, b = t * 4 + c, c % 4
                if not valid(n, NB):
                    return
                if half == 0:
                    eng.wait_ge(toka_done, n + 1)
                    eng.tensor_tensor(hs[:, b, 0, :], ps_a[:, 0:D], btok_sb[:, :], ALU.add).then_inc(ha_ready, 1)
                else:
                    p = slice(HB * (c % 2), HB * (c % 2) + HB)
                    eng.wait_ge(tokb_done, t * 2 + (c // 2 + 1))
                    eng.tensor_tensor(hs[p, b, 1, :], ps_b[c // 2 % 2][p, 0:D], btok_sb[p, :],
                                      ALU.add).then_inc(hb_ready, 1)

            def statistics1(t, c, half):
                n, b = t * 4 + c, c % 4
                if not valid(n, NB):
                    return
                if half:
                    eng.wait_ge(ld_txtb[b], (t + (c // 4 + 1)) * 32)
                eng.wait_ge((ha_ready, hb_ready)[half], n + 1)
                eng.bn_stats(st[:, half, :], hs[:, b, half, :]).then_inc(stat_done, 1)

            def aggregate(t, c, half):
                if valid(t * 4 + c, NB):
                    eng.bn_aggr(mv[:, half, :], st[:, half, :]).then_inc(mv_ready, 1)

            def statistics_there(t, c):
                n = t * 4 + c
                if valid(n, NB):
                    eng.wait_ge(stat_done, n * 2 + 2)

            def keep_columns(t, c):
                n, b = t * 4 + c, c % 2
                if not valid(n, NB):
                    return
                eng.wait_ge(t_done, n + 1)
                if after(n, 2):
                    eng.wait_ge(qk_done, n - 1)
                eng.tensor_copy(xt[:, b, :, 0:128], ps_t[0][:, :, :]).then_inc(xt_ready, 1)

            def normalise(t, c):
                n, b = t * 4 + c, c % 2
                if not valid(n, NB):
                    return
                eng.wait_ge(mv_ready, 2 * (n + 1))
                eng.wait_ge(rstd_ready, n + 1)
                if after(n, 2):
                    eng.wait_ge(vlo_ready, 2 * (n - 1))
                for a in range(2):
                    eng.tensor_scalar(x32[:, b, a, :], hs[:, c % 4, a, :], mv[:, a, 0:1], rstd[:, a:a + 1],
                                      ALU.subtract, ALU.mult).then_inc(x32_ready, 1)

            def denominators(t, c):
                n = t * 4 + c
                if not valid(n, NB):
                    return
                eng.wait_ge(pv_done, n + 1)
                eng.reciprocal(rden[:, 0:2], ps_o[:, 0:D + 2:D + 1]).then_inc(rden_ready, 1)
                eng.reciprocal(rden[0:MC, 2:3], ps_oc[0:MC, 0:1]).then_inc(rden_ready, 1)

            def add_attention(t, c):
                n, b = t * 4 + c, c % 2
                if not valid(n, NB):
                    return
                eng.wait_ge(rden_ready, 2 * (n + 1))
                for a in range(2):
                    eng.scalar_tensor_tensor(h[:, n * 2 + a, :], ps_o[:, (D + 1) * a + 1:(D + 1) * (a + 1)],
                                             rden[:, a:a + 1], hs[:, c % 4, a, :],
                                             ALU.mult, ALU.add).then_inc(attn_added, 1)
                if after(n, 2):
                    eng.wait_ge(st_ac[b], (t * 2 + c // 2) * 16)
                eng.tensor_scalar(ac[:, b, :], ps_oc[0:MC, 1:D + 1], rden[0:MC, 2:3], None,
                                  ALU.mult).then_inc(attn_added, 1)

            def slot(t, c):
                if isinstance(t, int) and c < 0:
                    first_slots(c)
                    return
                add_bias(t, c + 2, 1)
                statistics1(t, c + 2, 1)
                if not (isinstance(t, int) and c == NB - 1):
                    low_probs(t, c)
                add_bias(t, c + 2, 0)
                statistics1(t, c + 2, 0)
                statistics_there(t, c + 2)
                keep_columns(t, c + 1)
                aggregate(t, c + 2, 0)
                aggregate(t, c + 2, 1)
                if isinstance(t, int) and c in mid_slot:
                    mid_slot[c]()
                if c % 2:
                    normalise(t, c + 2)
                    denominators(t, c)
                else:
                    denominators(t, c)
                    normalise(t, c + 2)
                add_attention(t, c)
                if isinstance(t, int) and c == NB - 2:
                    low_probs(t, c + 1)

            def first_slots(c):
                n = c + 2
                add_bias(0, n, 1)
                add_bias(0, n, 0)
                if n == 0:
                    normalise_c()
                statistics1(0, n, 1)
                statistics1(0, n, 0)
                statistics_there(0, n)
                aggregate(0, n, 0)
                aggregate(0, n, 1)
                if n == 0:
                    split_rows_c(0)
                    normalise(0, n)
                    split_rows_c(1)
                else:
                    keep_c()
                    keep_columns(0, 0)
                    normalise(0, n)

            def weight_maxima(n):
                if n == 0:
                    eng.wait_ge(ld_fc1, 32)
                    eng.tensor_reduce(peak[:, 0:1], w1st[:, :, :], AX.XY, ALU.max, apply_absolute_value=True).then_inc(w_peak, 1)
                else:
                    eng.wait_ge(ld_fc2, 32)
                    eng.tensor_reduce(peak[:, 1:2], b1_sb[:, :], AX.X, ALU.max, apply_absolute_value=True).then_inc(w_peak, 1)
                    eng.tensor_reduce(peak[:, 2:3], w2st[:, :, :], AX.XY, ALU.max, apply_absolute_value=True).then_inc(w_peak, 1)

            def weight_scales():
                eng.wait_ge(w_peaks, 1)
                eng.scalar_tensor_tensor(peaks[:, 3:4], peaks[:, 0:1], float(D), peaks[:, 1:2],
                                         ALU.mult, ALU.add).then_inc(w_pow, 1)
                eng.wait_ge(w_pow, 1)
                eng.tensor_scalar(peaks[:, :], peaks[:, :], 2.0 ** -60, None, ALU.max).then_inc(w_pow, 1)
                eng.wait_ge(w_pow, 2)
                eng.tensor_scalar(pow2[:, :].bitcast(U32), peaks[:, :].bitcast(U32), 0x7F800000, None,
                                  ALU.bitwise_and).then_inc(w_pow, 1)
                eng.wait_ge(w_pow, 3)
                eng.tensor_scalar(down[:, :], pow2[:, :], 1 / TOP, None, ALU.mult).then_inc(w_pow, 1)
                eng.wait_ge(w_pow, 4)
                eng.reciprocal(up[:, :], down[:, :]).then_inc(w_pow, 1)
                eng.wait_ge(w_pow, 5)
                eng.tensor_tensor(down[:, 1:2], down[:, 2:3], down[:, 3:4], ALU.mult).then_inc(w_pow, 1)

            def statistics(s):
                n, m = tiles(s)
                if isinstance(s, int) and s == N_STEP:
                    eng.wait_ge(ld_acp, 32)
                    eng.tensor_tensor(hc[:, 0:NC - 1, :], hc[:, 0:NC - 1, :], acp[:, 0:NC - 1, :],
                                      ALU.add).then_inc(hc_ready, 1)
                    eng.tensor_tensor(hc[0:PCL, NC - 1, :], hc[0:PCL, NC - 1, :], acp[0:PCL, NC - 1, :],
                                      ALU.add).then_inc(hc_ready, 1)
                    eng.wait_ge(hc_ready, 2)
                if isinstance(s, int) and s <= 3:
                    eng.wait_ge(attn_added, 3 * (LN_SLOT + 2 * s if early(s) else NB))
                for k in range(n):
                    eng.bn_stats(st2[0:m, k, :], rows(s, k)).then_inc(stat2_done, 1)
                eng.wait_ge(stat2_done, tiles_before(s) + n)

            def aggregate2(s):
                n, m = tiles(s)
                for k in range(n):
                    eng.bn_aggr(mv2[0:m, k, :], st2[0:m, k, :]).then_inc(mv2_ready, 1)

            def normalise2(s, b):
                n, m = tiles(s)
                eng.wait_ge(mv2_ready, tiles_before(s) + n)
                eng.wait_ge(rstd2_ready, s + 1)
                if after(s, 2):
                    eng.wait_ge(v2lo_ready, 2 * (s - 1))
                for k in range(n):
                    eng.tensor_scalar(x2[0:m, b, k, :], rows(s, k), mv2[0:m, k, 0:1], rstd2[0:m, k:k + 1],
                                      ALU.subtract, ALU.mult).then_inc(x2_ready, 1)

            def keep_columns2(t, c):
                s, b = t * 2 + c, c % 2
                if not valid(s, last_step):
                    return
                n, m = tiles(s)
                if after(s, 2):
                    eng.wait_ge(f1_done, (s - 1) * KH)
                for j in range((n + 1) // 2):
                    w = min(2, n - 2 * j)
                    eng.wait_ge(t2_done, pairs_before(s) + (j + 1))
                    eng.tensor_copy(xt2[:, b, :, 2 * m * j:2 * m * j + w * m].rearrange("p k (a n) -> p a k n", a=w),
                                    ps_t2[j][:, 0:w, :, 0:m]).then_inc(xt2_ready, 1)

            def low_gelu(t, c, q):
                s = t * 2 + c
                if not valid(s, last_step):
                    return
                N = tiles(s)[0] * tiles(s)[1]
                eng.wait_ge(ghi_ready, s * KH + (q + 1))
                if q == 0 and after(s, 2):
                    eng.wait_ge(f2_done, pairs_before(s - 1))
                eng.scalar_tensor_tensor(glo[:, c % 2, q, 0:N], g32[:, q % 3, 0:N], up[:, 3:4],
                                         ghi[:, c % 2, q, 0:N], ALU.mult, ALU.subtract).then_inc(glo_ready, 1)

            def outputs(t, c):
                s = t * 2 + c
                if not valid(s, last_step):
                    return
                n, m = tiles(s)
                eng.wait_ge(h2b_ready, s + 1)
                for k in range(n):
                    if k % 2 == 0:
                        eng.wait_ge(f2_done, pairs_before(s) + (k // 2 + 1))
                    eng.scalar_tensor_tensor(rows(s, k), sums(s, k)[0:m, D * (k % 2):D * (k % 2) + D],
                                             down[0:m, 1:2], rows(s, k), ALU.mult, ALU.add).then_inc(y_ready, 1)

            def step(t, c):
                n = t * 2 + (c + 2)
                coming = valid(n, last_step) and not early(n)
                if coming:
                    statistics(n)
                if not (isinstance(t, int) and c == -1):
                    keep_columns2(t, c + 1)
                if coming:
                    aggregate2(n)
                for q in range(3):
                    low_gelu(t, c, q)
                if coming:
                    normalise2(n, c % 2)
                for q in range(3, KH):
                    low_gelu(t, c, q)
                outputs(t, c - 1)

            def class_rows():
                eng.wait_ge(ld_hcls, 16 * 2)
                for j in range(2):
                    eng.bn_stats(stk[:, j, :], hcls[:, j, :]).then_inc(k_dve, 1)
                eng.wait_ge(k_dve, 2)
                for j in range(2):
                    eng.bn_aggr(mvk[:, j, :], stk[:, j, :]).then_inc(k_dve, 1)
                eng.wait_ge(k_dve, 4)
                eng.wait_ge(k_rstd, 1)
                for j in range(2):
                    eng.tensor_scalar(xcls[:, j, :], hcls[:, j, :], mvk[:, j, 0:1], lg[:, j, 1:2],
                                      ALU.subtract, ALU.mult).then_inc(k_xcls, 1)

            def class_columns():
                eng.wait_ge(k_turned, 1)
                eng.tensor_copy(xct1[:, :, :], ps_ct[:, 0:192].rearrange("p (n b) -> p n b", b=NB)).then_inc(k_xct, 1)
                eng.tensor_copy(xct2[:, :, :],
                                ps_ct[0:64, 192:384].rearrange("p (n b) -> p n b", b=NB)).then_inc(k_xct, 1)

            def class_dots(j):
                eng.wait_ge(k_xcls, 2)
                eng.wait_ge(ld_gate, 16 * 2)
                w0, w1, xr = gw_sb[:, j, 0, :], gw_sb[:, j, 1, :], xcls[:, j, :]
                for k, (a, b) in enumerate(((xr, w0), (xr, w1), (xr, xr), (w0, w0), (w1, w1))):
                    eng.wait_ge(k_dve, 4 + 5 * j + k)
                    eng.tensor_tensor_reduce(scr[:, :], a, b, 1.0, 0.0, ALU.mult, ALU.add,
                                             dots[:, j, k:k + 1]).then_inc(k_dve, 1)

            def class_squares():
                class_dots(1)
                eng.wait_ge(k_dve, 14)
                eng.tensor_scalar(sq[:, :, :], dots[:, :, 2:5], 1e-24, None, ALU.max).then_inc(k_gates, 1)

            def class_gates():
                eng.wait_ge(k_rn, 1)
                eng.tensor_tensor(dots[:, :, 0:2], dots[:, :, 0:2], rn[:, :, 1:3], ALU.mult).then_inc(k_dve, 1)
                eng.wait_ge(k_dve, 15)
                eng.tensor_tensor(lg[:, :, 4], dots[:, :, 1], dots[:, :, 0], ALU.subtract).then_inc(k_dve, 1)
                eng.wait_ge(k_dve, 16)
                eng.tensor_tensor(lg[:, :, 4], lg[:, :, 4], rn[:, :, 0], ALU.mult).then_inc(k_dve, 1)
                eng.wait_ge(k_dve, 17)
                eng.tensor_tensor(lg[:, :, 5], gb_sb[:, :, 1], gb_sb[:, :, 0], ALU.subtract).then_inc(k_dve, 1)
                eng.wait_ge(k_dve, 18)
                eng.tensor_tensor(lg[:, :, 6], lg[:, :, 4], lg[:, :, 5], ALU.add).then_inc(k_dve, 1)
                eng.wait_ge(k_dve, 19)
                eng.scalar_tensor_tensor(lg[:, :, 2], lg[:, :, 6], -1.0, lg[:, :, 6], ALU.mult, ALU.max).then_inc(k_abs, 1)
                eng.tensor_scalar(lg[:, :, 7], lg[:, :, 6], 0.0, None, ALU.is_gt).then_inc(k_abs, 1)

            def class_weights():
                eng.wait_ge(k_abs, 2)
                eng.wait_ge(k_tanh, 1)
                eng.tensor_scalar(lg[:, :, 4], lg[:, :, 3], 0.5, 0.5, ALU.mult, ALU.add).then_inc(k_dve, 1)
                eng.wait_ge(k_dve, 20)
                eng.tensor_tensor(lg[:, :, 5], lg[:, :, 4], lg[:, :, 7], ALU.mult).then_inc(k_dve, 1)
                eng.wait_ge(k_dve, 21)
                eng.tensor_tensor(lg[:, :, 6], lg[:, :, 4], lg[:, :, 5], ALU.subtract).then_inc(k_dve, 1)
                eng.wait_ge(k_dve, 22)

            def class_sum(j):
                eng.wait_ge(k_back, j + 1)
                for r in range(2):
                    if r:
                        eng.wait_ge(k_out, 2 * j + 1)
                    eng.scalar_tensor_tensor(hcls[:, j, :], ps_ct[0:96, D * r:D * r + D], lg[:, j, 6 - r:7 - r],
                                             hcls[:, j, :], ALU.mult, ALU.add).then_inc(k_out, 1)

            def moments(s):
                statistics(s)
                aggregate2(s)

            mid_slot.update({1: lambda: weight_maxima(0), LOOPED: weight_scales,
                             LN_SLOT: lambda: moments(0), LN_SLOT + 1: lambda: normalise2(0, 0),
                             LN_SLOT + 2: lambda: moments(1), LN_SLOT + 3: lambda: normalise2(1, 1),
                             LN_SLOT + 4: lambda: moments(2), LN_SLOT + 5: lambda: normalise2(2, 0),
                             NB - 2: lambda: keep_columns2(0, 0)})

            def columns_and_dots():
                class_columns()
                class_dots(0)

            schedule(eng, slot, step,
                     {0: lambda: weight_maxima(1)},
                     {1: class_rows, 2: columns_and_dots, 3: class_squares, 4: class_gates, 7: class_weights,
                      N_STEP - 2: lambda: class_sum(0), N_STEP - 1: lambda: class_sum(1)})


_OUT_AB = (N_STEP, 128, 4, D)
_OUT_C = (PC, NC, D)
_OUT_CLS = (96, 2, D)


def kernel(**inputs):
    import numpy as np
    import concourse.bacc as bacc
    from concourse import mybir as mb
    from concourse.bass_utils import run_bass_kernel_spmd as run

    a = {k: np.asarray(val) for k, val in inputs.items()}
    x = a["x"].reshape(NB, 3, 14, 16, 14, 16).transpose(0, 1, 3, 5, 2, 4).reshape(NB, KP, 128, NI)
    x = x.transpose(0, 2, 1, 3)
    txt = a["txt"]
    txtc = np.zeros((NC * PC, D), txt.dtype)
    txtc[:NB * MC] = txt[:, NT:].reshape(NB * MC, D)
    fc1 = a["L0_ffn_fc1_w"].T
    ain = a["L0_ffn_atom_in_w"].transpose(2, 0, 1)
    aout = a["L0_ffn_atom_out_w"].transpose(0, 2, 1).reshape(NATOM, KH, 128, D)
    about = a["L0_ffn_atom_out_b"].T

    def per_class(w):
        w = w.reshape(2, 3, 1, *w.shape[1:]).swapaxes(0, 1)
        w = np.broadcast_to(w, (3, 2, NB) + w.shape[3:])
        return w.swapaxes(1, 2).reshape(96, 2, *w.shape[3:])

    laid = {
        "xa": x[..., :128],
        "xb": x[..., 128:128 + HB].reshape(NP, 2, 128, KP, HB).transpose(0, 2, 3, 1, 4).reshape(NP, 128, KP, 2 * HB),
        "xl": x[..., 128 + HB:].transpose(1, 2, 0, 3).reshape(128, KP, NB * NL),
        "wtok": a["L0_tok_W"].T.reshape(KP, 128, D).transpose(1, 0, 2),
        "btok": np.broadcast_to(a["L0_tok_b"], (128, D)),
        "txtb": txt[:, :NT],
        "txtc": txtc.reshape(NC, PC, D).transpose(1, 0, 2),
        "fc1": np.stack([fc1[:128], np.concatenate([fc1[128:], fc1[128:]])], 1),
        "b1": a["L0_ffn_fc1_b"].reshape(KH, 128).T,
        "fc2": a["L0_ffn_fc2_w"].T.reshape(KH, 128, D).transpose(1, 0, 2),
        "b2": np.broadcast_to(a["L0_ffn_fc2_b"], (128, D)),
        "gatew": per_class(a["L0_ffn_gate_pair"]),
        "gateb": per_class(a["L0_ffn_balance_bias"]),
        "ain1": ain[:128],
        "ain2": ain[128:],
        "abin": a["L0_ffn_atom_in_b"].reshape(NATOM, KH, 128).transpose(2, 0, 1),
        "aout": aout.transpose(2, 0, 1, 3),
        "about1": about[:128],
        "about2": about[128:],
    }
    nc = bacc.Bacc("TRN2", target_bir_lowering=False, num_devices=1)
    arrays, args = {}, []
    for name, val in laid.items():
        val = np.ascontiguousarray(val)
        arrays[f"in_{name}"] = val
        args.append(nc.dram_tensor(f"in_{name}", val.shape, mb.dt.from_np(val.dtype), kind="ExternalInput").ap())
    for name, shape in (("ab", _OUT_AB), ("c", _OUT_C), ("cls", _OUT_CLS)):
        args.append(nc.dram_tensor(f"out_{name}", shape, F32, kind="ExternalOutput").ap())
    build(nc, *args)
    r = run(nc, [arrays], core_ids=[0]).results[0]
    out = np.empty((NB, S, D), np.float32)
    ab = np.asarray(r["out_ab"]).reshape(N_STEP, 128, 2, 2, D).transpose(0, 2, 3, 1, 4)
    out[:, :256] = ab.reshape(NB, 256, D)
    out[1::2, 128:128 + HB], out[1::2, 128 + HB:256] = ab[:, 1, 1, HB:], ab[:, 1, 1, :HB]
    out[:, 256:] = np.asarray(r["out_c"]).transpose(1, 0, 2).reshape(NC * PC, D)[:NB * MC].reshape(NB, MC, D)
    cls = np.asarray(r["out_cls"]).reshape(3, NB, 2, D).transpose(1, 2, 0, 3)
    out[:, :NCLS] = cls.reshape(NB, NCLS, D)
    return out
```
